# Optimizing a Trainium2 kernel written in Bass

```python
import numpy as np
import jax
import jax.numpy as jnp

def _softmax(x, axis=-1):
    return jax.nn.softmax(x, axis=axis)

def _gelu(x):
    return jax.nn.gelu(x, approximate=True)

def _silu(x):
    return jax.nn.silu(x)

def _sigmoid(x):
    return jax.nn.sigmoid(x)

def _layernorm(x, axis=-1, eps=1e-05):
    m = jnp.mean(x, axis=axis, keepdims=True)
    v = jnp.var(x, axis=axis, keepdims=True)
    return (x - m) / jnp.sqrt(v + eps)

def _scatter_add(tgt, idx, src, axis=0):
    return tgt.at[idx].add(src)

def _segment_sum(src, seg, n):
    return jax.ops.segment_sum(src, seg, n)
kernel_name = 'mk_decoder_postln_d2_seqx_r8_e42f1d'

def setup_inputs(seed: int=0):
    np.random.seed(seed)
    _w = jnp.asarray

    def _rec_inputs():
        import jax
        import jax.numpy as jnp
        _rk = jax.random.key(seed)
        x = -0.0002928 + 1 * jax.random.normal(jax.random.fold_in(_rk, 1), (64, 128, 128), jnp.float32)
        _lenS = 128 - jax.random.randint(jax.random.fold_in(_rk, 7), (64,), 0, max(1, 128 // 4) + 1, jnp.int32)
        _lenS2 = 77 - jax.random.randint(jax.random.fold_in(_rk, 8), (64,), 0, max(1, 77 // 4) + 1, jnp.int32)
        _ctx_1024P = jax.random.normal(jax.random.fold_in(_rk, 11), (64, 16, 128), jnp.float32)
        _ctx_1024c = jax.random.dirichlet(jax.random.fold_in(_rk, 511), 0.3 * jnp.ones((16,), jnp.float32), (64, 77))
        _ctx_1024t = jnp.einsum('bsk,bkd->bsd', _ctx_1024c, _ctx_1024P)
        _ctx_1024t = _ctx_1024t * jax.lax.rsqrt(jnp.mean(jnp.square(_ctx_1024t)) + 1e-12) * 0.953939
        ctx_1024 = 4.13588e-05 + 0.999923 * (_ctx_1024t + 0.3 * jax.random.normal(jax.random.fold_in(_rk, 611), (64, 77, 128), jnp.float32))
        return (x, ctx_1024)
    x, ctx_1024 = _rec_inputs()

    def _L0_attn_setup():
        import jax, jax.numpy as jnp
        import numpy as np
        DIM = 128
        DIM_HEAD = 16
        HEADS = 8
        EPS = 1e-05

        def rms_norm(x, gamma):
            n = jnp.sqrt(jnp.sum(x * x, axis=-1, keepdims=True))
            return gamma * (x / jnp.maximum(n, 1e-12)) * x.shape[-1] ** 0.5

        def second_taylor_expansion(x):
            d = x.shape[-1]
            x0 = jnp.ones(x.shape[:-1] + (1,), dtype=x.dtype)
            x2 = jnp.einsum('...i,...j->...ij', x, x) * 0.5 ** 0.5
            x2 = x2.reshape(x.shape[:-1] + (d * d,))
            return jnp.concatenate([x0, x, x2], axis=-1)
        key = jax.random.key(seed)
        ks = jax.random.split(key, 4)
        b, n = (4, 1024)
        dim_inner = DIM_HEAD * HEADS
        x = jax.random.normal(ks[0], (b, n, DIM), dtype=jnp.float32)
        gamma = jnp.ones((DIM,), dtype=jnp.float32)
        w_q = jax.random.normal(ks[1], (DIM, dim_inner), dtype=jnp.float32) * DIM ** (-0.5)
        w_kv = jax.random.normal(ks[2], (DIM, dim_inner * 2), dtype=jnp.float32) * DIM ** (-0.5)
        w_out = jax.random.normal(ks[3], (dim_inner, DIM), dtype=jnp.float32) * dim_inner ** (-0.5)
        return {'x': x, 'gamma': gamma, 'w_q': w_q, 'w_kv': w_kv, 'w_out': w_out}
    _L0_attn_all = _L0_attn_setup()
    _L0_attn_in = {k: v for k, v in _L0_attn_all.items() if k in ('gamma', 'w_q', 'w_kv', 'w_out')}
    del _L0_attn_all

    def _L0_xattn_setup():
        import jax, jax.numpy as jnp
        import numpy as np
        DIM = 128
        NUM_HEADS = 16
        DIM_HEAD = 64
        INNER = NUM_HEADS * DIM_HEAD
        SCALE = DIM_HEAD ** (-0.5)

        def _layernorm(x, gamma, beta, eps=1e-05):
            mu = jnp.mean(x, axis=-1, keepdims=True)
            var = jnp.mean(jnp.square(x - mu), axis=-1, keepdims=True)
            return (x - mu) * jax.lax.rsqrt(var + eps) * gamma + beta
        key = jax.random.key(seed)
        ks = jax.random.split(key, 8)
        B, SQ, SK = (2, 256, 512)
        x = jax.random.normal(ks[0], (B, SQ, DIM), dtype=jnp.float32)
        context = jax.random.normal(ks[1], (B, SK, DIM), dtype=jnp.float32)
        ln_gamma = jnp.ones((DIM,), jnp.float32)
        ln_beta = jnp.zeros((DIM,), jnp.float32)
        w_q = jax.random.normal(ks[2], (DIM, INNER), dtype=jnp.float32) / np.sqrt(DIM)
        w_kv = jax.random.normal(ks[3], (DIM, 2 * INNER), dtype=jnp.float32) / np.sqrt(DIM)
        w_out = jax.random.normal(ks[4], (INNER, DIM), dtype=jnp.float32) / np.sqrt(INNER)
        b_out = jnp.zeros((DIM,), jnp.float32)
        gate = jnp.array([0.5], jnp.float32)
        return {'x': x, 'context': context, 'ln_gamma': ln_gamma, 'ln_beta': ln_beta, 'w_q': w_q, 'w_kv': w_kv, 'w_out': w_out, 'b_out': b_out, 'gate': gate}
    _L0_xattn_all = _L0_xattn_setup()
    _L0_xattn_in = {k: v for k, v in _L0_xattn_all.items() if k in ('ln_gamma', 'ln_beta', 'w_q', 'w_kv', 'w_out', 'b_out', 'gate')}
    del _L0_xattn_all

    def _L0_ffn_setup():
        import jax, jax.numpy as jnp
        import numpy as np
        DIM = 128
        FF_DIM = 512
        N_EXPERTS = 8
        TOP_K = 2
        key = jax.random.key(seed)
        ks = jax.random.split(key, 6)
        s_in = 1.0 / np.sqrt(DIM)
        s_ff = 1.0 / np.sqrt(FF_DIM)
        x = jax.random.normal(ks[0], (4, 256, DIM), dtype=jnp.float32)
        Wr = jax.random.uniform(ks[1], (N_EXPERTS, DIM), jnp.float32, -s_in, s_in)
        W1 = jax.random.uniform(ks[2], (N_EXPERTS, FF_DIM, DIM), jnp.float32, -s_in, s_in)
        b1 = jax.random.uniform(ks[3], (N_EXPERTS, FF_DIM), jnp.float32, -s_in, s_in)
        W2 = jax.random.uniform(ks[4], (N_EXPERTS, DIM, FF_DIM), jnp.float32, -s_ff, s_ff)
        b2 = jax.random.uniform(ks[5], (N_EXPERTS, DIM), jnp.float32, -s_ff, s_ff)
        return {'x': x, 'Wr': Wr, 'W1': W1, 'b1': b1, 'W2': W2, 'b2': b2}
    _L0_ffn_all = _L0_ffn_setup()
    _L0_ffn_in = {k: v for k, v in _L0_ffn_all.items() if k in ('Wr', 'W1', 'b1', 'W2', 'b2')}
    del _L0_ffn_all

    def _L1_attn_setup():
        import jax, jax.numpy as jnp
        import numpy as np
        DIM = 128
        NUM_HEADS = 16
        HEAD_DIM = DIM // NUM_HEADS
        B, L = (4, 256)

        def _alibi_bias_causal(seq_len, dtype):
            h = jnp.arange(1, NUM_HEADS + 1, dtype=jnp.float32)
            slopes = jnp.power(2.0, -8.0 * h / NUM_HEADS)
            pos = jnp.arange(seq_len, dtype=jnp.float32)
            rel = jnp.abs(pos[:, None] - pos[None, :])
            bias = -slopes[:, None, None] * rel[None, :, :]
            causal = pos[:, None] >= pos[None, :]
            bias = jnp.where(causal[None, :, :], bias, -jnp.inf)
            return bias.astype(dtype)
        key = jax.random.key(seed)
        ks = jax.random.split(key, 9)
        s = 0.02
        return {'x': jax.random.normal(ks[0], (B, L, DIM), jnp.float32), 'Wq': jax.random.normal(ks[1], (DIM, DIM), jnp.float32) * s, 'bq': jax.random.normal(ks[2], (DIM,), jnp.float32) * s, 'Wk': jax.random.normal(ks[3], (DIM, DIM), jnp.float32) * s, 'bk': jax.random.normal(ks[4], (DIM,), jnp.float32) * s, 'Wv': jax.random.normal(ks[5], (DIM, DIM), jnp.float32) * s, 'bv': jax.random.normal(ks[6], (DIM,), jnp.float32) * s, 'Wo': jax.random.normal(ks[7], (DIM, DIM), jnp.float32) * s, 'bo': jax.random.normal(ks[8], (DIM,), jnp.float32) * s}
    _L1_attn_all = _L1_attn_setup()
    _L1_attn_in = {k: v for k, v in _L1_attn_all.items() if k in ('Wq', 'bq', 'Wk', 'bk', 'Wv', 'bv', 'Wo', 'bo')}
    del _L1_attn_all

    def _L1_xattn_setup():
        import jax, jax.numpy as jnp
        import numpy as np
        DIM = 128
        N_HEADS = 16
        HEAD_DIM = DIM // N_HEADS
        EPS = 1e-06
        Q_THETA = 32.0
        K_THETA = 1000.0

        def precompute_freqs_1d(dim, seq_len, theta):
            freqs = theta ** (-jnp.arange(0, dim, 2, dtype=jnp.float32) / dim)
            t = jnp.arange(seq_len, dtype=jnp.float32)
            ang = t[:, None] * freqs[None, :]
            return (jnp.cos(ang), jnp.sin(ang))

        def rms_norm(x, w):
            var = jnp.mean(x * x, axis=-1, keepdims=True)
            return x * jax.lax.rsqrt(var + EPS) * w

        def apply_rope(t, cos, sin):
            cos = cos[None, None, :, :]
            sin = sin[None, None, :, :]
            t1, t2 = jnp.split(t, 2, axis=-1)
            return jnp.concatenate([t1 * cos - t2 * sin, t2 * cos + t1 * sin], axis=-1)
        key = jax.random.key(seed)
        ks = jax.random.split(key, 8)
        B, T, S = (128, 64, 48)
        s = 1.0 / np.sqrt(DIM)
        return {'x': jax.random.normal(ks[0], (B, T, DIM), jnp.float32), 'context': jax.random.normal(ks[1], (B, S, DIM), jnp.float32), 'Wq': jax.random.normal(ks[2], (DIM, DIM), jnp.float32) * s, 'Wk': jax.random.normal(ks[3], (DIM, DIM), jnp.float32) * s, 'Wv': jax.random.normal(ks[4], (DIM, DIM), jnp.float32) * s, 'Wo': jax.random.normal(ks[5], (DIM, DIM), jnp.float32) * s, 'q_norm_w': jnp.ones((HEAD_DIM,), jnp.float32), 'k_norm_w': jnp.ones((HEAD_DIM,), jnp.float32)}
    _L1_xattn_all = _L1_xattn_setup()
    _L1_xattn_in = {k: v for k, v in _L1_xattn_all.items() if k in ('Wq', 'Wk', 'Wv', 'Wo', 'q_norm_w', 'k_norm_w')}
    del _L1_xattn_all

    def _L1_ffn_setup():
        import jax, jax.numpy as jnp
        import numpy as np
        DIM = 128
        INTER = 256
        E = 8
        TOPK = 2
        ROUTE_SCALE = 1.0

        def _mlp(x, w1, w2, w3):
            h = jax.nn.silu(x @ w1.T) * (x @ w3.T)
            return h @ w2.T
        key = jax.random.key(seed)
        ks = jax.random.split(key, 10)
        s_in = 0.02
        return {'x': jax.random.normal(ks[0], (4, 256, DIM), dtype=jnp.float32), 'gate_w': jax.random.normal(ks[1], (E, DIM), dtype=jnp.float32) * s_in, 'gate_bias': jax.random.normal(ks[2], (E,), dtype=jnp.float32) * 0.01, 'w1': jax.random.normal(ks[3], (E, INTER, DIM), dtype=jnp.float32) * s_in, 'w2': jax.random.normal(ks[4], (E, DIM, INTER), dtype=jnp.float32) * s_in, 'w3': jax.random.normal(ks[5], (E, INTER, DIM), dtype=jnp.float32) * s_in, 'sw1': jax.random.normal(ks[6], (INTER, DIM), dtype=jnp.float32) * s_in, 'sw2': jax.random.normal(ks[7], (DIM, INTER), dtype=jnp.float32) * s_in, 'sw3': jax.random.normal(ks[8], (INTER, DIM), dtype=jnp.float32) * s_in}
    _L1_ffn_all = _L1_ffn_setup()
    _L1_ffn_in = {k: v for k, v in _L1_ffn_all.items() if k in ('gate_w', 'gate_bias', 'w1', 'w2', 'w3', 'sw1', 'sw2', 'sw3')}
    del _L1_ffn_all
    return {'x': x, 'ctx_1024': ctx_1024, 'L0_attn_gamma': _L0_attn_in['gamma'], 'L0_attn_w_q': _L0_attn_in['w_q'], 'L0_attn_w_kv': _L0_attn_in['w_kv'], 'L0_attn_w_out': _L0_attn_in['w_out'], 'L0_xattn_ln_gamma': _L0_xattn_in['ln_gamma'], 'L0_xattn_ln_beta': _L0_xattn_in['ln_beta'], 'L0_xattn_w_q': _L0_xattn_in['w_q'], 'L0_xattn_w_kv': _L0_xattn_in['w_kv'], 'L0_xattn_w_out': _L0_xattn_in['w_out'], 'L0_xattn_b_out': _L0_xattn_in['b_out'], 'L0_xattn_gate': _L0_xattn_in['gate'], 'L0_ffn_Wr': _L0_ffn_in['Wr'], 'L0_ffn_W1': _L0_ffn_in['W1'], 'L0_ffn_b1': _L0_ffn_in['b1'], 'L0_ffn_W2': _L0_ffn_in['W2'], 'L0_ffn_b2': _L0_ffn_in['b2'], 'L1_attn_Wq': _L1_attn_in['Wq'], 'L1_attn_bq': _L1_attn_in['bq'], 'L1_attn_Wk': _L1_attn_in['Wk'], 'L1_attn_bk': _L1_attn_in['bk'], 'L1_attn_Wv': _L1_attn_in['Wv'], 'L1_attn_bv': _L1_attn_in['bv'], 'L1_attn_Wo': _L1_attn_in['Wo'], 'L1_attn_bo': _L1_attn_in['bo'], 'L1_xattn_Wq': _L1_xattn_in['Wq'], 'L1_xattn_Wk': _L1_xattn_in['Wk'], 'L1_xattn_Wv': _L1_xattn_in['Wv'], 'L1_xattn_Wo': _L1_xattn_in['Wo'], 'L1_xattn_q_norm_w': _L1_xattn_in['q_norm_w'], 'L1_xattn_k_norm_w': _L1_xattn_in['k_norm_w'], 'L1_ffn_gate_w': _L1_ffn_in['gate_w'], 'L1_ffn_gate_bias': _L1_ffn_in['gate_bias'], 'L1_ffn_w1': _L1_ffn_in['w1'], 'L1_ffn_w2': _L1_ffn_in['w2'], 'L1_ffn_w3': _L1_ffn_in['w3'], 'L1_ffn_sw1': _L1_ffn_in['sw1'], 'L1_ffn_sw2': _L1_ffn_in['sw2'], 'L1_ffn_sw3': _L1_ffn_in['sw3']}

def reference(x, ctx_1024, L0_attn_gamma, L0_attn_w_q, L0_attn_w_kv, L0_attn_w_out, L0_xattn_ln_gamma, L0_xattn_ln_beta, L0_xattn_w_q, L0_xattn_w_kv, L0_xattn_w_out, L0_xattn_b_out, L0_xattn_gate, L0_ffn_Wr, L0_ffn_W1, L0_ffn_b1, L0_ffn_W2, L0_ffn_b2, L1_attn_Wq, L1_attn_bq, L1_attn_Wk, L1_attn_bk, L1_attn_Wv, L1_attn_bv, L1_attn_Wo, L1_attn_bo, L1_xattn_Wq, L1_xattn_Wk, L1_xattn_Wv, L1_xattn_Wo, L1_xattn_q_norm_w, L1_xattn_k_norm_w, L1_ffn_gate_w, L1_ffn_gate_bias, L1_ffn_w1, L1_ffn_w2, L1_ffn_w3, L1_ffn_sw1, L1_ffn_sw2, L1_ffn_sw3):
    import jax
    import jax.numpy as jnp

    def _L0_attn_ref(x, gamma, w_q, w_kv, w_out):
        import jax, jax.numpy as jnp
        import numpy as np
        DIM = 128
        DIM_HEAD = 16
        HEADS = 8
        EPS = 1e-05

        def rms_norm(x, gamma):
            n = jnp.sqrt(jnp.sum(x * x, axis=-1, keepdims=True))
            return gamma * (x / jnp.maximum(n, 1e-12)) * x.shape[-1] ** 0.5

        def second_taylor_expansion(x):
            d = x.shape[-1]
            x0 = jnp.ones(x.shape[:-1] + (1,), dtype=x.dtype)
            x2 = jnp.einsum('...i,...j->...ij', x, x) * 0.5 ** 0.5
            x2 = x2.reshape(x.shape[:-1] + (d * d,))
            return jnp.concatenate([x0, x, x2], axis=-1)
        b, n, _ = x.shape
        h, dh = (HEADS, DIM_HEAD)
        normed = rms_norm(x, gamma)
        q = (normed @ w_q).reshape(b, n, h, dh).transpose(0, 2, 1, 3)
        kv = (normed @ w_kv).reshape(b, n, 2, h, dh).transpose(2, 0, 3, 1, 4)
        k, v = (kv[0], kv[1])
        q = q * dh ** (-0.5)
        q = second_taylor_expansion(q)
        k = second_taylor_expansion(k)
        kv_state = jnp.einsum('bhnd,bhne->bhde', k, v)
        k_sum = jnp.sum(k, axis=2)
        den = jnp.einsum('bhnd,bhd->bhn', q, k_sum)
        qk_inv = 1.0 / jnp.maximum(den, EPS)
        out = jnp.einsum('bhnd,bhde->bhne', q, kv_state) * qk_inv[..., None]
        out = out.transpose(0, 2, 1, 3).reshape(b, n, h * dh)
        return out @ w_out

    def _L0_xattn_ref(x, context, ln_gamma, ln_beta, w_q, w_kv, w_out, b_out, gate):
        import jax, jax.numpy as jnp
        import numpy as np
        DIM = 128
        NUM_HEADS = 16
        DIM_HEAD = 64
        INNER = NUM_HEADS * DIM_HEAD
        SCALE = DIM_HEAD ** (-0.5)

        def _layernorm(x, gamma, beta, eps=1e-05):
            mu = jnp.mean(x, axis=-1, keepdims=True)
            var = jnp.mean(jnp.square(x - mu), axis=-1, keepdims=True)
            return (x - mu) * jax.lax.rsqrt(var + eps) * gamma + beta
        B, SQ, _ = x.shape
        SK = context.shape[1]
        xn = _layernorm(x, ln_gamma, ln_beta)
        q = (xn @ w_q).reshape(B, SQ, NUM_HEADS, DIM_HEAD)
        kv = context @ w_kv
        k, v = jnp.split(kv, 2, axis=-1)
        k = k.reshape(B, SK, NUM_HEADS, DIM_HEAD)
        v = v.reshape(B, SK, NUM_HEADS, DIM_HEAD)
        scores = jnp.einsum('bqhd,bkhd->bhqk', q * SCALE, k)
        attn = jax.nn.softmax(scores, axis=-1)
        out = jnp.einsum('bhqk,bkhd->bqhd', attn, v).reshape(B, SQ, INNER)
        out = out @ w_out + b_out
        return out * jnp.tanh(gate[0])

    def _L0_ffn_ref(x, Wr, W1, b1, W2, b2):
        import jax, jax.numpy as jnp
        import numpy as np
        DIM = 128
        FF_DIM = 512
        N_EXPERTS = 8
        TOP_K = 2
        B, T, D = x.shape
        E = Wr.shape[0]
        xf = x.reshape(-1, D)
        logits = jnp.einsum('nd,ed->ne', xf, Wr)
        probs = jax.nn.softmax(logits, axis=-1)
        w, idx = jax.lax.top_k(probs, TOP_K)
        w = w / jnp.sum(w, axis=-1, keepdims=True)
        gate = jnp.sum(jax.nn.one_hot(idx, E, dtype=xf.dtype) * w[..., None], axis=1)
        out = jnp.zeros_like(xf)
        for e in range(E):
            h = jax.nn.gelu(xf @ W1[e].T + b1[e], approximate=False)
            y = h @ W2[e].T + b2[e]
            out = out + gate[:, e:e + 1] * y
        return out.reshape(B, T, D)

    def _L1_attn_ref(x, Wq, bq, Wk, bk, Wv, bv, Wo, bo):
        import jax, jax.numpy as jnp
        import numpy as np
        DIM = 128
        NUM_HEADS = 16
        HEAD_DIM = DIM // NUM_HEADS
        B, L = (4, 256)

        def _alibi_bias_causal(seq_len, dtype):
            h = jnp.arange(1, NUM_HEADS + 1, dtype=jnp.float32)
            slopes = jnp.power(2.0, -8.0 * h / NUM_HEADS)
            pos = jnp.arange(seq_len, dtype=jnp.float32)
            rel = jnp.abs(pos[:, None] - pos[None, :])
            bias = -slopes[:, None, None] * rel[None, :, :]
            causal = pos[:, None] >= pos[None, :]
            bias = jnp.where(causal[None, :, :], bias, -jnp.inf)
            return bias.astype(dtype)
        b, l, d = x.shape
        q = (jnp.einsum('bld,ed->ble', x, Wq) + bq).reshape(b, l, NUM_HEADS, HEAD_DIM).transpose(0, 2, 1, 3)
        k = (jnp.einsum('bld,ed->ble', x, Wk) + bk).reshape(b, l, NUM_HEADS, HEAD_DIM).transpose(0, 2, 1, 3)
        v = (jnp.einsum('bld,ed->ble', x, Wv) + bv).reshape(b, l, NUM_HEADS, HEAD_DIM).transpose(0, 2, 1, 3)
        scale = 1.0 / np.sqrt(HEAD_DIM)
        scores = jnp.einsum('bhqd,bhkd->bhqk', q, k) * scale
        scores = scores + _alibi_bias_causal(l, scores.dtype)[None]
        attn = jax.nn.softmax(scores, axis=-1)
        out = jnp.einsum('bhqk,bhkd->bhqd', attn, v)
        out = out.transpose(0, 2, 1, 3).reshape(b, l, d)
        return jnp.einsum('bld,ed->ble', out, Wo) + bo

    def _L1_xattn_ref(x, context, Wq, Wk, Wv, Wo, q_norm_w, k_norm_w):
        import jax, jax.numpy as jnp
        import numpy as np
        DIM = 128
        N_HEADS = 16
        HEAD_DIM = DIM // N_HEADS
        EPS = 1e-06
        Q_THETA = 32.0
        K_THETA = 1000.0

        def precompute_freqs_1d(dim, seq_len, theta):
            freqs = theta ** (-jnp.arange(0, dim, 2, dtype=jnp.float32) / dim)
            t = jnp.arange(seq_len, dtype=jnp.float32)
            ang = t[:, None] * freqs[None, :]
            return (jnp.cos(ang), jnp.sin(ang))

        def rms_norm(x, w):
            var = jnp.mean(x * x, axis=-1, keepdims=True)
            return x * jax.lax.rsqrt(var + EPS) * w

        def apply_rope(t, cos, sin):
            cos = cos[None, None, :, :]
            sin = sin[None, None, :, :]
            t1, t2 = jnp.split(t, 2, axis=-1)
            return jnp.concatenate([t1 * cos - t2 * sin, t2 * cos + t1 * sin], axis=-1)
        B, T, C = x.shape
        S = context.shape[1]
        H, D = (N_HEADS, HEAD_DIM)
        q = (x @ Wq.T).reshape(B, T, H, D).transpose(0, 2, 1, 3)
        k = (context @ Wk.T).reshape(B, S, H, D).transpose(0, 2, 1, 3)
        v = (context @ Wv.T).reshape(B, S, H, D).transpose(0, 2, 1, 3)
        q = rms_norm(q, q_norm_w)
        k = rms_norm(k, k_norm_w)
        q_cos, q_sin = precompute_freqs_1d(D, T, Q_THETA)
        k_cos, k_sin = precompute_freqs_1d(D, S, K_THETA)
        q = apply_rope(q, q_cos, q_sin)
        k = apply_rope(k, k_cos, k_sin)
        scale = D ** (-0.5)
        attn = jnp.einsum('bhtd,bhsd->bhts', q, k) * scale
        attn = jax.nn.softmax(attn, axis=-1)
        out = jnp.einsum('bhts,bhsd->bhtd', attn, v)
        out = out.transpose(0, 2, 1, 3).reshape(B, T, C)
        return out @ Wo.T

    def _L1_ffn_ref(x, gate_w, gate_bias, w1, w2, w3, sw1, sw2, sw3):
        import jax, jax.numpy as jnp
        import numpy as np
        DIM = 128
        INTER = 256
        E = 8
        TOPK = 2
        ROUTE_SCALE = 1.0

        def _mlp(x, w1, w2, w3):
            h = jax.nn.silu(x @ w1.T) * (x @ w3.T)
            return h @ w2.T
        shape = x.shape
        xt = x.reshape(-1, DIM)
        T = xt.shape[0]
        logits = xt @ gate_w.T
        scores = jax.nn.softmax(logits.astype(jnp.float32), axis=-1)
        original_scores = scores
        biased = scores + gate_bias
        _, indices = jax.lax.top_k(biased, TOPK)
        weights = jnp.take_along_axis(original_scores, indices, axis=1)
        weights = (weights * ROUTE_SCALE).astype(x.dtype)
        combine = (jax.nn.one_hot(indices, E, dtype=weights.dtype) * weights[..., None]).sum(axis=1)
        y = jnp.zeros_like(xt)
        for e in range(E):
            y = y + _mlp(xt, w1[e], w2[e], w3[e]) * combine[:, e:e + 1]
        z = _mlp(xt, sw1, sw2, sw3)
        return (y + z).reshape(shape)
    x = _layernorm(x + _L0_attn_ref(x, L0_attn_gamma, L0_attn_w_q, L0_attn_w_kv, L0_attn_w_out), axis=-1)
    x = _layernorm(x + _L0_xattn_ref(x, ctx_1024, L0_xattn_ln_gamma, L0_xattn_ln_beta, L0_xattn_w_q, L0_xattn_w_kv, L0_xattn_w_out, L0_xattn_b_out, L0_xattn_gate), axis=-1)
    x = _layernorm(x + _L0_ffn_ref(x, L0_ffn_Wr, L0_ffn_W1, L0_ffn_b1, L0_ffn_W2, L0_ffn_b2), axis=-1)
    x = _layernorm(x + _L1_attn_ref(x, L1_attn_Wq, L1_attn_bq, L1_attn_Wk, L1_attn_bk, L1_attn_Wv, L1_attn_bv, L1_attn_Wo, L1_attn_bo), axis=-1)
    x = _layernorm(x + _L1_xattn_ref(x, ctx_1024, L1_xattn_Wq, L1_xattn_Wk, L1_xattn_Wv, L1_xattn_Wo, L1_xattn_q_norm_w, L1_xattn_k_norm_w), axis=-1)
    x = _layernorm(x + _L1_ffn_ref(x, L1_ffn_gate_w, L1_ffn_gate_bias, L1_ffn_w1, L1_ffn_w2, L1_ffn_w3, L1_ffn_sw1, L1_ffn_sw2, L1_ffn_sw3), axis=-1)
    return x

_drawn_inputs = setup_inputs


def setup_inputs(seed=0):
    import zlib

    import numpy as np

    out = dict(_drawn_inputs(seed))
    spreads = {'L0_attn_gamma': (1.0, 0.2),
     'L0_xattn_ln_gamma': (1.0, 0.6),
     'L0_xattn_ln_beta': (0.0, 0.525),
     'L0_xattn_b_out': (0.0, 0.1),
     'L1_xattn_q_norm_w': (1.0, 0.2),
     'L1_xattn_k_norm_w': (1.0, 0.2)}
    factors = {'L0_ffn_b1': 4.844,
     'L0_ffn_b2': 3.477,
     'L1_attn_Wq': 8.0,
     'L1_attn_bq': 8.0,
     'L1_attn_Wk': 8.0,
     'L1_attn_bk': 8.0,
     'L1_attn_Wv': 3.194,
     'L1_attn_bv': 8.0,
     'L1_attn_Wo': 3.07,
     'L1_attn_bo': 3.03,
     'L1_ffn_gate_w': 8.0,
     'L1_ffn_gate_bias': 8.0,
     'L1_ffn_w1': 8.0,
     'L1_ffn_w2': 8.0,
     'L1_ffn_w3': 8.0,
     'L1_ffn_sw1': 6.937,
     'L1_ffn_sw2': 6.927,
     'L1_ffn_sw3': 6.907}
    for name, (base, spread) in spreads.items():
        noise = np.random.default_rng([zlib.crc32(name.encode()), seed]).standard_normal(out[name].shape)
        drawn = base * np.exp(spread * noise) if base else spread * noise
        out[name] = jnp.asarray(drawn.astype(out[name].dtype))
    for name, factor in factors.items():
        out[name] = (out[name] * factor).astype(out[name].dtype)
    return out
```

```python
from contextlib import ExitStack

import concourse.bass as bass
from concourse import mybir

P = 128
F32 = mybir.dt.float32
ALU = mybir.AluOpType
ACT = mybir.ActivationFunctionType
AX = mybir.AxisListType
PEEL = 4
LN_EPS = 1e-5


class At:

    def __init__(self, c, i=None, unroll=4):
        self.c, self.i, self.unroll = c, i, unroll

    def back(self, n):
        return At(self.c - n, self.i, self.unroll)

    @property
    def real(self):
        return self.c >= 0 if self.i is None else self.c + PEEL >= 0

    def count(self, per, k):
        assert self.real
        v = self.c * per + k
        return v if self.i is None else self.i * (self.unroll * per) + v

    def load(self, slots):
        v = 16 * (self.c // slots + 1)
        return v if self.i is None else self.i * (16 * self.unroll // slots) + v

    def index(self, scale=1, plus=0):
        v = self.c * scale + plus
        return v if self.i is None else self.i * (self.unroll * scale) + v


def run_steps(engine, step, units, stages, unroll):
    for t in range(PEEL):
        step(*[At(t - s, None, unroll) if 0 <= t - s < units else None for s in range(stages)])
    with engine.Fori(PEEL // unroll, units // unroll) as i:
        for t in range(unroll):
            step(*[At(t - s, i, unroll) for s in range(stages)])
    for t in range(units, units + stages - 1):
        step(*[At(t - s, None, unroll) if 0 <= t - s < units else None for s in range(stages)])


class Chip:

    def __init__(self, nc, ctx):
        self.nc, self.used = nc, []
        self.banks = ctx.enter_context(nc.psum_tensor("banks", [P, 8, 512], F32))

    def sb(self, ctx, name, shape, dt=F32):
        return ctx.enter_context(self.nc.sbuf_tensor(name, shape, dt))

    def sem(self, ctx, name):
        self.used.append(ctx.enter_context(self.nc.semaphore(name)))
        return self.used[-1]

    def clear_semaphores(self):
        used, self.used = self.used, []
        with self.nc.Block() as block:
            @block.gpsimd
            def _(pool):
                for s in used:
                    pool.sem_clear(s)


def load_x(sp, source, xin, loaded, freed, unit, slots, per, width):
    if unit.back(slots).real:
        sp.wait_ge(freed, unit.back(slots).count(1, 1))
    s = unit.c % slots
    sp.dma_start(xin[:, s], source(unit, width)).then_inc(loaded[s], 16)


def taylor_attention(chip, n_seq, x_dram, X, w, consts):
    nc = chip.nc
    H, D = 8, 16
    with ExitStack() as ctx:
        def sb(name, shape):
            return chip.sb(ctx, "taylor_" + name, shape)

        def sem(name):
            return chip.sem(ctx, "taylor_" + name)

        wq, wk, wv = (sb(n, [P, P]) for n in ("wq", "wk", "wv"))
        ones = sb("ones", [P, P])
        power, eps = sb("power", [P, 1]), sb("eps", [P, 1])
        xin = sb("xin", [P, 4, P])
        squares = sb("squares", [P, P])
        sumsq = sb("sumsq", [P, 4])
        guarded = sb("guarded", [P, 4])
        inv_norm = sb("inv_norm", [P, 4])
        xs = sb("xs", [P, 2, P])
        xsT = sb("xsT", [P, 2, P])
        q_masked = sb("q_masked", [P, 2, H, P])
        kT = sb("kT", [P, 2, P])
        v_one = sb("v_one", [P, 2, H, D + 1])
        weights = sb("weights", [P, 2, 4, P])
        den = sb("den", [P, 2, H])
        inv_den = sb("inv_den", [P, 2, H])
        o = sb("o", [P, 2, P])
        oT = sb("oT", [P, 2, P])
        z = sb("z", [P, 4, P])
        stats = sb("stats", [P, 6])
        mean_var = sb("mean_var", [P, 4, 2])
        var_eps = sb("var_eps", [P, 4])
        rstd = sb("rstd", [P, 4])
        xsT_bank, q_bank, kv_bank, o_bank, oT_bank, y_bank = (chip.banks[:, n] for n in (0, 1, 2, 5, 6, 7))
        s_bank = [chip.banks[:, 3], chip.banks[:, 4]]

        x_loaded = [sem(f"x_loaded{n}") for n in range(4)]
        power_ready, ready = sem("power_ready"), sem("ready")
        sumsq_done, guarded_done, inv_norm_done, xs_done, xsT_ps, xsT_done = (
            sem(n) for n in ("sumsq_done", "guarded_done", "inv_norm_done", "xs_done", "xsT_ps", "xsT_done"))
        q_ps, kv_ps, q_done, k_done, v_done, s_ps, weights_done = (
            sem(n) for n in ("q_ps", "kv_ps", "q_done", "k_done", "v_done", "s_ps", "weights_done"))
        o_ps, den_done, inv_den_done, o_done, oT_ps, oT_done, y_ps = (
            sem(n) for n in ("o_ps", "den_done", "inv_den_done", "o_done", "oT_ps", "oT_done", "y_ps"))
        z_done, stats_done, mean_done, var_done, rstd_done, x_written = (
            sem(n) for n in ("z_done", "stats_done", "mean_done", "var_done", "rstd_done", "x_written"))
        block = ctx.enter_context(nc.Block())

        @block.sync
        def _(sp):
            def step(f):
                if f is not None:
                    load_x(sp, lambda u, n: x_dram[u.index()], xin, x_loaded, z_done, f, 4, 1, P)

            run_steps(sp, step, n_seq, 1, 4)

        @block.gpsimd
        def _(pool):
            pool.memset(power[:], -0.5).then_inc(power_ready, 1)
            pool.memset(eps[:], LN_EPS).then_inc(power_ready, 1)
            pool.wait_ge(power_ready, 2)

            def step(f, c, u, n):
                if f is not None:
                    s = f.c % 4
                    pool.wait_ge(sumsq_done, f.count(1, 1))
                    pool.nop(nofuse=True)
                    pool.tensor_scalar(guarded[:, s:s + 1], sumsq[:, s:s + 1], 1e-24, None, ALU.max).then_inc(guarded_done, 1)
                    pool.wait_ge(guarded_done, f.count(1, 1))
                    pool.tensor_tensor(inv_norm[:, s:s + 1], guarded[:, s:s + 1], power[:], ALU.pow).then_inc(inv_norm_done, 1)
                if u is not None:
                    s = u.c % 4
                    pool.wait_ge(mean_done, u.count(1, 1))
                    pool.tensor_tensor(var_eps[:, s:s + 1], mean_var[:, s, 1:2], eps[:], ALU.add).then_inc(var_done, 1)
                    pool.wait_ge(var_done, u.count(1, 1))
                    pool.tensor_tensor(rstd[:, s:s + 1], var_eps[:, s:s + 1], power[:], ALU.pow).then_inc(rstd_done, 1)

            run_steps(pool, step, n_seq, 4, 4)

        @block.scalar
        def _(act):
            def step(f, c, u):
                if f is not None:
                    s = f.c % 4
                    act.wait_ge(x_loaded[s], f.load(4))
                    act.activation(squares[:], xin[:, s], ACT.Square, accum_out=sumsq[:, s:s + 1]).then_inc(sumsq_done, 1)
                if c is not None:
                    for j in range(2):
                        act.wait_ge(s_ps, c.count(2, j + 1))
                        act.activation(weights[:, j], s_bank[j].rearrange("p (h q) -> p h q", h=4), ACT.Square,
                                       bias=1.0, scale=0.25).then_inc(weights_done, 1)
                if u is not None:
                    act.wait_ge(oT_ps, u.count(1, 1))
                    act.activation(oT[:, u.c % 2], oT_bank[:, 0:P], ACT.Copy).then_inc(oT_done, 1)
                if f is not None:
                    s = f.c % 2
                    act.wait_ge(xsT_ps, f.count(1, 1))
                    act.activation(xsT[:, s], xsT_bank[:, 0:P], ACT.Copy).then_inc(xsT_done, 1)
                    act.wait_ge(kv_ps, f.count(1, 1))
                    act.activation(kT[:, s], kv_bank[:, 0:P], ACT.Copy).then_inc(k_done, 1)
                    act.activation(v_one[:, s, :, 0:D], kv_bank[:, P:2 * P].rearrange("p (h d) -> p h d", h=H),
                                   ACT.Copy).then_inc(v_done, 1)

            run_steps(act, step, n_seq, 3, 4)

        @block.vector
        def _(dve):
            for t, name in ((wq, "wq"), (wk, "wk"), (wv, "wv")):
                dve.tensor_scalar(t[:], w[name], w["gamma"], float(P) ** 0.5, ALU.mult, ALU.mult).then_inc(ready, 1)
            dve.memset(ones[:], 1.0).then_inc(ready, 1)
            dve.memset(v_one[:], 1.0).then_inc(ready, 1)

            def step(f, c, u, n):
                if n is not None:
                    s = n.c % 4
                    dve.wait_ge(rstd_done, n.count(1, 1))
                    dve.tensor_scalar(X[:, n.index(), :], z[:, s], mean_var[:, s, 0:1], rstd[:, s:s + 1],
                                      ALU.subtract, ALU.mult).then_inc(x_written, 1)
                if u is not None:
                    s = u.c % 2
                    sums = o_bank[:, 0:H * (D + 1)].rearrange("p (h d) -> p h d", h=H)
                    dve.wait_ge(o_ps, u.count(1, 1))
                    dve.tensor_scalar(den[:, s], sums[:, :, D], 2e-5, None, ALU.max).then_inc(den_done, 1)
                    dve.wait_ge(den_done, u.count(1, 1))
                    dve.reciprocal(inv_den[:, s], den[:, s]).then_inc(inv_den_done, 1)
                    dve.wait_ge(inv_den_done, u.count(1, 1))
                    dve.tensor_tensor(o[:, s].rearrange("p (h d) -> p h d", h=H), sums[:, :, 0:D],
                                      inv_den[:, s].unsqueeze(2).to_broadcast([P, H, D]), ALU.mult).then_inc(o_done, 1)
                if f is not None:
                    s = f.c % 2
                    dve.wait_ge(inv_norm_done, f.count(1, 1))
                    dve.tensor_scalar(xs[:, s], xin[:, f.c % 4], inv_norm[:, f.c % 4:f.c % 4 + 1], None,
                                      ALU.mult).then_inc(xs_done, 1)
                    dve.wait_ge(q_ps, f.count(1, 1))
                    if f.back(2).real:
                        dve.wait_ge(s_ps, f.back(2).count(2, 2))
                    dve.tensor_tensor(q_masked[:, s], q_bank[:, 0:P].unsqueeze(1).to_broadcast([P, H, P]),
                                      consts["heads8"].unsqueeze(2).to_broadcast([P, H, P]), ALU.mult).then_inc(q_done, 1)
                if u is not None:
                    s = u.c % 4
                    dve.wait_ge(y_ps, u.count(1, 1))
                    dve.tensor_tensor(z[:, s], y_bank[:, 0:P], xin[:, s], ALU.add).then_inc(z_done, 1)
                    dve.wait_ge(z_done, u.count(1, 1))
                    dve.bn_stats(stats[:], z[:, s]).then_inc(stats_done, 1)
                    dve.wait_ge(stats_done, u.count(1, 1))
                    dve.nop(nofuse=True)
                    dve.bn_aggr(mean_var[:, s], stats[:]).then_inc(mean_done, 1)

            run_steps(dve, step, n_seq, 4, 4)

        @block.tensor
        def _(pe):
            pe.wait_ge(ready, 5)
            ident = consts["ident"]

            def step(f, c, u):
                if c is not None:
                    s = c.c % 2
                    pe.wait_ge(q_done, c.count(1, 1))
                    pe.wait_ge(k_done, c.count(1, 1))
                    for j in range(2):
                        if c.back(1).real:
                            pe.wait_ge(weights_done, c.back(1).count(2, j + 1))
                        pe.matmul(s_bank[j], kT[:, s], q_masked[:, s, 4 * j:4 * j + 4], start=True, stop=True).then_inc(s_ps, 1)
                if u is not None:
                    s = u.c % 2
                    pe.wait_ge(o_done, u.count(1, 1))
                    if u.back(1).real:
                        pe.wait_ge(oT_done, u.back(1).count(1, 1))
                    pe.transpose(oT_bank[:, 0:P], o[:, s], ident).then_inc(oT_ps, 1)
                if f is not None:
                    s = f.c % 2
                    pe.wait_ge(xs_done, f.count(1, 1))
                    if f.back(1).real:
                        pe.wait_ge(xsT_done, f.back(1).count(1, 1))
                    pe.transpose(xsT_bank[:, 0:P], xs[:, s], ident).then_inc(xsT_ps, 1)
                if c is not None:
                    s = c.c % 2
                    pe.wait_ge(v_done, c.count(1, 1))
                    if c.back(1).real:
                        pe.wait_ge(o_done, c.back(1).count(1, 1))
                    pe.matmul(o_bank[:, 0:H * (D + 1)], ones[:], v_one[:, s].rearrange("p h d -> p (h d)"),
                              start=True, stop=False, skip_group_check=True)
                    for h in range(H):
                        pe.wait_ge(weights_done, c.count(2, h // 4 + 1))
                        mm = pe.matmul(o_bank[:, h * (D + 1):(h + 1) * (D + 1)], weights[:, h // 4, h % 4], v_one[:, s, h],
                                       start=False, stop=h == H - 1, skip_group_check=True)
                    mm.then_inc(o_ps, 1)
                if f is not None:
                    s = f.c % 2
                    pe.wait_ge(xsT_done, f.count(1, 1))
                    if f.back(1).real:
                        pe.wait_ge(q_done, f.back(1).count(1, 1))
                        pe.wait_ge(v_done, f.back(1).count(1, 1))
                    pe.matmul(q_bank[:, 0:P], wq[:], xsT[:, s], start=True, stop=True).then_inc(q_ps, 1)
                    pe.matmul(kv_bank[:, 0:P], wk[:], xsT[:, s], start=True, stop=True)
                    pe.matmul(kv_bank[:, P:2 * P], xsT[:, s], wv[:], start=True, stop=True).then_inc(kv_ps, 1)
                if u is not None:
                    s = u.c % 2
                    pe.wait_ge(oT_done, u.count(1, 1))
                    if u.back(1).real:
                        pe.wait_ge(z_done, u.back(1).count(1, 1))
                    pe.matmul(y_bank[:, 0:P], oT[:, s], w["wo"], start=True, stop=True).then_inc(y_ps, 1)

            run_steps(pe, step, n_seq, 3, 4)


def softmax_attention(chip, kind, n_seq, X, ctxT_dram, w, consts):
    nc = chip.nc
    H = 16
    D = 64 if kind == "wide" else 8
    NK = P if kind == "causal" else 77
    HU = 4
    UB = H // HU
    NU = 2 * UB
    OG = NU if kind == "wide" else 2
    OW = HU * (D + 1) * (NU // OG)
    n_pairs = n_seq // 2
    FU = {"wide": 11, "causal": 4, "rotary": 4}[kind]
    YU = {"wide": 5, "causal": 2, "rotary": 2}[kind]
    NC = H * D // P
    with ExitStack() as ctx:
        def sb(name, shape):
            return chip.sb(ctx, kind + "_" + name, shape)

        def sem(name):
            return chip.sem(ctx, kind + "_" + name)

        power = sb("power", [P, 64])
        eps = sb("eps", [P, 2])
        xin = sb("xin", [P, 4, 2, P])
        xT = sb("xT", [P, 2, 2, P])
        v_one = sb("v_one", [P, 2, 2, H, D + 1])
        keys = sb("keys", [P, 2, H, 2, NK] if kind == "wide" else [P, 2, 2, H, NK])
        shifted = sb("shifted", [P, 2, HU * NK])
        probs = sb("probs", [P, 2, HU, NK])
        probsT = sb("probsT", [P, 2, HU * P])
        row_max = sb("row_max", [P, 2, HU])
        inv_sum = sb("inv_sum", [P, 2, HU * (NU // OG)])
        o = sb("o", [P, 2, 2, H * D])
        oT = sb("oT", [P, 2, NC, P])
        residual = sb("residual", [P, 2, 2, P])
        z = sb("z", [P, 4, 2, P])
        stats = sb("stats", [P, 2, 6])
        mean_var = sb("mean_var", [P, 4, 2, 2])
        var_eps = sb("var_eps", [P, 4, 2])
        rstd = sb("rstd", [P, 4, 2])
        if kind != "causal":
            ctxT = sb("ctxT", [P, 4, 2, P])
        if kind == "wide":
            xn = sb("xn", [P, 2, P])
            pre_stats = sb("pre_stats", [P, 2, 6])
            pre_mean_var = sb("pre_mean_var", [P, 2, 2])
            pre_var_eps = sb("pre_var_eps", [P, 2])
            pre_rstd = sb("pre_rstd", [P, 2])
            product = sb("product", [P, H, P])
        else:
            qT = sb("qT", [P, 2, 2, P])
            kT = sb("kT", [P, 2, P])
        if kind == "rotary":
            qk = sb("qk", [P, 2, 2, H, 8])
            qk_sq = sb("qk_sq", [P, 4, H, 8])
            qk_eps = sb("qk_eps", [P, 4 * H])
            qk_sum = sb("qk_sum", [P, 4 * H])
            qk_mean = sb("qk_mean", [P, 4 * H])
            qk_rstd = sb("qk_rstd", [P, 4 * H])
            turned = sb("turned", [P, 4, H, 8])
            crossed = sb("crossed", [P, 4, H, 8])
            table = sb("table", [P, 2, 2, 8])
        if kind == "causal":
            biased = sb("biased", [P, 2, HU * NK])
            value_row = sb("value_row", [P, P])
            q_bias = sb("q_bias", [P, 1])
        extra = sb("extra", [P, P])

        s_bank = [chip.banks[:, 0], chip.banks[:, 1]]
        p_bank = [chip.banks[:, 2], chip.banks[:, 3]]
        o_bank = [chip.banks[:, 4], chip.banks[:, 5]]
        f_bank, y_bank = chip.banks[:, 6], chip.banks[:, 7]

        x_loaded = [sem(f"x_loaded{n}") for n in range(4)]
        ready, prepared, prepared_ps, product_done = (sem(n) for n in ("ready", "prepared", "prepared_ps", "product_done"))
        READY = 5 if kind == "rotary" else 4
        PREPARED = {"wide": 2, "causal": 3, "rotary": 6}[kind]
        front_ps, front_done, keys_done = sem("front_ps"), sem("front_done"), sem("keys_done")
        s_ps, max_done, shifted_done, probs_done = (sem(n) for n in ("s_ps", "max_done", "shifted_done", "probs_done"))
        biased_done = sem("biased_done")
        probsT_ps, probsT_done, pv_done = (sem(n) for n in ("probsT_ps", "probsT_done", "pv_done"))
        inv_done, o_done, tail_ps, tail_done, residual_done = (
            sem(n) for n in ("inv_done", "o_done", "tail_ps", "tail_done", "residual_done"))
        z_done, stats_done, mean_done, var_done, rstd_done, x_written = (
            sem(n) for n in ("z_done", "stats_done", "mean_done", "var_done", "rstd_done", "x_written"))
        pre_done, pre_var_done, pre_rstd_done, turn_done = (
            sem(n) for n in ("pre_done", "pre_var_done", "pre_rstd_done", "turn_done"))
        square_done, qk_mean_done, qk_rstd_done = (sem(n) for n in ("square_done", "qk_mean_done", "qk_rstd_done"))
        block = ctx.enter_context(nc.Block())
        TURNS = 3

        def lagged(c, u, k, lag):
            if k - lag >= 0:
                return (c, k - lag) if c is not None else None
            return (u, k - lag + NU) if u is not None else None

        def before(pair, k, n):
            pair = pair.back((n - k + NU - 1) // NU) if n > k else pair
            return (pair, (k - n) % NU) if pair.real else None

        @block.sync
        def _(sp):
            def step(f):
                if f is None:
                    return
                s = f.c % 4
                if f.back(4).real:
                    sp.wait_ge(z_done, f.back(4).count(1, 1))
                sp.dma_start(xin[:, s], X[:, bass.ds(f.index(2), 2), :]).then_inc(x_loaded[s], 16)
                if kind != "causal":
                    sp.dma_start(ctxT[:, s, :, 0:77], ctxT_dram[:, bass.ds(f.index(2), 2), :]).then_inc(x_loaded[s], 16)

            if kind != "causal":
                sp.wait_ge(ready, READY)
            run_steps(sp, step, n_pairs, 1, 4)

        def wait_loaded(engine, f):
            m = 2 if kind != "causal" else 1
            v = 16 * m * (f.c // 4 + 1)
            engine.wait_ge(x_loaded[f.c % 4], v if f.i is None else f.i * (16 * m) + v)

        @block.gpsimd
        def _(pool):
            pool.memset(power[:], -0.5).then_inc(ready, 1)
            pool.memset(v_one[:], 1.0).then_inc(ready, 1)
            pool.memset(eps[:, 0:2], LN_EPS).then_inc(ready, 1)
            if kind == "rotary":
                pool.memset(qk_eps[:], 8e-6).then_inc(ready, 1)
            pool.memset(value_row[:] if kind == "causal" else ctxT[:], 1.0 if kind == "causal" else 0.0).then_inc(ready, 1)
            pool.wait_ge(ready, READY)
            pool.wait_ge(prepared, PREPARED)

            def step(f, c, u, n):
                if f is not None and kind == "wide":
                    pool.wait_ge(pre_done, f.count(4, 4))
                    pool.tensor_tensor(pre_var_eps[:], pre_mean_var[:, :, 1], eps[:], ALU.add).then_inc(pre_var_done, 1)
                    pool.wait_ge(pre_var_done, f.count(1, 1))
                    pool.tensor_tensor(pre_rstd[:], pre_var_eps[:], power[:, 0:2], ALU.pow).then_inc(pre_rstd_done, 1)
                if f is not None and kind == "rotary":
                    pool.wait_ge(square_done, f.count(2, 2))
                    pool.tensor_tensor(qk_mean[:], qk_sum[:], qk_eps[:], ALU.add).then_inc(qk_mean_done, 1)
                    pool.wait_ge(qk_mean_done, f.count(1, 1))
                    if f.back(1).real:
                        pool.wait_ge(turn_done, f.back(1).count(TURNS, TURNS))
                    pool.tensor_tensor(qk_rstd[:], qk_mean[:], power[:], ALU.pow).then_inc(qk_rstd_done, 1)
                if c is not None and kind != "rotary":
                    wait_loaded(pool, c)
                    if c.back(2).real:
                        pool.wait_ge(z_done, c.back(2).count(1, 1))
                    pool.tensor_tensor(residual[:, c.c % 2], xin[:, c.c % 4], extra[:].unsqueeze(1).to_broadcast([P, 2, P]),
                                       ALU.add).then_inc(residual_done, 1)
                if f is not None and kind != "wide":
                    pool.wait_ge(front_done, f.count(FU, 4 if kind == "rotary" else 2))
                    if f.back(2).real:
                        pool.wait_ge(s_ps, f.back(2).count(NU, NU))
                    for b in range(2):
                        pool.tensor_tensor(keys[:, f.c % 2, b], kT[:, b, 0:NK].unsqueeze(1).to_broadcast([P, H, NK]),
                                           consts["heads16"].unsqueeze(2).to_broadcast([P, H, NK]), ALU.mult).then_inc(keys_done, 1)
                if u is not None:
                    s = u.c % 4
                    pool.wait_ge(mean_done, u.count(2, 2))
                    pool.tensor_tensor(var_eps[:, s], mean_var[:, s, :, 1], eps[:], ALU.add).then_inc(var_done, 1)
                    pool.wait_ge(var_done, u.count(1, 1))
                    pool.tensor_tensor(rstd[:, s], var_eps[:, s], power[:, 0:2], ALU.pow).then_inc(rstd_done, 1)

            run_steps(pool, step, n_pairs, 4, 4)

        ident = consts["ident"]

        def front_pe(pe, f, m):
            s2, s4 = f.c % 2, f.c % 4
            if m == 0:
                if kind == "wide":
                    pe.wait_ge(turn_done, f.count(2, 2))
                else:
                    wait_loaded(pe, f)
                for b in range(2):
                    last = pe.transpose(f_bank[:, b * P:(b + 1) * P], xn[:, b] if kind == "wide" else xin[:, s4, b], ident)
                return last
            if kind == "wide":
                if m <= 6:
                    first = 3 * (m - 1)
                    wait_loaded(pe, f)
                    for n in range(min(3, H - first)):
                        last = pe.matmul(f_bank[:, n * 154:(n + 1) * 154], product[:, first + n], ctxT[:, s4, :, 0:NK],
                                         start=True, stop=True)
                else:
                    b, half = divmod(m - 7, 2)
                    last = pe.matmul(f_bank[0:NK, :], ctxT[:, s4, b, 0:NK], w["wv"][:, half * 512:(half + 1) * 512],
                                     start=True, stop=True)
                return last
            pe.wait_ge(front_done, f.count(FU, 1))
            if kind == "causal":
                if m == 3:
                    for b in range(2):
                        last = pe.matmul(f_bank[:, b * P:(b + 1) * P], xT[:, s2, b], w["wv"], start=True, stop=True)
                    return last
                return pe.matmul(f_bank[:, 0:2 * P], w["wk"] if m == 1 else w["wq"], xT[:, s2], start=True, stop=True)
            if m == 1:
                for b in range(2):
                    pe.matmul(f_bank[:, 2 * b * P:(2 * b + 1) * P], xT[:, s2, b], w["wq"], start=True, stop=True)
                    last = pe.matmul(f_bank[:, (2 * b + 1) * P:(2 * b + 2) * P], ctxT[:, s4, b], w["wk"], start=True, stop=True)
            elif m == 2:
                for b in range(2):
                    last = pe.matmul(f_bank[0:NK, b * P:(b + 1) * P], ctxT[:, s4, b, 0:NK], w["wv"], start=True, stop=True)
            else:
                pe.wait_ge(turn_done, f.count(TURNS, TURNS))
                for n in range(4):
                    last = pe.transpose(f_bank[:, n * P:(n + 1) * P], turned[:, n].rearrange("p h d -> p (h d)"), ident)
            return last

        def front_act(act, f, m):
            s2 = f.c % 2
            copy = ACT.Copy
            if kind == "wide":
                if m == 0:
                    return act.activation(xT[:, s2], f_bank[:, 0:2 * P].rearrange("p (b q) -> p b q", b=2), ACT.Identity,
                                          scale=w["gamma"], bias=w["beta"])
                if m <= 6:
                    first = 3 * (m - 1)
                    n = min(3, H - first)
                    return act.activation(keys[:, s2, first:first + n],
                                          f_bank[:, 0:n * 154].rearrange("p (h b k) -> p h b k", h=n, b=2), copy)
                b, half = divmod(m - 7, 2)
                return act.activation(v_one[0:NK, s2, b, 8 * half:8 * half + 8, 0:D],
                                      f_bank[0:NK, :].rearrange("p (h d) -> p h d", h=8), copy)
            if m == 0:
                return act.activation(xT[:, s2], f_bank[:, 0:2 * P].rearrange("p (b q) -> p b q", b=2), copy)
            if kind == "causal":
                two = f_bank[:, 0:2 * P].rearrange("p (b q) -> p b q", b=2)
                if m == 1:
                    if f.back(1).real:
                        act.wait_ge(keys_done, f.back(1).count(2, 2))
                    return act.activation(kT[:], two, ACT.Identity, bias=w["bk"])
                if m == 2:
                    return act.activation(qT[:, s2], two, ACT.Identity, bias=q_bias[:], scale=8.0 ** -0.5)
                return act.activation(v_one[:, s2, :, :, 0:D], f_bank[:, 0:2 * P].rearrange("p (b h d) -> p b h d", b=2, h=H), copy)
            if m == 1:
                if f.back(1).real:
                    act.wait_ge(turn_done, f.back(1).count(TURNS, 1))
                return act.activation(qk[:].rearrange("p b t h d -> p (b t h d)"), f_bank, copy)
            if m == 2:
                return act.activation(v_one[0:NK, s2, :, :, 0:D],
                                      f_bank[0:NK, 0:2 * P].rearrange("p (b h d) -> p b h d", b=2, h=H), copy)
            if f.back(1).real:
                act.wait_ge(keys_done, f.back(1).count(2, 2))
            four = f_bank.rearrange("p (b t q) -> p b t q", b=2, t=2)
            act.activation(qT[:, s2], four[:, :, 0], copy)
            return act.activation(kT[:], four[:, :, 1], copy)

        FRONT_AT = {"wide": [2, 2, 3, 3, 4, 4, 5, 5, 6, 6, 7], "causal": [0, 1, 2, 3], "rotary": [0, 1, 2, 5]}[kind]
        TAIL_AT = {"wide": [2, 3, 4, 5, 6], "causal": [3, 5], "rotary": [3, 5]}[kind]
        TLAG, PLAG = 1, 2

        @block.tensor
        def _(pe):
            pe.wait_ge(ready, READY)
            if kind == "wide":
                for h in range(H):
                    if h >= 1:
                        pe.wait_ge(product_done, h)
                    pe.matmul(f_bank[:, 0:P], w["wkT"][:, h], w["wqT"][:, h], start=True, stop=True).then_inc(prepared_ps, 1)
                pe.wait_ge(product_done, H)
                pe.wait_ge(prepared, PREPARED)
            elif kind == "causal":
                pe.wait_ge(prepared, 1)
                pe.matmul(f_bank[:, 0:P], value_row[:], w["wo"], start=True, stop=True).then_inc(prepared_ps, 1)
                pe.wait_ge(prepared, PREPARED)
            else:
                pe.wait_ge(prepared, PREPARED)

            def front(f, k):
                for m in range(FU):
                    if FRONT_AT[m] == k:
                        if m >= 1:
                            pe.wait_ge(front_done, f.count(FU, m))
                        elif f.back(1).real:
                            pe.wait_ge(front_done, f.back(1).count(FU, FU))
                        front_pe(pe, f, m).then_inc(front_ps, 1)

            def tail(u, k):
                for m in range(YU):
                    if TAIL_AT[m] != k:
                        continue
                    if m >= 1:
                        pe.wait_ge(tail_done, u.count(YU - 1, m))
                    elif u.back(1).real:
                        pe.wait_ge(z_done, u.back(1).count(1, 1))
                    if m < YU - 1:
                        pe.wait_ge(o_done, u.count(OG, OG) if kind != "wide" else u.count(OG, 4 * (m // 2) + 4))
                        for n in range(4 if kind == "wide" else 2):
                            b, chunk = (m // 2, 4 * (m % 2) + n) if kind == "wide" else (n, 0)
                            last = pe.transpose(y_bank[:, n * P:(n + 1) * P], o[:, u.c % 2, b, chunk * P:(chunk + 1) * P], ident)
                    else:
                        for b in range(2):
                            for n in range(NC):
                                last = pe.matmul(y_bank[:, b * P:(b + 1) * P], oT[:, b, n],
                                                 wide_out[:, n] if kind == "wide" else w["wo"],
                                                 start=n == 0, stop=n == NC - 1)
                    last.then_inc(tail_ps, 1)

            wide_out = w["wo_scaled"] if kind == "wide" else None

            def step(f, c, u):
                for k in range(NU):
                    if c is not None:
                        b, j = divmod(k, UB)
                        if k == 0:
                            pe.wait_ge(front_done, c.count(FU, FU))
                            if kind != "wide":
                                pe.wait_ge(keys_done, c.count(2, 2))
                        if before(c, k, 2) is not None:
                            bc, bk = before(c, k, 2)
                            pe.wait_ge(shifted_done, bc.count(NU, bk + 1))
                        if kind == "wide":
                            q = xT[:, c.c % 2, b]
                            moving = keys[:, c.c % 2, HU * j:HU * j + HU, b]
                        else:
                            q = qT[:, c.c % 2, b]
                            moving = keys[:, c.c % 2, b, HU * j:HU * j + HU]
                        pe.matmul(s_bank[k % 2][:, 0:HU * NK], q, moving, start=True, stop=True).then_inc(s_ps, 1)
                    if f is not None:
                        front(f, k)
                    at = lagged(c, u, k, TLAG)
                    if at is not None:
                        pair, n = at
                        pe.wait_ge(probs_done, pair.count(NU, n + 1))
                        if before(pair, n, 2) is not None:
                            bc, bk = before(pair, n, 2)
                            pe.wait_ge(probsT_done, bc.count(NU, bk + 1))
                        for h in range(HU):
                            last = pe.transpose(p_bank[n % 2][0:NK, h * P:(h + 1) * P], probs[:, n % 2, h], ident)
                        last.then_inc(probsT_ps, 1)
                    at = lagged(c, u, k, PLAG)
                    if at is not None:
                        pair, n = at
                        b, j = divmod(n, UB)
                        g = n * OG // NU
                        pe.wait_ge(probsT_done, pair.count(NU, n + 1))
                        if n % (NU // OG) == 0 and before(pair, n, 2 * NU // OG) is not None:
                            bc, bk = before(pair, n, 2 * NU // OG)
                            pe.wait_ge(o_done, bc.count(OG, bk * OG // NU + 1))
                        for h in range(HU):
                            col = ((n % (NU // OG)) * HU + h) * (D + 1)
                            last = pe.matmul(o_bank[g % 2][:, col:col + D + 1], probsT[0:NK, n % 2, h * P:(h + 1) * P],
                                             v_one[0:NK, pair.c % 2, b, HU * j + h], start=True, stop=True)
                        last.then_inc(pv_done, 1)
                    if u is not None:
                        tail(u, k)

            run_steps(pe, step, n_pairs, 3, 4)

        @block.scalar
        def _(act):
            if kind == "wide":
                for h in range(H):
                    act.wait_ge(prepared_ps, h + 1)
                    act.activation(product[:, h], f_bank[:, 0:P], ACT.Copy, scale=64.0 ** -0.5).then_inc(product_done, 1)

            def step(f, c, u):
                for k in range(NU):
                    if c is not None:
                        act.wait_ge(shifted_done, c.count(NU, k + 1))
                        if before(c, k, 2) is not None:
                            bc, bk = before(c, k, 2)
                            act.wait_ge(probsT_ps, bc.count(NU, bk + 1))
                        act.activation(probs[:, k % 2].rearrange("p h n -> p (h n)"), shifted[:, k % 2], ACT.Exp).then_inc(probs_done, 1)
                    if f is not None:
                        for m in range(FU):
                            if FRONT_AT[m] == k:
                                act.wait_ge(front_ps, f.count(FU, m + 1))
                                if m == (0 if kind == "wide" else 2) and f.back(2).real:
                                    act.wait_ge(pv_done, f.back(2).count(NU, NU))
                                front_act(act, f, m).then_inc(front_done, 1)
                    at = lagged(c, u, k, TLAG)
                    if at is not None:
                        pair, n = at
                        act.wait_ge(probsT_ps, pair.count(NU, n + 1))
                        if before(pair, n, 2) is not None:
                            bc, bk = before(pair, n, 2)
                            act.wait_ge(pv_done, bc.count(NU, bk + 1))
                        act.activation(probsT[0:NK, n % 2], p_bank[n % 2][0:NK], ACT.Copy).then_inc(probsT_done, 1)
                    if u is not None:
                        for m in range(YU - 1):
                            if TAIL_AT[m] == k:
                                act.wait_ge(tail_ps, u.count(YU, m + 1))
                                if kind == "wide":
                                    out, src = oT[:, m // 2, 4 * (m % 2):4 * (m % 2) + 4], y_bank.rearrange("p (n q) -> p n q", n=4)
                                else:
                                    out, src = oT[:, :, 0], y_bank[:, 0:2 * P].rearrange("p (n q) -> p n q", n=2)
                                act.activation(out, src, ACT.Copy).then_inc(tail_done, 1)

            run_steps(act, step, n_pairs, 3, 4)

        @block.vector
        def _(dve):
            if kind == "wide":
                dve.tensor_scalar(w["wo_scaled"], w["wo"], w["tanh_gate"], None, ALU.mult).then_inc(prepared, 1)
                dve.tensor_scalar(extra[:], w["bo"], w["tanh_gate"], None, ALU.mult).then_inc(prepared, 1)
            elif kind == "causal":
                dve.wait_ge(ready, READY)
                dve.tensor_scalar(value_row[:], value_row[:], w["bv"], None, ALU.mult).then_inc(prepared, 1)
                dve.tensor_scalar(q_bias[:], w["bq"], 8.0 ** -0.5, None, ALU.mult).then_inc(prepared, 1)
                dve.wait_ge(prepared_ps, 1)
                dve.tensor_tensor(extra[:], f_bank[:, 0:P], w["bo"], ALU.add).then_inc(prepared, 1)
            else:
                for t, name in enumerate(("q_norm", "k_norm")):
                    wn = w[name]
                    scale = 1.0 if t == 0 else 8.0 ** 0.5
                    dve.scalar_tensor_tensor(out=table[:, 0, t], in0=consts["rope"][:, 0, t], scalar=scale, in1=wn,
                                             op0=ALU.mult, op1=ALU.mult).then_inc(prepared, 1)
                    for half in range(2):
                        a, b = 4 * half, 4 * (1 - half)
                        dve.scalar_tensor_tensor(out=table[:, 1, t, a:a + 4], in0=consts["rope"][:, 1, t, a:a + 4], scalar=scale,
                                                 in1=wn[:, b:b + 4], op0=ALU.mult, op1=ALU.mult).then_inc(prepared, 1)
                dve.wait_ge(prepared, 6)

            def normalise(pair, g):
                n_heads = HU * NU // OG
                s = g % 2
                sums = o_bank[s][:, 0:OW].rearrange("p (h d) -> p h d", h=n_heads)
                dve.wait_ge(pv_done, pair.count(NU, (g + 1) * NU // OG))
                dve.reciprocal(inv_sum[:, s], sums[:, :, D]).then_inc(inv_done, 1)
                dve.wait_ge(inv_done, pair.count(OG, g + 1))
                b, first = divmod(g * n_heads, H)
                if pair.back(2).real:
                    dve.wait_ge(tail_ps, pair.back(2).count(YU, YU - 1))
                dve.tensor_tensor(o[:, pair.c % 2, b, first * D:(first + n_heads) * D].rearrange("p (h d) -> p h d", h=n_heads),
                                  sums[:, :, 0:D], inv_sum[:, s].unsqueeze(2).to_broadcast([P, n_heads, D]),
                                  ALU.mult).then_inc(o_done, 1)

            def step(f, c, u, n):
                for k in range(NU):
                    if n is not None and k in (3, 4):
                        s, b = n.c % 4, k - 3
                        dve.wait_ge(rstd_done, n.count(1, 1))
                        dve.tensor_scalar(X[:, n.index(2, b), :], z[:, s, b], mean_var[:, s, b, 0:1], rstd[:, s, b:b + 1],
                                          ALU.subtract, ALU.mult).then_inc(x_written, 1)
                    if c is not None:
                        dve.wait_ge(s_ps, c.count(NU, k + 1))
                        scores = s_bank[k % 2][:, 0:HU * NK]
                        if kind == "causal":
                            j = k % UB
                            dve.tensor_tensor(biased[:, k % 2], scores, consts["alibi"][:, HU * NK * j:HU * NK * (j + 1)],
                                              ALU.add).then_inc(biased_done, 1)
                            dve.wait_ge(biased_done, c.count(NU, k + 1))
                            scores = biased[:, k % 2]
                        scores = scores.rearrange("p (h n) -> p h n", h=HU)
                        dve.tensor_reduce(row_max[:, k % 2], scores, AX.X, ALU.max).then_inc(max_done, 1)
                        dve.wait_ge(max_done, c.count(NU, k + 1))
                        if before(c, k, 2) is not None:
                            bc, bk = before(c, k, 2)
                            dve.wait_ge(probs_done, bc.count(NU, bk + 1))
                        dve.tensor_tensor(shifted[:, k % 2].rearrange("p (h n) -> p h n", h=HU), scores,
                                          row_max[:, k % 2].unsqueeze(2).to_broadcast([P, HU, NK]),
                                          ALU.subtract).then_inc(shifted_done, 1)
                    at = lagged(c, u, k, PLAG)
                    if at is not None and (at[1] + 1) % (NU // OG) == 0:
                        normalise(at[0], at[1] * OG // NU)
                    if f is not None and kind == "wide":
                        if k == 0:
                            wait_loaded(dve, f)
                            for b in range(2):
                                dve.bn_stats(pre_stats[:, b], xin[:, f.c % 4, b]).then_inc(pre_done, 1)
                            dve.wait_ge(pre_done, f.count(4, 2))
                            if f.back(1).real:
                                dve.wait_ge(turn_done, f.back(1).count(2, 2))
                            dve.nop(nofuse=True)
                            for b in range(2):
                                dve.bn_aggr(pre_mean_var[:, b], pre_stats[:, b]).then_inc(pre_done, 1)
                        if k == 1:
                            dve.wait_ge(pre_rstd_done, f.count(1, 1))
                            if f.back(1).real:
                                dve.wait_ge(front_ps, f.back(1).count(FU, 1))
                            for b in range(2):
                                dve.tensor_scalar(xn[:, b], xin[:, f.c % 4, b], pre_mean_var[:, b, 0:1], pre_rstd[:, b:b + 1],
                                                  ALU.subtract, ALU.mult).then_inc(turn_done, 1)
                    if f is not None and kind == "rotary":
                        four = qk[:].rearrange("p b t h d -> p (b t) h d")
                        if k == 1:
                            dve.wait_ge(front_done, f.count(FU, 2))
                            dve.tensor_tensor(qk_sq[:], four, four, ALU.mult).then_inc(square_done, 1)
                            dve.wait_ge(square_done, f.count(2, 1))
                            if f.back(1).real:
                                dve.wait_ge(qk_mean_done, f.back(1).count(1, 1))
                            dve.tensor_reduce(qk_sum[:].rearrange("p (n h) -> p n h", n=4), qk_sq[:], AX.X, ALU.add).then_inc(square_done, 1)
                        if k == 2:
                            if f.back(1).real:
                                dve.wait_ge(front_ps, f.back(1).count(FU, 4))
                            def tab(which, t, a, b):
                                return table[:, which, t, a:b].unsqueeze(1).to_broadcast([P, H, b - a])

                            for part in range(4):
                                t = part % 2
                                last = dve.tensor_tensor(turned[:, part], four[:, part], tab(0, t, 0, 8), ALU.mult)
                                dve.tensor_tensor(crossed[:, part, :, 0:4], four[:, part, :, 4:8], tab(1, t, 0, 4), ALU.mult)
                                last = dve.tensor_tensor(crossed[:, part, :, 4:8], four[:, part, :, 0:4], tab(1, t, 4, 8), ALU.mult)
                            last.then_inc(turn_done, 1)
                        if k == 3:
                            dve.wait_ge(turn_done, f.count(TURNS, 1))
                            dve.tensor_tensor(crossed[:], turned[:], crossed[:], ALU.add).then_inc(turn_done, 1)
                            dve.wait_ge(turn_done, f.count(TURNS, 2))
                            dve.wait_ge(qk_rstd_done, f.count(1, 1))
                            dve.tensor_tensor(turned[:].rearrange("p n h d -> p (n h) d"), crossed[:].rearrange("p n h d -> p (n h) d"),
                                              qk_rstd[:].unsqueeze(2).to_broadcast([P, 4 * H, 8]), ALU.mult).then_inc(turn_done, 1)
                    if u is not None and k == TAIL_AT[YU - 1]:
                        s = u.c % 4
                        dve.wait_ge(tail_ps, u.count(YU, YU))
                        if kind == "rotary":
                            x_part = xin[:, s]
                        else:
                            dve.wait_ge(residual_done, u.count(1, 1))
                            x_part = residual[:, u.c % 2]
                        dve.tensor_tensor(z[:, s], y_bank[:, 0:2 * P].rearrange("p (b q) -> p b q", b=2), x_part, ALU.add).then_inc(z_done, 1)
                        dve.wait_ge(z_done, u.count(1, 1))
                        for b in range(2):
                            dve.bn_stats(stats[:, b], z[:, s, b]).then_inc(stats_done, 1)
                        dve.wait_ge(stats_done, u.count(2, 2))
                        dve.nop(nofuse=True)
                        for b in range(2):
                            dve.bn_aggr(mean_var[:, s, b], stats[:, b]).then_inc(mean_done, 1)

            run_steps(dve, step, n_pairs, 4, 4)


def mixture(chip, kind, n_seq, X, out_dram, w, consts):
    nc = chip.nc
    swiglu = kind == "swiglu"
    E = 8
    NE = E + 1 if swiglu else E
    C = 2 if swiglu else 4
    T = 4
    groups = n_seq // T
    R = 19
    with ExitStack() as ctx:
        def sb(name, shape):
            return chip.sb(ctx, kind + "_" + name, shape)

        def sem(name):
            return chip.sem(ctx, kind + "_" + name)

        power, eps = sb("power", [P, T]), sb("eps", [P, T])
        xin = sb("xin", [P, 2, T, P])
        xT = sb("xT", [P, 2, T * P])
        hidden = sb("hidden", [P, 2, C, T * P])
        gate = sb("gate", [P, 2, T, NE])
        small = {n: sb(n, [P, T, E]) for n in ("logits", "expd", "choice", "equal", "ranked", "picked", "first")}
        tops = {n: sb(n, [P, T]) for n in ("top", "key_top", "rank_top", "total", "inv_total")}
        z = sb("z", [P, 4, T, P])
        stats = sb("stats", [P, T, 6])
        mean_var = sb("mean_var", [P, 4, T, 2])
        var_eps = sb("var_eps", [P, T])
        rstd = sb("rstd", [P, 2, T])
        if swiglu:
            silu = sb("silu", [P, 2, T * P])
        else:
            gateT = sb("gateT", [E, T * P])
        h_bank = [chip.banks[:, n] for n in range(4)]
        y_bank = [chip.banks[:, 4], chip.banks[:, 5]]
        x_bank, r_bank = chip.banks[:, 6], chip.banks[:, 7]

        x_loaded = [sem(f"x_loaded{n}") for n in range(2)]
        ready, xT_ps, xT_done, logits_ps, routed, exp_done, gateT_ps, gateT_done, base_ps, base_done = (
            sem(n) for n in ("ready", "xT_ps", "xT_done", "logits_ps", "routed", "exp_done", "gateT_ps", "gateT_done",
                             "base_ps", "base_done"))
        h_ps, silu_done, h_done, y_ps, summed = (sem(n) for n in ("h_ps", "silu_done", "h_done", "y_ps", "summed"))
        stats_done, mean_done, var_done, rstd_done, x_written, stored = (
            sem(n) for n in ("stats_done", "mean_done", "var_done", "rstd_done", "x_written", "stored"))
        block = ctx.enter_context(nc.Block())
        ident = consts["ident"]

        def lagged(c, u, e):
            if e >= 1:
                return (c, e - 1) if c is not None else None
            return (u, NE - 1) if u is not None else None

        def before(g, e, n):
            if e >= n:
                return (g, e - n)
            return (g.back(1), e - n + NE) if g.back(1).real else None

        @block.sync
        def _(sp):
            def step(f, c, u, n):
                if f is not None:
                    s = f.c % 2
                    if f.back(2).real:
                        sp.wait_ge(mean_done, f.back(2).count(T, T))
                    sp.dma_start(xin[:, s], X[:, bass.ds(f.index(T), T), :]).then_inc(x_loaded[s], 16)
                if n is not None and out_dram is not None:
                    sp.wait_ge(x_written, n.count(T, T))
                    sp.dma_start(out_dram[bass.ds(n.index(T), T)].rearrange("b t d -> t b d"),
                                 X[:, bass.ds(n.index(T), T), :]).then_inc(stored, 16)

            run_steps(sp, step, groups, 4, 4)
            if out_dram is not None:
                sp.wait_ge(stored, 16 * groups)

        @block.gpsimd
        def _(pool):
            pool.memset(power[:], -0.5).then_inc(ready, 1)
            pool.memset(gate[:], 1.0).then_inc(ready, 1)
            pool.memset(eps[:], LN_EPS).then_inc(ready, 1)
            pool.wait_ge(ready, 3)

            def step(f, c, u):
                if u is not None:
                    s = u.c % 4
                    pool.wait_ge(mean_done, u.count(T, T))
                    if u.back(1).real:
                        pool.wait_ge(rstd_done, u.back(1).count(1, 1))
                    pool.tensor_tensor(var_eps[:], mean_var[:, s, :, 1], eps[:], ALU.add).then_inc(var_done, 1)
                    pool.wait_ge(var_done, u.count(1, 1))
                    if u.back(2).real:
                        pool.wait_ge(x_written, u.back(2).count(T, T))
                    pool.tensor_tensor(rstd[:, u.c % 2], var_eps[:], power[:], ALU.pow).then_inc(rstd_done, 1)

            run_steps(pool, step, groups, 3, 4)

        @block.scalar
        def _(act):
            def step(f, c, u):
                for e in range(NE):
                    if c is not None:
                        par = (c.c * NE + e) % 2
                        if before(c, e, 2) is not None:
                            g, be = before(c, e, 2)
                            act.wait_ge(y_ps, g.count(NE, be + 1))
                        for m in range(C):
                            act.wait_ge(h_ps, c.count(NE * C, e * C + m + 1))
                            if swiglu:
                                if e >= 1 or c.back(1).real:
                                    act.wait_ge(h_done, c.count(NE * C, (e - 1) * C + m + 1))
                                act.activation(silu[:, m], h_bank[2 * m], ACT.Silu).then_inc(silu_done, 1)
                            else:
                                act.activation(hidden[:, par, m], h_bank[m], ACT.Gelu, bias=w["b1"][:, e, m:m + 1]).then_inc(h_done, 1)
                    if f is not None:
                        if e == 1:
                            act.wait_ge(xT_ps, f.count(1, 1))
                            if f.back(2).real:
                                act.wait_ge(h_ps, f.back(2).count(NE * C, NE * C))
                            act.activation(xT[:, f.c % 2], x_bank, ACT.Copy).then_inc(xT_done, 1)
                        if e == 3:
                            act.wait_ge(routed, f.count(R, 2))
                            act.activation(small["expd"][:], small["logits"][:], ACT.Exp).then_inc(exp_done, 1)
                        if e == 6 and not swiglu:
                            act.wait_ge(gateT_ps, f.count(1, 1))
                            act.activation(gateT[:], r_bank[0:E], ACT.Copy).then_inc(gateT_done, 1)

            run_steps(act, step, groups, 3, 4)

        @block.vector
        def _(dve):
            dve.wait_ge(ready, 3)

            def route(f):
                n = [0]

                def link(ins):
                    n[0] += 1
                    ins.then_inc(routed, 1)
                    dve.wait_ge(routed, f.count(R, n[0]))

                def over(t):
                    return t[:].unsqueeze(2).to_broadcast([P, T, E])

                def row(t):
                    return t.unsqueeze(1).to_broadcast([P, T, E])

                logits, expd, choice, equal, ranked, picked, first = (
                    small[n][:] for n in ("logits", "expd", "choice", "equal", "ranked", "picked", "first"))
                top, key_top, rank_top, total, inv_total = (tops[n] for n in ("top", "key_top", "rank_top", "total", "inv_total"))
                dve.wait_ge(logits_ps, f.count(1, 1))
                ps = r_bank[:, 0:T * E].rearrange("p (t e) -> p t e", t=T)
                link(dve.tensor_reduce(top[:], ps, AX.X, ALU.max))
                link(dve.tensor_tensor(logits, ps, over(top), ALU.subtract))
                dve.wait_ge(exp_done, f.count(1, 1))
                if swiglu:
                    link(dve.tensor_reduce(total[:], expd, AX.X, ALU.add))
                    link(dve.reciprocal(inv_total[:], total[:]))
                    link(dve.tensor_tensor(expd, expd, over(inv_total), ALU.mult))
                    link(dve.tensor_tensor(choice, expd, row(w["gate_bias"]), ALU.add))
                else:
                    link(dve.tensor_copy(choice, expd))
                for turn in range(2):
                    link(dve.tensor_reduce(key_top[:], choice, AX.X, ALU.max))
                    link(dve.tensor_tensor(equal, choice, over(key_top), ALU.is_equal))
                    link(dve.tensor_tensor(ranked, equal, row(consts["rank8"]), ALU.mult))
                    link(dve.tensor_reduce(rank_top[:], ranked, AX.X, ALU.max))
                    link(dve.tensor_tensor(first if turn == 0 else picked, ranked, over(rank_top), ALU.is_equal))
                    if turn == 0:
                        link(dve.scalar_tensor_tensor(out=choice.rearrange("p t e -> p (t e)"), in0=first.rearrange("p t e -> p (t e)"),
                                                      scalar=-1e30, in1=choice.rearrange("p t e -> p (t e)"), op0=ALU.mult, op1=ALU.add))
                if swiglu:
                    link(dve.tensor_tensor(picked, picked, first, ALU.add))
                else:
                    link(dve.tensor_tensor(picked, picked, first, ALU.add))
                    dve_gate(f, picked, expd, link, over, total, inv_total)
                    assert n[0] == R, n
                    return
                out = gate[:, f.c % 2, :, 0:E]
                if f.back(2).real:
                    dve.wait_ge(summed, f.back(2).count(NE * T, NE * T))
                link(dve.tensor_tensor(out, picked, expd, ALU.mult))
                assert n[0] == R, n

            def dve_gate(f, picked, expd, link, over, total, inv_total):
                link(dve.tensor_tensor(picked, picked, expd, ALU.mult))
                link(dve.tensor_reduce(total[:], picked, AX.X, ALU.add))
                link(dve.reciprocal(inv_total[:], total[:]))
                link(dve.tensor_tensor(gate[:, f.c % 2, :, 0:E], picked, over(inv_total), ALU.mult))

            def step(f, c, u, n):
                for e in range(NE):
                    if c is not None and swiglu:
                        par = (c.c * NE + e) % 2
                        for m in range(C):
                            dve.wait_ge(silu_done, c.count(NE * C, e * C + m + 1))
                            dve.tensor_tensor(hidden[:, par, m], silu[:, m], h_bank[2 * m + 1], ALU.mult).then_inc(h_done, 1)
                    at = lagged(c, u, e)
                    if at is not None:
                        g, n_exp = at
                        dve.wait_ge(y_ps, g.count(NE, n_exp + 1))
                        if n_exp >= 1:
                            dve.wait_ge(summed, g.count(NE * T, n_exp * T))
                        elif not swiglu:
                            dve.wait_ge(base_done, g.count(1, 1))
                        for t in range(T):
                            rest = z[:, g.c % 4, t] if n_exp >= 1 or not swiglu else xin[:, g.c % 2, t]
                            dve.scalar_tensor_tensor(out=z[:, g.c % 4, t], in0=y_bank[(g.c * NE + n_exp) % 2][:, t * P:(t + 1) * P],
                                                     scalar=gate[:, g.c % 2, t, n_exp:n_exp + 1], in1=rest,
                                                     op0=ALU.mult, op1=ALU.add).then_inc(summed, 1)
                    if u is not None and e == 0:
                        s = u.c % 4
                        dve.wait_ge(summed, u.count(NE * T, NE * T))
                        for t in range(T):
                            dve.bn_stats(stats[:, t], z[:, s, t]).then_inc(stats_done, 1)
                        dve.wait_ge(stats_done, u.count(T, T))
                        dve.nop(nofuse=True)
                        for t in range(T):
                            dve.bn_aggr(mean_var[:, s, t], stats[:, t]).then_inc(mean_done, 1)
                    if n is not None and e == 1:
                        s = n.c % 4
                        dve.wait_ge(rstd_done, n.count(1, 1))
                        for t in range(T):
                            dve.tensor_scalar(X[:, n.index(T, t), :], z[:, s, t], mean_var[:, s, t, 0:1],
                                              rstd[:, n.c % 2, t:t + 1], ALU.subtract, ALU.mult).then_inc(x_written, 1)
                    if f is not None and e == 3:
                        route(f)
                    if f is not None and e == 7 and not swiglu:
                        dve.wait_ge(base_ps, f.count(1, 1))
                        dve.tensor_tensor(z[:, f.c % 4], r_bank.rearrange("p (t d) -> p t d", t=T), xin[:, f.c % 2], ALU.add).then_inc(base_done, 1)

            run_steps(dve, step, groups, 4, 4)

        @block.tensor
        def _(pe):
            def step(f, c, u):
                for e in range(NE):
                    if c is not None:
                        if e == 0:
                            pe.wait_ge(xT_done, c.count(1, 1))
                        for m in range(C):
                            if e >= 1 or c.back(1).real:
                                pe.wait_ge(h_done, c.count(NE * C, (e - 1) * C + m + 1))
                            cols = slice(e * C * P + m * P, e * C * P + (m + 1) * P)
                            last = pe.matmul(h_bank[2 * m if swiglu else m], w["w1"][:, cols], xT[:, c.c % 2], start=True, stop=True)
                            if swiglu:
                                last = pe.matmul(h_bank[2 * m + 1], w["w3"][:, cols], xT[:, c.c % 2], start=True, stop=True)
                            last.then_inc(h_ps, 1)
                    at = lagged(c, u, e)
                    if at is not None:
                        g, n_exp = at
                        par = (g.c * NE + n_exp) % 2
                        if before(g, n_exp, 2) is not None:
                            bg, be = before(g, n_exp, 2)
                            pe.wait_ge(summed, bg.count(NE * T, (be + 1) * T))
                        for t in range(T):
                            for m in range(C):
                                if t == 0:
                                    pe.wait_ge(h_done, g.count(NE * C, n_exp * C + m + 1))
                                last = pe.matmul(y_bank[par][:, t * P:(t + 1) * P], hidden[:, par, m, t * P:(t + 1) * P],
                                                 w["w2"][:, n_exp, m], start=m == 0, stop=m == C - 1)
                        last.then_inc(y_ps, 1)
                    if f is not None and e == 0:
                        pe.wait_ge(x_loaded[f.c % 2], f.load(2))
                        if f.back(1).real:
                            pe.wait_ge(xT_done, f.back(1).count(1, 1))
                        for t in range(T):
                            last = pe.transpose(x_bank[:, t * P:(t + 1) * P], xin[:, f.c % 2, t], ident)
                        last.then_inc(xT_ps, 1)
                    if f is not None and e == 2:
                        pe.wait_ge(xT_done, f.count(1, 1))
                        if f.back(1).real:
                            if swiglu:
                                pe.wait_ge(routed, f.back(1).count(R, 2))
                            else:
                                pe.wait_ge(base_done, f.back(1).count(1, 1))
                        for t in range(T):
                            last = pe.matmul(r_bank[:, t * E:(t + 1) * E], xT[:, f.c % 2, t * P:(t + 1) * P], w["router"],
                                             start=True, stop=True)
                        last.then_inc(logits_ps, 1)
                    if f is not None and not swiglu:
                        if e == 6:
                            pe.wait_ge(routed, f.count(R, R))
                            for t in range(T):
                                last = pe.transpose(r_bank[0:E, t * P:(t + 1) * P], gate[:, f.c % 2, t, 0:E], ident)
                            last.then_inc(gateT_ps, 1)
                        if e == 7:
                            pe.wait_ge(gateT_done, f.count(1, 1))
                            for t in range(T):
                                last = pe.matmul(r_bank[:, t * P:(t + 1) * P], gateT[:, t * P:(t + 1) * P], w["b2"],
                                                 start=True, stop=True)
                            last.then_inc(base_ps, 1)

            run_steps(pe, step, groups, 3, 4)


SMALL = {
    "ident": [P, P], "heads8": [P, 8], "heads16": [P, 16], "rank8": [P, 8], "rope": [P, 2, 2, 8],
    "ta_gamma": [P, 1], "ta_wq": [P, P], "ta_wk": [P, P], "ta_wv": [P, P], "ta_wo": [P, P],
    "cx_gamma": [P, 1], "cx_beta": [P, 1], "cx_gate": [P, 1], "cx_bo": [P, P],
    "g_router": [P, 8], "g_b1": [P, 8, 4], "g_b2": [8, P],
    "sa_wq": [P, P], "sa_wk": [P, P], "sa_wv": [P, P], "sa_wo": [P, P], "sa_bq": [P, 1], "sa_bk": [P, 1], "sa_bv": [P, 1], "sa_bo": [P, P],
    "ra_wq": [P, P], "ra_wk": [P, P], "ra_wv": [P, P], "ra_wo": [P, P], "ra_qn": [P, 8], "ra_kn": [P, 8],
    "s_router": [P, 8], "s_bias": [P, 8],
}
LARGE = {
    "cx_wqT": [64, 16, P], "cx_wkT": [64, 16, P], "cx_wv": [P, 1024], "cx_wo": [P, 8, P],
    "g_w1": [P, 8 * 512], "g_w2": [P, 8, 4, P],
    "alibi": [P, 16 * P],
    "s_w1": [P, 9 * 256], "s_w3": [P, 9 * 256], "s_w2": [P, 9, 2, P],
}


def build(nc, n_seq, x_dram, ctxT_dram, weights_dram, out_dram, blocks=(1, 2, 3, 4, 5, 6), x_state=None):
    with ExitStack() as ctx:
        chip = Chip(nc, ctx)
        X = chip.sb(ctx, "X", [P, n_seq, P])
        small = {n: chip.sb(ctx, n, s) for n, s in SMALL.items()}
        tanh_gate = chip.sb(ctx, "tanh_gate", [P, 1])
        region_a = chip.sb(ctx, "region_a", [P, 8 * 512 * 2])
        region_b = chip.sb(ctx, "region_b", [P, 2048 * 2 + 1024 * 3])
        sems = {n: ctx.enter_context(nc.semaphore("loaded_" + n)) for n in ("first", "small", "cx", "gelu", "alibi", "swiglu")}

        def cut(region, at, shape):
            n = 1
            for k in shape[1:]:
                n *= k
            v = region[0:shape[0], at:at + n]
            if len(shape) == 3:
                v = v.rearrange("p (a b) -> p a b", a=shape[1])
            if len(shape) == 4:
                v = v.rearrange("p (a b c) -> p a b c", a=shape[1], b=shape[2])
            return v

        large, at = {}, {"a": 0, "b": 0}
        for names, region, key in ((("cx_wqT", "cx_wkT", "cx_wv", "cx_wo"), region_b, "b"), (("g_w1", "g_w2"), region_a, "a")):
            for n in names:
                large[n] = cut(region, at[key], LARGE[n])
                at[key] += _free(LARGE[n])
        wo_scaled = cut(region_b, at["b"], [P, 8, P])
        large["alibi"] = cut(region_b, 0, LARGE["alibi"])
        a = 0
        for n in ("s_w1", "s_w3", "s_w2"):
            large[n] = cut(region_a, a, LARGE[n])
            a += _free(LARGE[n])

        first = ["ident", "heads8", "ta_gamma", "ta_wq", "ta_wk", "ta_wv", "ta_wo"]
        rest = [n for n in SMALL if n not in first]

        def load_block(queue, names, sem, wait=True):
            with nc.Block() as block:
                @block.scalar
                def _(act):
                    for names_, sem_ in queue:
                        for n in names_:
                            dst = small[n] if n in small else None
                            act.dma_start(dst[:] if dst is not None else large[n], weights_dram[n]).then_inc(sem_, 16)
                    if wait:
                        act.wait_ge(sem, 16 * len(names))

        load_block([(first, sems["first"]), (rest, sems["small"]),
                    (["cx_wqT", "cx_wkT", "cx_wv", "cx_wo"], sems["cx"]), (["g_w1", "g_w2"], sems["gelu"])], first, sems["first"])
        if x_state is not None:
            with nc.semaphore("x_state_loaded") as loaded, nc.Block() as block:
                @block.sync
                def _(sp):
                    sp.dma_start(X[:], x_state.rearrange("b t d -> t b d")).then_inc(loaded, 16)
                    sp.wait_ge(loaded, 16)
        consts = {n: small[n][:] for n in ("ident", "heads8", "heads16", "rank8", "rope")}
        consts["alibi"] = large["alibi"]
        if 1 in blocks:
            taylor_attention(chip, n_seq, x_dram, X, {"gamma": small["ta_gamma"][:], "wq": small["ta_wq"][:], "wk": small["ta_wk"][:],
                                                      "wv": small["ta_wv"][:], "wo": small["ta_wo"][:]}, consts)
            chip.clear_semaphores()
        with nc.Block() as block:
            @block.scalar
            def _(act):
                act.wait_ge(sems["small"], 16 * len(rest))
                act.wait_ge(sems["cx"], 16 * 4)
                act.activation(tanh_gate[:], small["cx_gate"][:], ACT.Tanh)
        if 2 in blocks:
            softmax_attention(chip, "wide", n_seq, X, ctxT_dram, {
                "wqT": large["cx_wqT"], "wkT": large["cx_wkT"], "wv": large["cx_wv"], "wo": large["cx_wo"], "wo_scaled": wo_scaled,
                "gamma": small["cx_gamma"][:], "beta": small["cx_beta"][:], "tanh_gate": tanh_gate[:], "bo": small["cx_bo"][:]}, consts)
            chip.clear_semaphores()
        load_block([(["alibi"], sems["alibi"])], ["g_w1", "g_w2"], sems["gelu"])
        if 3 in blocks:
            mixture(chip, "gelu", n_seq, X, out_dram if blocks[-1] == 3 else None, {
                "w1": large["g_w1"], "w2": large["g_w2"], "b1": small["g_b1"][:], "b2": small["g_b2"][:], "router": small["g_router"][:]}, consts)
            chip.clear_semaphores()
        load_block([(["s_w1", "s_w3", "s_w2"], sems["swiglu"])], ["alibi"], sems["alibi"])
        if 4 in blocks:
            softmax_attention(chip, "causal", n_seq, X, None, {
                "wq": small["sa_wq"][:], "wk": small["sa_wk"][:], "wv": small["sa_wv"][:], "wo": small["sa_wo"][:],
                "bq": small["sa_bq"][:], "bk": small["sa_bk"][:], "bv": small["sa_bv"][:], "bo": small["sa_bo"][:]}, consts)
            chip.clear_semaphores()
        if 5 in blocks:
            softmax_attention(chip, "rotary", n_seq, X, ctxT_dram, {
                "wq": small["ra_wq"][:], "wk": small["ra_wk"][:], "wv": small["ra_wv"][:], "wo": small["ra_wo"][:],
                "q_norm": small["ra_qn"][:], "k_norm": small["ra_kn"][:]}, consts)
            chip.clear_semaphores()
        with nc.Block() as block:
            @block.scalar
            def _(act):
                act.wait_ge(sems["swiglu"], 16 * 3)
        if 6 in blocks:
            mixture(chip, "swiglu", n_seq, X, out_dram, {
                "w1": large["s_w1"], "w3": large["s_w3"], "w2": large["s_w2"], "router": small["s_router"][:],
                "gate_bias": small["s_bias"][:]}, consts)
        if blocks[-1] not in (3, 6):
            with nc.semaphore("x_stored") as stored, nc.Block() as block:
                @block.sync
                def _(sp):
                    sp.dma_start(out_dram.rearrange("b t d -> t b d"), X[:]).then_inc(stored, 16)
                    sp.wait_ge(stored, 16)


def _free(shape):
    n = 1
    for k in shape[1:]:
        n *= k
    return n


def layouts(inputs, np):
    g = {k: np.asarray(v) for k, v in inputs.items()}

    def down(v):
        return v.reshape(-1, 1)

    def rows(v):
        return np.broadcast_to(v.reshape(1, -1), (P, v.size))

    def hidden_major(w1):
        return w1.transpose(2, 0, 1).reshape(P, -1)

    def chunks(w2):
        e, d, h = w2.shape
        return w2.transpose(0, 2, 1).reshape(e, h // P, P, d).transpose(2, 0, 1, 3)

    q = np.arange(P)
    slopes = np.power(np.float32(2.0), np.float32(-8.0) * np.arange(1, 17, dtype=np.float32) / np.float32(16))
    rel = np.abs(q[:, None] - q[None, :]).astype(np.float32)
    alibi = np.where((q[:, None] >= q[None, :])[:, None, :], -slopes[None, :, None] * rel[:, None, :], np.float32(-1e30))
    rope = np.zeros((P, 2, 2, 8), np.float32)
    for t, theta in enumerate((32.0, 1000.0)):
        freqs = np.power(np.float32(theta), -np.arange(0, 8, 2, dtype=np.float32) / np.float32(8))
        angle = np.arange(P, dtype=np.float32)[:, None] * freqs[None, :]
        rope[:, 0, t] = np.concatenate([np.cos(angle), np.cos(angle)], -1)
        rope[:, 1, t] = np.concatenate([-np.sin(angle), np.sin(angle)], -1)
    w_kv, x_kv = g["L0_attn_w_kv"], g["L0_xattn_w_kv"]
    return {
        "ident": np.eye(P, dtype=np.float32),
        "heads8": (q[:, None] // 16 == np.arange(8)[None, :]).astype(np.float32),
        "heads16": (q[:, None] // 8 == np.arange(16)[None, :]).astype(np.float32),
        "rank8": np.broadcast_to(np.arange(8, 0, -1).astype(np.float32)[None, :], (P, 8)),
        "rope": rope,
        "alibi": alibi.reshape(P, -1).astype(np.float32),
        "ta_gamma": down(g["L0_attn_gamma"]), "ta_wq": g["L0_attn_w_q"], "ta_wk": w_kv[:, :P], "ta_wv": w_kv[:, P:],
        "ta_wo": g["L0_attn_w_out"],
        "cx_gamma": down(g["L0_xattn_ln_gamma"]), "cx_beta": down(g["L0_xattn_ln_beta"]),
        "cx_gate": rows(g["L0_xattn_gate"]), "cx_bo": rows(g["L0_xattn_b_out"]),
        "cx_wqT": g["L0_xattn_w_q"].T.reshape(16, 64, P).transpose(1, 0, 2),
        "cx_wkT": x_kv[:, :1024].T.reshape(16, 64, P).transpose(1, 0, 2),
        "cx_wv": x_kv[:, 1024:], "cx_wo": g["L0_xattn_w_out"].reshape(8, P, P).transpose(1, 0, 2),
        "g_router": g["L0_ffn_Wr"].T, "g_w1": hidden_major(g["L0_ffn_W1"]), "g_w2": chunks(g["L0_ffn_W2"]),
        "g_b1": g["L0_ffn_b1"].reshape(8, 4, P).transpose(2, 0, 1), "g_b2": g["L0_ffn_b2"],
        "sa_wq": g["L1_attn_Wq"].T, "sa_wk": g["L1_attn_Wk"].T, "sa_wv": g["L1_attn_Wv"].T, "sa_wo": g["L1_attn_Wo"].T,
        "sa_bq": down(g["L1_attn_bq"]), "sa_bk": down(g["L1_attn_bk"]), "sa_bv": down(g["L1_attn_bv"]), "sa_bo": rows(g["L1_attn_bo"]),
        "ra_wq": g["L1_xattn_Wq"].T, "ra_wk": g["L1_xattn_Wk"].T, "ra_wv": g["L1_xattn_Wv"].T, "ra_wo": g["L1_xattn_Wo"].T,
        "ra_qn": rows(g["L1_xattn_q_norm_w"]), "ra_kn": rows(g["L1_xattn_k_norm_w"]),
        "s_router": g["L1_ffn_gate_w"].T, "s_bias": rows(g["L1_ffn_gate_bias"]),
        "s_w1": hidden_major(np.concatenate([g["L1_ffn_w1"], g["L1_ffn_sw1"][None]])),
        "s_w3": hidden_major(np.concatenate([g["L1_ffn_w3"], g["L1_ffn_sw3"][None]])),
        "s_w2": chunks(np.concatenate([g["L1_ffn_w2"], g["L1_ffn_sw2"][None]])),
    }


def kernel(**inputs):
    import numpy as np
    import concourse.bacc as bacc
    from concourse.bass_utils import run_bass_kernel_spmd

    nc = bacc.Bacc("TRN2", target_bir_lowering=False, num_devices=1)
    arrays = {n: np.ascontiguousarray(a) for n, a in layouts(inputs, np).items()}
    arrays["x"] = np.ascontiguousarray(inputs["x"])
    arrays["ctxT"] = np.ascontiguousarray(np.asarray(inputs["ctx_1024"]).transpose(2, 0, 1))
    arrays = {"in_" + n: a for n, a in arrays.items()}
    dram = {n: nc.dram_tensor(n, list(a.shape), F32, kind="ExternalInput").ap() for n, a in arrays.items()}
    n_seq = arrays["in_x"].shape[0]
    out = nc.dram_tensor("out", [n_seq, P, P], F32, kind="ExternalOutput").ap()
    build(nc, n_seq, dram["in_x"], dram["in_ctxT"], {n[3:]: a for n, a in dram.items()}, out)
    result = run_bass_kernel_spmd(nc, [arrays], core_ids=[0])
    return result.results[0]["out"]
```

```python
from contextlib import ExitStack

import concourse.bass as bass
from concourse import mybir

P = 128
F32 = mybir.dt.float32
ALU = mybir.AluOpType
ACT = mybir.ActivationFunctionType
AX = mybir.AxisListType
PEEL = 4
LN_EPS = 1e-5
F32R = mybir.dt.float32r
I32 = mybir.dt.int32
HIGH = -4096
NEWTON = 3
SEED_SCALE = 1.8352578e-20


class At:

    def __init__(self, c, i=None, unroll=4):
        self.c, self.i, self.unroll = c, i, unroll

    def back(self, n):
        return At(self.c - n, self.i, self.unroll)

    @property
    def real(self):
        return self.c >= 0 if self.i is None else self.c + PEEL >= 0

    def count(self, per, k):
        assert self.real
        v = self.c * per + k
        return v if self.i is None else self.i * (self.unroll * per) + v

    def load(self, slots):
        v = 16 * (self.c // slots + 1)
        return v if self.i is None else self.i * (16 * self.unroll // slots) + v

    def index(self, scale=1, plus=0):
        v = self.c * scale + plus
        return v if self.i is None else self.i * (self.unroll * scale) + v


def run_steps(engine, step, units, stages, unroll):
    for t in range(PEEL):
        step(*[At(t - s, None, unroll) if 0 <= t - s < units else None for s in range(stages)])
    with engine.Fori(PEEL // unroll, units // unroll) as i:
        for t in range(unroll):
            step(*[At(t - s, i, unroll) for s in range(stages)])
    for t in range(units, units + stages - 1):
        step(*[At(t - s, None, unroll) if 0 <= t - s < units else None for s in range(stages)])


class Chip:

    def __init__(self, nc, ctx):
        self.nc, self.used = nc, []
        self.banks = ctx.enter_context(nc.psum_tensor("banks", [P, 8, 512], F32))

    def sb(self, ctx, name, shape, dt=F32):
        return ctx.enter_context(self.nc.sbuf_tensor(name, shape, dt))

    def sem(self, ctx, name):
        self.used.append(ctx.enter_context(self.nc.semaphore(name)))
        return self.used[-1]

    def clear_semaphores(self):
        used, self.used = self.used, []
        with self.nc.Block() as block:
            @block.gpsimd
            def _(pool):
                for s in used:
                    pool.sem_clear(s)


def load_x(sp, source, xin, loaded, freed, unit, slots, per, width):
    if unit.back(slots).real:
        sp.wait_ge(freed, unit.back(slots).count(1, 1))
    s = unit.c % slots
    sp.dma_start(xin[:, s], source(unit, width)).then_inc(loaded[s], 16)


def taylor_attention(chip, n_seq, x_dram, X, w, consts):
    nc = chip.nc
    H, D = 8, 16
    with ExitStack() as ctx:
        def sb(name, shape):
            return chip.sb(ctx, "taylor_" + name, shape)

        def sem(name):
            return chip.sem(ctx, "taylor_" + name)

        wq, wk, wv = (sb(n, [P, P]) for n in ("wq", "wk", "wv"))
        ones = sb("ones", [P, P])
        power, eps = sb("power", [P, 1]), sb("eps", [P, 1])
        xin = sb("xin", [P, 4, P])
        squares = sb("squares", [P, P])
        sumsq = sb("sumsq", [P, 4])
        guarded = sb("guarded", [P, 4])
        inv_norm = sb("inv_norm", [P, 4])
        xs = sb("xs", [P, 2, P])
        xsT = sb("xsT", [P, 2, P])
        q_masked = sb("q_masked", [P, 2, H, P])
        kT = sb("kT", [P, 2, P])
        v_one = sb("v_one", [P, 2, H, D + 1])
        weights = sb("weights", [P, 2, 4, P])
        den = sb("den", [P, 2, H])
        inv_den = sb("inv_den", [P, 2, H])
        o = sb("o", [P, 2, P])
        oT = sb("oT", [P, 2, P])
        z = sb("z", [P, 4, P])
        stats = sb("stats", [P, 6])
        mean_var = sb("mean_var", [P, 4, 2])
        var_eps = sb("var_eps", [P, 4])
        rstd = sb("rstd", [P, 4])
        xsT_bank, q_bank, kv_bank, o_bank, oT_bank, y_bank = (chip.banks[:, n] for n in (0, 1, 2, 5, 6, 7))
        s_bank = [chip.banks[:, 3], chip.banks[:, 4]]

        x_loaded = [sem(f"x_loaded{n}") for n in range(4)]
        power_ready, ready = sem("power_ready"), sem("ready")
        sumsq_done, guarded_done, inv_norm_done, xs_done, xsT_ps, xsT_done = (
            sem(n) for n in ("sumsq_done", "guarded_done", "inv_norm_done", "xs_done", "xsT_ps", "xsT_done"))
        q_ps, kv_ps, q_done, k_done, v_done, s_ps, weights_done = (
            sem(n) for n in ("q_ps", "kv_ps", "q_done", "k_done", "v_done", "s_ps", "weights_done"))
        o_ps, den_done, inv_den_done, o_done, oT_ps, oT_done, y_ps = (
            sem(n) for n in ("o_ps", "den_done", "inv_den_done", "o_done", "oT_ps", "oT_done", "y_ps"))
        z_done, stats_done, mean_done, var_done, rstd_done, x_written = (
            sem(n) for n in ("z_done", "stats_done", "mean_done", "var_done", "rstd_done", "x_written"))
        block = ctx.enter_context(nc.Block())

        @block.sync
        def _(sp):
            def step(f):
                if f is not None:
                    load_x(sp, lambda u, n: x_dram[u.index()], xin, x_loaded, z_done, f, 4, 1, P)

            run_steps(sp, step, n_seq, 1, 4)

        @block.gpsimd
        def _(pool):
            pool.memset(power[:], -0.5).then_inc(power_ready, 1)
            pool.memset(eps[:], LN_EPS).then_inc(power_ready, 1)
            pool.wait_ge(power_ready, 2)

            def step(a, f, c, u, n):
                if a is not None:
                    s = a.c % 4
                    pool.wait_ge(sumsq_done, a.count(1, 1))
                    pool.nop(nofuse=True)
                    pool.tensor_scalar(guarded[:, s:s + 1], sumsq[:, s:s + 1], 1e-24, None, ALU.max).then_inc(guarded_done, 1)
                    pool.wait_ge(guarded_done, a.count(1, 1))
                    pool.tensor_tensor(inv_norm[:, s:s + 1], guarded[:, s:s + 1], power[:], ALU.pow).then_inc(inv_norm_done, 1)
                if u is not None:
                    s = u.c % 4
                    pool.wait_ge(mean_done, u.count(1, 1))
                    pool.tensor_tensor(var_eps[:, s:s + 1], mean_var[:, s, 1:2], eps[:], ALU.add).then_inc(var_done, 1)
                    pool.wait_ge(var_done, u.count(1, 1))
                    pool.tensor_tensor(rstd[:, s:s + 1], var_eps[:, s:s + 1], power[:], ALU.pow).then_inc(rstd_done, 1)

            run_steps(pool, step, n_seq, 5, 4)

        @block.scalar
        def _(act):
            def step(a, f, c, u):
                if c is not None:
                    for j in range(2):
                        act.wait_ge(s_ps, c.count(2, j + 1))
                        act.activation(weights[:, j], s_bank[j].rearrange("p (h q) -> p h q", h=4), ACT.Square,
                                       bias=1.0, scale=0.25).then_inc(weights_done, 1)
                if u is not None:
                    act.wait_ge(oT_ps, u.count(1, 1))
                    act.activation(oT[:, u.c % 2], oT_bank[:, 0:P], ACT.Copy).then_inc(oT_done, 1)
                if f is not None:
                    s = f.c % 2
                    act.wait_ge(xsT_ps, f.count(1, 1))
                    act.activation(xsT[:, s], xsT_bank[:, 0:P], ACT.Copy).then_inc(xsT_done, 1)
                    act.wait_ge(kv_ps, f.count(1, 1))
                    act.activation(kT[:, s], kv_bank[:, 0:P], ACT.Copy).then_inc(k_done, 1)
                    act.activation(v_one[:, s, :, 0:D], kv_bank[:, P:2 * P].rearrange("p (h d) -> p h d", h=H),
                                   ACT.Copy).then_inc(v_done, 1)
                if a is not None:
                    s = a.c % 4
                    act.wait_ge(x_loaded[s], a.load(4))
                    if a.back(4).real:
                        act.wait_ge(inv_norm_done, a.back(4).count(1, 1))
                    act.activation(squares[:], xin[:, s], ACT.Square, accum_out=sumsq[:, s:s + 1]).then_inc(sumsq_done, 1)

            run_steps(act, step, n_seq, 4, 4)

        @block.vector
        def _(dve):
            for t, name in ((wq, "wq"), (wk, "wk"), (wv, "wv")):
                dve.tensor_scalar(t[:], w[name], w["gamma"], float(P) ** 0.5, ALU.mult, ALU.mult).then_inc(ready, 1)
            dve.memset(ones[:], 1.0).then_inc(ready, 1)
            dve.memset(v_one[:], 1.0).then_inc(ready, 1)

            def step(a, f, c, u, n):
                if n is not None:
                    s = n.c % 4
                    dve.wait_ge(rstd_done, n.count(1, 1))
                    dve.tensor_scalar(X[:, n.index(), :], z[:, s], mean_var[:, s, 0:1], rstd[:, s:s + 1],
                                      ALU.subtract, ALU.mult).then_inc(x_written, 1)
                if u is not None:
                    s = u.c % 2
                    sums = o_bank[:, 0:H * (D + 1)].rearrange("p (h d) -> p h d", h=H)
                    dve.wait_ge(o_ps, u.count(1, 1))
                    dve.tensor_scalar(den[:, s], sums[:, :, D], 2e-5, None, ALU.max).then_inc(den_done, 1)
                    dve.wait_ge(den_done, u.count(1, 1))
                    dve.reciprocal(inv_den[:, s], den[:, s]).then_inc(inv_den_done, 1)
                    dve.wait_ge(inv_den_done, u.count(1, 1))
                    dve.tensor_tensor(o[:, s].rearrange("p (h d) -> p h d", h=H), sums[:, :, 0:D],
                                      inv_den[:, s].unsqueeze(2).to_broadcast([P, H, D]), ALU.mult).then_inc(o_done, 1)
                if f is not None:
                    s = f.c % 2
                    dve.wait_ge(inv_norm_done, f.count(1, 1))
                    dve.tensor_scalar(xs[:, s], xin[:, f.c % 4], inv_norm[:, f.c % 4:f.c % 4 + 1], None,
                                      ALU.mult).then_inc(xs_done, 1)
                    dve.wait_ge(q_ps, f.count(1, 1))
                    if f.back(2).real:
                        dve.wait_ge(s_ps, f.back(2).count(2, 2))
                    dve.tensor_tensor(q_masked[:, s], q_bank[:, 0:P].unsqueeze(1).to_broadcast([P, H, P]),
                                      consts["heads8"].unsqueeze(2).to_broadcast([P, H, P]), ALU.mult).then_inc(q_done, 1)
                if u is not None:
                    s = u.c % 4
                    dve.wait_ge(y_ps, u.count(1, 1))
                    dve.tensor_tensor(z[:, s], y_bank[:, 0:P], xin[:, s], ALU.add).then_inc(z_done, 1)
                    dve.wait_ge(z_done, u.count(1, 1))
                    dve.bn_stats(stats[:], z[:, s]).then_inc(stats_done, 1)
                    dve.wait_ge(stats_done, u.count(1, 1))
                    dve.nop(nofuse=True)
                    dve.bn_aggr(mean_var[:, s], stats[:]).then_inc(mean_done, 1)

            run_steps(dve, step, n_seq, 5, 4)

        @block.tensor
        def _(pe):
            pe.wait_ge(ready, 5)
            ident = consts["ident"]

            def step(a, f, c, u):
                if c is not None:
                    s = c.c % 2
                    pe.wait_ge(q_done, c.count(1, 1))
                    pe.wait_ge(k_done, c.count(1, 1))
                    for j in range(2):
                        if c.back(1).real:
                            pe.wait_ge(weights_done, c.back(1).count(2, j + 1))
                        pe.matmul(s_bank[j], kT[:, s], q_masked[:, s, 4 * j:4 * j + 4], start=True, stop=True).then_inc(s_ps, 1)
                if u is not None:
                    s = u.c % 2
                    pe.wait_ge(o_done, u.count(1, 1))
                    if u.back(1).real:
                        pe.wait_ge(oT_done, u.back(1).count(1, 1))
                    pe.transpose(oT_bank[:, 0:P], o[:, s], ident).then_inc(oT_ps, 1)
                if f is not None:
                    s = f.c % 2
                    pe.wait_ge(xs_done, f.count(1, 1))
                    if f.back(1).real:
                        pe.wait_ge(xsT_done, f.back(1).count(1, 1))
                    pe.transpose(xsT_bank[:, 0:P], xs[:, s], ident).then_inc(xsT_ps, 1)
                if c is not None:
                    s = c.c % 2
                    pe.wait_ge(v_done, c.count(1, 1))
                    if c.back(1).real:
                        pe.wait_ge(o_done, c.back(1).count(1, 1))
                    pe.matmul(o_bank[:, 0:H * (D + 1)], ones[:], v_one[:, s].rearrange("p h d -> p (h d)"),
                              start=True, stop=False, skip_group_check=True)
                    for h in range(H):
                        pe.wait_ge(weights_done, c.count(2, h // 4 + 1))
                        mm = pe.matmul(o_bank[:, h * (D + 1):(h + 1) * (D + 1)], weights[:, h // 4, h % 4], v_one[:, s, h],
                                       start=False, stop=h == H - 1, skip_group_check=True)
                    mm.then_inc(o_ps, 1)
                if f is not None:
                    s = f.c % 2
                    pe.wait_ge(xsT_done, f.count(1, 1))
                    if f.back(1).real:
                        pe.wait_ge(q_done, f.back(1).count(1, 1))
                        pe.wait_ge(v_done, f.back(1).count(1, 1))
                    pe.matmul(q_bank[:, 0:P], wq[:], xsT[:, s], start=True, stop=True).then_inc(q_ps, 1)
                    pe.matmul(kv_bank[:, 0:P], wk[:], xsT[:, s], start=True, stop=True)
                    pe.matmul(kv_bank[:, P:2 * P], xsT[:, s], wv[:], start=True, stop=True).then_inc(kv_ps, 1)
                if u is not None:
                    s = u.c % 2
                    pe.wait_ge(oT_done, u.count(1, 1))
                    if u.back(1).real:
                        pe.wait_ge(z_done, u.back(1).count(1, 1))
                    pe.matmul(y_bank[:, 0:P], oT[:, s], w["wo"], start=True, stop=True).then_inc(y_ps, 1)

            run_steps(pe, step, n_seq, 4, 4)


def softmax_attention(chip, kind, n_seq, X, ctxT_dram, w, consts):
    nc = chip.nc
    H = 16
    D = 64 if kind == "wide" else 8
    NK = P if kind == "causal" else 77
    HU = 4
    UB = H // HU
    NU = 2 * UB
    OG = NU // 2
    n_pairs = n_seq // 2
    FU = {"wide": 11, "causal": 4, "rotary": 4}[kind]
    STRIP = 64 if kind == "wide" else 32
    CU = HU * STRIP // P
    NC = UB * CU
    SLOTS = 2
    with ExitStack() as ctx:
        def sb(name, shape):
            return chip.sb(ctx, kind + "_" + name, shape)

        def sem(name):
            return chip.sem(ctx, kind + "_" + name)

        power = sb("power", [P, 64])
        eps = sb("eps", [P, 2])
        xin = sb("xin", [P, 4, 2, P])
        xT = sb("xT", [P, 2, 2, P])
        values = sb("values", [P, 2, 2, H, STRIP])
        keys = sb("keys", [P, 2, H, 2, NK] if kind == "wide" else [P, 2, H, NK])
        shifted = sb("shifted", [P, SLOTS, HU * NK])
        exps = sb("exps", [P, SLOTS, HU, NK])
        exp_sum = sb("exp_sum", [P, SLOTS, HU])
        inv_sum = sb("inv_sum", [P, SLOTS, HU])
        probs = sb("probs", [P, SLOTS, HU, NK])
        probsT = sb("probsT", [P, 2, HU * P])
        row_max = sb("row_max", [P, 2, HU])
        oT = sb("oT", [P, 2, 2, NC, P])
        residual = sb("residual", [P, 2, 2, P])
        z = sb("z", [P, 4, 2, P])
        stats = sb("stats", [P, 2, 6])
        mean_var = sb("mean_var", [P, 4, 2, 2])
        var_eps = sb("var_eps", [P, 4, 2])
        rstd = sb("rstd", [P, 4, 2])
        if kind != "causal":
            ctxT = sb("ctxT", [P, 4, 2, P])
        if kind == "wide":
            xn = sb("xn", [P, 2, P])
            pre_stats = sb("pre_stats", [P, 2, 6])
            pre_mean_var = sb("pre_mean_var", [P, 2, 2])
            pre_var_eps = sb("pre_var_eps", [P, 2])
            pre_rstd = sb("pre_rstd", [P, 2])
            product = sb("product", [P, H, P])
        else:
            qT = sb("qT", [P, 2, 2, P])
            kT = sb("kT", [P, 2, 2, P])
        if kind == "rotary":
            qk = sb("qk", [P, 2, 2, H, 8])
            qk_sq = sb("qk_sq", [P, 4, H, 8])
            qk_sum = sb("qk_sum", [P, 4 * H])
            root_part = sb("root_part", [P, 4 * H])
            qk_rstd = sb("qk_rstd", [P, 4 * H])
            turned = sb("turned", [P, 4, H, 8])
            crossed = sb("crossed", [P, 4, H, 8])
            table = sb("table", [P, 2, 2, 8])
        if kind == "causal":
            biased = sb("biased", [P, 2, HU * NK])
            value_row = sb("value_row", [P, NC, P])
            q_bias = sb("q_bias", [P, 1])
        extra = sb("extra", [P, P])

        s_bank = [chip.banks[:, 0], chip.banks[:, 1]]
        p_bank = [chip.banks[:, 2], chip.banks[:, 3]]
        o_bank = [chip.banks[:, 4], chip.banks[:, 5]]
        f_bank, y_bank = chip.banks[:, 6], chip.banks[:, 7]

        x_loaded = [sem(f"x_loaded{n}") for n in range(4)]
        ready, prepared, prepared_ps, product_done = (sem(n) for n in ("ready", "prepared", "prepared_ps", "product_done"))
        READY = 4
        ROOT = 3 + 3 * NEWTON
        PREPARED = {"wide": 2, "causal": 3, "rotary": 6}[kind]
        front_ps, front_done, keys_done = sem("front_ps"), sem("front_done"), sem("keys_done")
        s_ps, max_done, shifted_done, exps_done, inv_done, probs_done = (
            sem(n) for n in ("s_ps", "max_done", "shifted_done", "exps_done", "inv_done", "probs_done"))
        biased_done = sem("biased_done")
        probsT_ps, probsT_done, pv_done = (sem(n) for n in ("probsT_ps", "probsT_done", "pv_done"))
        o_done, y_ps, residual_done = (sem(n) for n in ("o_done", "y_ps", "residual_done"))
        z_done, stats_done, mean_done, var_done, rstd_done, x_written = (
            sem(n) for n in ("z_done", "stats_done", "mean_done", "var_done", "rstd_done", "x_written"))
        pre_done, pre_var_done, pre_rstd_done, turn_done = (
            sem(n) for n in ("pre_done", "pre_var_done", "pre_rstd_done", "turn_done"))
        square_done, qk_rstd_done, scaled_done = (sem(n) for n in ("square_done", "qk_rstd_done", "scaled_done"))
        block = ctx.enter_context(nc.Block())
        TURNS = 3
        MLAG = 1
        KEYS_LEAD = 3 if kind == "causal" else 2

        def lagged(c, u, k, lag):
            if k - lag >= 0:
                return (c, k - lag) if c is not None else None
            return (u, k - lag + NU) if u is not None else None

        def before(pair, k, n):
            pair = pair.back((n - k + NU - 1) // NU) if n > k else pair
            return (pair, (k - n) % NU) if pair.real else None

        @block.sync
        def _(sp):
            def step(f):
                if f is None:
                    return
                s = f.c % 4
                if f.back(4).real:
                    sp.wait_ge(z_done, f.back(4).count(1, 1))
                sp.dma_start(xin[:, s], X[:, bass.ds(f.index(2), 2), :]).then_inc(x_loaded[s], 16)
                if kind != "causal":
                    sp.dma_start(ctxT[:, s, :, 0:77], ctxT_dram[:, bass.ds(f.index(2), 2), :]).then_inc(x_loaded[s], 16)

            if kind != "causal":
                sp.wait_ge(ready, READY)
            run_steps(sp, step, n_pairs, 1, 4)

        def wait_loaded(engine, f):
            m = 2 if kind != "causal" else 1
            v = 16 * m * (f.c // 4 + 1)
            engine.wait_ge(x_loaded[f.c % 4], v if f.i is None else f.i * (16 * m) + v)

        @block.gpsimd
        def _(pool):
            pool.memset(power[:], -0.5).then_inc(ready, 1)
            pool.memset(values[:], 0.0).then_inc(ready, 1)
            pool.memset(eps[:, 0:2], LN_EPS).then_inc(ready, 1)
            pool.memset(value_row[:] if kind == "causal" else ctxT[:], 1.0 if kind == "causal" else 0.0).then_inc(ready, 1)
            pool.wait_ge(ready, READY)
            pool.wait_ge(prepared, PREPARED)

            def make_keys(pair, piece):
                pool.wait_ge(front_done, pair.count(FU, 3 if kind == "rotary" else 2))
                if pair.back(1).real:
                    pool.wait_ge(s_ps, pair.back(1).count(NU, piece + 1))
                b, j = divmod(piece, UB)
                heads = slice(HU * j, HU * (j + 1))
                pool.tensor_tensor(keys[:, b, heads], kT[:, pair.c % 2, b, 0:NK].unsqueeze(1).to_broadcast([P, HU, NK]),
                                   consts["heads16"][:, heads].unsqueeze(2).to_broadcast([P, HU, NK]), ALU.mult).then_inc(keys_done, 1)

            def rotate(f, seq):
                for which, out, a, b, src in ((0, turned, 0, 8, 0), (1, crossed, 0, 4, 4), (1, crossed, 4, 8, 0)):
                    last = pool.tensor_tensor(out[:, 2 * seq:2 * seq + 2, :, a:b], qk[:, seq, :, :, src:src + b - a],
                                              table[:, which, :, a:b].unsqueeze(2).to_broadcast([P, 2, H, b - a]), ALU.mult)
                last.then_inc(turn_done, 1)

            def add_halves(f):
                pool.wait_ge(turn_done, f.count(TURNS, 2))
                pool.tensor_tensor(crossed[:], turned[:], crossed[:], ALU.add).then_inc(turn_done, 1)

            def step(f, c, u, n):
                for k in range(NU):
                    if kind != "wide":
                        at = (f, k - NU + KEYS_LEAD) if k >= NU - KEYS_LEAD else (c, k + KEYS_LEAD)
                        if at[0] is not None:
                            make_keys(*at)
                    at = lagged(c, u, k, MLAG)
                    if at is not None:
                        pair, m = at
                        pool.wait_ge(inv_done, pair.count(NU, m + 1))
                        if before(pair, m, SLOTS) is not None:
                            bc, bk = before(pair, m, SLOTS)
                            pool.wait_ge(probsT_ps, bc.count(NU, bk + 1))
                        pool.tensor_tensor(probs[:, m % SLOTS], exps[:, m % SLOTS], inv_sum[:, m % SLOTS].unsqueeze(2).to_broadcast([P, HU, NK]),
                                           ALU.mult).then_inc(probs_done, 1)
                    if f is not None and kind == "wide" and k == 1:
                        pool.wait_ge(pre_done, f.count(4, 4))
                        pool.tensor_tensor(pre_var_eps[:], pre_mean_var[:, :, 1], eps[:], ALU.add).then_inc(pre_var_done, 1)
                        pool.wait_ge(pre_var_done, f.count(1, 1))
                        pool.tensor_tensor(pre_rstd[:], pre_var_eps[:], power[:, 0:2], ALU.pow).then_inc(pre_rstd_done, 1)
                    if f is not None and kind == "rotary" and k in (1, 2):
                        pool.wait_ge(front_done, f.count(FU, 2))
                        if f.back(1).real:
                            pool.wait_ge(scaled_done, f.back(1).count(1, 1))
                        rotate(f, k - 1)
                    if f is not None and kind == "rotary" and k == 3:
                        add_halves(f)
                    if c is not None and kind != "rotary" and k == 3:
                        wait_loaded(pool, c)
                        if c.back(2).real:
                            pool.wait_ge(z_done, c.back(2).count(1, 1))
                        pool.tensor_tensor(residual[:, c.c % 2], xin[:, c.c % 4], extra[:].unsqueeze(1).to_broadcast([P, 2, P]),
                                           ALU.add).then_inc(residual_done, 1)
                    if n is not None and k == 0:
                        s = n.c % 4
                        pool.wait_ge(mean_done, n.count(2, 2))
                        pool.tensor_tensor(var_eps[:, s], mean_var[:, s, :, 1], eps[:], ALU.add).then_inc(var_done, 1)
                        pool.wait_ge(var_done, n.count(1, 1))
                        pool.tensor_tensor(rstd[:, s], var_eps[:, s], power[:, 0:2], ALU.pow).then_inc(rstd_done, 1)

            run_steps(pool, step, n_pairs, 4, 4)

        ident = consts["ident"]

        def front_pe(pe, f, m):
            s2, s4 = f.c % 2, f.c % 4
            if m == (10 if kind == "wide" else 0):
                if kind == "wide":
                    pe.wait_ge(turn_done, f.count(2, 2))
                else:
                    wait_loaded(pe, f)
                for b in range(2):
                    last = pe.transpose(f_bank[:, b * P:(b + 1) * P], xn[:, b] if kind == "wide" else xin[:, s4, b], ident)
                return last
            if kind == "wide":
                if m <= 5:
                    first = 3 * m
                    wait_loaded(pe, f)
                    for n in range(min(3, H - first)):
                        last = pe.matmul(f_bank[:, n * 154:(n + 1) * 154], product[:, first + n], ctxT[:, s4, :, 0:NK],
                                         start=True, stop=True)
                else:
                    b, half = divmod(m - 6, 2)
                    last = pe.matmul(f_bank[0:NK, :], ctxT[:, s4, b, 0:NK], w["wv"][:, half * 512:(half + 1) * 512],
                                     start=True, stop=True)
                return last
            pe.wait_ge(front_done, f.count(FU, 1))
            if kind == "causal":
                if m == 3:
                    for b in range(2):
                        last = pe.matmul(f_bank[:, b * P:(b + 1) * P], xT[:, s2, b], w["wv"], start=True, stop=True)
                    return last
                return pe.matmul(f_bank[:, 0:2 * P], w["wk"] if m == 1 else w["wq"], xT[:, s2], start=True, stop=True)
            if m == 1:
                for b in range(2):
                    pe.matmul(f_bank[:, 2 * b * P:(2 * b + 1) * P], xT[:, s2, b], w["wq"], start=True, stop=True)
                    last = pe.matmul(f_bank[:, (2 * b + 1) * P:(2 * b + 2) * P], ctxT[:, s4, b], w["wk"], start=True, stop=True)
            elif m == 3:
                for b in range(2):
                    last = pe.matmul(f_bank[0:NK, b * P:(b + 1) * P], ctxT[:, s4, b, 0:NK], w["wv"], start=True, stop=True)
            else:
                pe.wait_ge(scaled_done, f.count(1, 1))
                for n in range(4):
                    last = pe.transpose(f_bank[:, n * P:(n + 1) * P], turned[:, n].rearrange("p h d -> p (h d)"), ident)
            return last

        def front_act(act, f, m):
            s2 = f.c % 2
            copy = ACT.Copy
            if kind == "wide":
                if m == 10:
                    return act.activation(xT[:, s2], f_bank[:, 0:2 * P].rearrange("p (b q) -> p b q", b=2), ACT.Identity,
                                          scale=w["gamma"], bias=w["beta"])
                if m <= 5:
                    first = 3 * m
                    n = min(3, H - first)
                    return act.activation(keys[:, s2, first:first + n],
                                          f_bank[:, 0:n * 154].rearrange("p (h b k) -> p h b k", h=n, b=2), copy)
                b, half = divmod(m - 6, 2)
                return act.activation(values[0:NK, s2, b, 8 * half:8 * half + 8, 0:D],
                                      f_bank[0:NK, :].rearrange("p (h d) -> p h d", h=8), copy)
            if m == 0:
                return act.activation(xT[:, s2], f_bank[:, 0:2 * P].rearrange("p (b q) -> p b q", b=2), copy)
            if kind == "causal":
                two = f_bank[:, 0:2 * P].rearrange("p (b q) -> p b q", b=2)
                if m == 1:
                    if f.back(2).real:
                        act.wait_ge(keys_done, f.back(2).count(NU, NU))
                    return act.activation(kT[:, s2], two, ACT.Identity, bias=w["bk"])
                if m == 2:
                    return act.activation(qT[:, s2], two, ACT.Identity, bias=q_bias[:], scale=8.0 ** -0.5)
                return act.activation(values[:, s2, :, :, 0:D], f_bank[:, 0:2 * P].rearrange("p (b h d) -> p b h d", b=2, h=H), copy)
            if m == 1:
                if f.back(1).real:
                    act.wait_ge(turn_done, f.back(1).count(TURNS, 1))
                    act.wait_ge(square_done, f.back(1).count(1, 1))
                act.activation(qk_sq[:].rearrange("p n h d -> p (n h d)"), f_bank, ACT.Square)
                return act.activation(qk[:].rearrange("p b t h d -> p (b t h d)"), f_bank, copy)
            if m == 3:
                return act.activation(values[0:NK, s2, :, :, 0:D],
                                      f_bank[0:NK, 0:2 * P].rearrange("p (b h d) -> p b h d", b=2, h=H), copy)
            if f.back(2).real:
                act.wait_ge(keys_done, f.back(2).count(NU, NU))
            four = f_bank.rearrange("p (b t q) -> p b t q", b=2, t=2)
            act.activation(qT[:, s2], four[:, :, 0], copy)
            return act.activation(kT[:, s2], four[:, :, 1], copy)

        FRONT_AT = {"wide": [(0, 0), (0, 1), (1, 0), (2, 0), (3, 0), (4, 0), (5, 0), (5, 1), (6, 0), (6, 1), (7, 0)],
                    "causal": [(0, 0), (1, 0), (3, 0), (5, 0)], "rotary": [(0, 0), (1, 0), (6, 0), (7, 0)]}[kind]
        TLAG, PLAG, OLAG = 3, 4, 5
        Y_AT, Z_AT = 6, 7

        @block.tensor
        def _(pe):
            pe.wait_ge(ready, READY)
            if kind == "wide":
                for h in range(H):
                    if h >= 1:
                        pe.wait_ge(product_done, h)
                    pe.matmul(f_bank[:, 0:P], w["wkT"][:, h], w["wqT"][:, h], start=True, stop=True).then_inc(prepared_ps, 1)
                pe.wait_ge(product_done, H)
                pe.wait_ge(prepared, PREPARED)
            elif kind == "causal":
                pe.wait_ge(prepared, 1)
                for n in range(NC):
                    last = pe.matmul(f_bank[:, 0:P], value_row[:, n], w["wo"][:, n], start=n == 0, stop=n == NC - 1)
                last.then_inc(prepared_ps, 1)
                pe.wait_ge(prepared, PREPARED)
            else:
                pe.wait_ge(prepared, PREPARED)

            def front(f, k, place):
                for m in range(FU):
                    if FRONT_AT[m] == (k, place):
                        if m >= 1:
                            pe.wait_ge(front_done, f.count(FU, m))
                        elif f.back(1).real:
                            pe.wait_ge(front_done, f.back(1).count(FU, FU))
                        front_pe(pe, f, m).then_inc(front_ps, 1)

            def project(u):
                pe.wait_ge(o_done, u.count(OG, OG))
                if u.back(1).real:
                    pe.wait_ge(z_done, u.back(1).count(1, 1))
                for b in range(2):
                    for n in range(NC):
                        last = pe.matmul(y_bank[:, b * P:(b + 1) * P], oT[:, u.c % 2, b, n],
                                         w["wo_scaled" if kind == "wide" else "wo"][:, n], start=n == 0, stop=n == NC - 1)
                last.then_inc(y_ps, 1)

            def step(f, c, u):
                for k in range(NU):
                    if c is not None:
                        b, j = divmod(k, UB)
                        if k == 0:
                            pe.wait_ge(front_done, c.count(FU, FU))
                        if kind != "wide":
                            pe.wait_ge(keys_done, c.count(NU, k + 1))
                        if before(c, k, 2) is not None:
                            bc, bk = before(c, k, 2)
                            pe.wait_ge(biased_done if kind == "causal" else shifted_done, bc.count(NU, bk + 1))
                        if kind == "wide":
                            q = xT[:, c.c % 2, b]
                            moving = keys[:, c.c % 2, HU * j:HU * j + HU, b]
                        else:
                            q = qT[:, c.c % 2, b]
                            moving = keys[:, b, HU * j:HU * j + HU]
                        pe.matmul(s_bank[k % 2][:, 0:HU * NK], q, moving, start=True, stop=True).then_inc(s_ps, 1)
                    at = lagged(c, u, k, TLAG)
                    if at is not None:
                        pair, n = at
                        pe.wait_ge(probs_done, pair.count(NU, n + 1))
                        if before(pair, n, 2) is not None:
                            bc, bk = before(pair, n, 2)
                            pe.wait_ge(probsT_done, bc.count(NU, bk + 1))
                        for h in range(HU):
                            last = pe.transpose(p_bank[n % 2][0:NK, h * P:(h + 1) * P], probs[:, n % SLOTS, h], ident)
                        last.then_inc(probsT_ps, 1)
                    if f is not None:
                        front(f, k, 0)
                    at = lagged(c, u, k, PLAG)
                    if at is not None:
                        pair, n = at
                        b, j = divmod(n, UB)
                        g = n // 2
                        pe.wait_ge(probsT_done, pair.count(NU, n + 1))
                        if n % 2 == 0 and before(pair, n, 4) is not None:
                            bc, bk = before(pair, n, 4)
                            pe.wait_ge(o_done, bc.count(OG, bk // 2 + 1))
                        for h in range(HU):
                            chunk, row = divmod(STRIP * h, P)
                            col = ((n % 2) * CU + chunk) * P
                            last = pe.matmul(o_bank[g % 2][row:row + STRIP, col:col + P], values[0:NK, pair.c % 2, b, HU * j + h],
                                             probsT[0:NK, n % 2, h * P:(h + 1) * P], start=True, stop=True)
                        last.then_inc(pv_done, 1)
                    if f is not None:
                        front(f, k, 1)
                    if u is not None and k == Y_AT:
                        project(u)

            run_steps(pe, step, n_pairs, 3, 4)

        @block.scalar
        def _(act):
            if kind == "wide":
                for h in range(H):
                    act.wait_ge(prepared_ps, h + 1)
                    act.activation(product[:, h], f_bank[:, 0:P], ACT.Copy, scale=64.0 ** -0.5).then_inc(product_done, 1)

            def front(f, k, place):
                for m in range(FU):
                    if FRONT_AT[m] == (k, place):
                        act.wait_ge(front_ps, f.count(FU, m + 1))
                        if f.back(2).real:
                            if m == (0 if kind == "wide" else 2):
                                act.wait_ge(s_ps, f.back(2).count(NU, NU))
                            if m == (6 if kind == "wide" else 3):
                                act.wait_ge(pv_done, f.back(2).count(NU, NU))
                        front_act(act, f, m).then_inc(front_done, 1)

            def step(f, c, u):
                for k in range(NU):
                    at = lagged(c, u, k, TLAG)
                    if at is not None:
                        pair, n = at
                        act.wait_ge(probsT_ps, pair.count(NU, n + 1))
                        if before(pair, n, 2) is not None:
                            bc, bk = before(pair, n, 2)
                            act.wait_ge(pv_done, bc.count(NU, bk + 1))
                        act.activation(probsT[0:NK, n % 2], p_bank[n % 2][0:NK], ACT.Copy).then_inc(probsT_done, 1)
                    if f is not None:
                        front(f, k, 0)
                    if c is not None:
                        act.wait_ge(shifted_done, c.count(NU, k + 1))
                        if before(c, k, SLOTS) is not None:
                            bc, bk = before(c, k, SLOTS)
                            act.wait_ge(probs_done, bc.count(NU, bk + 1))
                        for h in range(HU):
                            last = act.activation(exps[:, k % SLOTS, h], shifted[:, k % SLOTS, h * NK:(h + 1) * NK], ACT.Exp,
                                                  accum_out=exp_sum[:, k % SLOTS, h:h + 1])
                        last.then_inc(exps_done, 1)
                    if f is not None:
                        front(f, k, 1)
                    at = lagged(c, u, k, OLAG)
                    if at is not None and at[1] % 2 == 1:
                        pair, n = at
                        b, j = divmod(n - 1, UB)
                        act.wait_ge(pv_done, pair.count(NU, n + 1))
                        if pair.back(2).real:
                            act.wait_ge(y_ps, pair.back(2).count(1, 1))
                        act.activation(oT[:, pair.c % 2, b, CU * j:CU * (j + 2)].rearrange("p n q -> p (n q)"),
                                       o_bank[(n // 2) % 2][:, 0:2 * CU * P], ACT.Copy).then_inc(o_done, 1)

            run_steps(act, step, n_pairs, 3, 4)

        @block.vector
        def _(dve):
            if kind == "wide":
                dve.tensor_scalar(w["wo_scaled"], w["wo"], w["tanh_gate"], None, ALU.mult).then_inc(prepared, 1)
                dve.tensor_scalar(extra[:], w["bo"], w["tanh_gate"], None, ALU.mult).then_inc(prepared, 1)
            elif kind == "causal":
                dve.wait_ge(ready, READY)
                dve.tensor_tensor(value_row[:], value_row[:], w["bv"].unsqueeze(2).to_broadcast([P, NC, P]), ALU.mult).then_inc(prepared, 1)
                dve.tensor_scalar(q_bias[:], w["bq"], 8.0 ** -0.5, None, ALU.mult).then_inc(prepared, 1)
                dve.wait_ge(prepared_ps, 1)
                dve.tensor_tensor(extra[:], f_bank[:, 0:P], w["bo"], ALU.add).then_inc(prepared, 1)
            else:
                for t, name in enumerate(("q_norm", "k_norm")):
                    wn = w[name]
                    scale = 1.0 if t == 0 else 8.0 ** 0.5
                    dve.scalar_tensor_tensor(out=table[:, 0, t], in0=consts["rope"][:, 0, t], scalar=scale, in1=wn,
                                             op0=ALU.mult, op1=ALU.mult).then_inc(prepared, 1)
                    for half in range(2):
                        a, b = 4 * half, 4 * (1 - half)
                        dve.scalar_tensor_tensor(out=table[:, 1, t, a:a + 4], in0=consts["rope"][:, 1, t, a:a + 4], scalar=scale,
                                                 in1=wn[:, b:b + 4], op0=ALU.mult, op1=ALU.mult).then_inc(prepared, 1)
                dve.wait_ge(prepared, 6)

            def inverse_root(f, part):
                n = [3 * part]

                def link(ins):
                    n[0] += 1
                    ins.then_inc(qk_rstd_done, 1)
                    dve.wait_ge(qk_rstd_done, f.count(ROOT, n[0]))

                y, bits = qk_rstd[:], qk_rstd[:].bitcast(I32)
                if part == 0:
                    dve.wait_ge(square_done, f.count(1, 1))
                    link(dve.tensor_scalar(qk_sum[:], qk_sum[:], 8e-6, None, ALU.add))
                    link(dve.tensor_scalar(bits, qk_sum[:].bitcast(I32), 1, 0x7fffffff,
                                           ALU.logical_shift_right, ALU.bitwise_xor))
                    link(dve.tensor_scalar(y, y, SEED_SCALE, None, ALU.mult))
                else:
                    link(dve.tensor_tensor(root_part[:], y, y, ALU.mult))
                    link(dve.scalar_tensor_tensor(out=root_part[:], in0=root_part[:], scalar=-0.5, in1=qk_sum[:], op0=ALU.mult, op1=ALU.mult))
                    link(dve.scalar_tensor_tensor(out=y, in0=root_part[:], scalar=1.5, in1=y, op0=ALU.add, op1=ALU.mult))
                assert n[0] == 3 * part + 3, n

            def step(f, c, u, n):
                for k in range(NU):
                    if n is not None and k in (3, 4):
                        s, b = n.c % 4, k - 3
                        dve.wait_ge(rstd_done, n.count(1, 1))
                        dve.tensor_scalar(X[:, n.index(2, b), :], z[:, s, b], mean_var[:, s, b, 0:1], rstd[:, s, b:b + 1],
                                          ALU.subtract, ALU.mult).then_inc(x_written, 1)
                    if c is not None:
                        dve.wait_ge(s_ps, c.count(NU, k + 1))
                        scores = s_bank[k % 2][:, 0:HU * NK]
                        if kind == "causal":
                            j = k % UB
                            dve.tensor_tensor(biased[:, k % 2], scores, consts["alibi"][:, HU * NK * j:HU * NK * (j + 1)],
                                              ALU.add).then_inc(biased_done, 1)
                            dve.wait_ge(biased_done, c.count(NU, k + 1))
                            scores = biased[:, k % 2]
                        scores = scores.rearrange("p (h n) -> p h n", h=HU)
                        dve.tensor_reduce(row_max[:, k % 2], scores, AX.X, ALU.max).then_inc(max_done, 1)
                        dve.wait_ge(max_done, c.count(NU, k + 1))
                        if before(c, k, SLOTS) is not None:
                            bc, bk = before(c, k, SLOTS)
                            dve.wait_ge(exps_done, bc.count(NU, bk + 1))
                        dve.tensor_tensor(shifted[:, k % SLOTS].rearrange("p (h n) -> p h n", h=HU), scores,
                                          row_max[:, k % 2].unsqueeze(2).to_broadcast([P, HU, NK]),
                                          ALU.subtract).then_inc(shifted_done, 1)
                    at = lagged(c, u, k, MLAG)
                    if at is not None:
                        pair, m = at
                        dve.wait_ge(exps_done, pair.count(NU, m + 1))
                        if before(pair, m, SLOTS) is not None:
                            bc, bk = before(pair, m, SLOTS)
                            dve.wait_ge(probs_done, bc.count(NU, bk + 1))
                        dve.reciprocal(inv_sum[:, m % SLOTS], exp_sum[:, m % SLOTS]).then_inc(inv_done, 1)
                    if f is not None and kind == "wide":
                        if k == 0:
                            wait_loaded(dve, f)
                            for b in range(2):
                                dve.bn_stats(pre_stats[:, b], xin[:, f.c % 4, b]).then_inc(pre_done, 1)
                            dve.wait_ge(pre_done, f.count(4, 2))
                            if f.back(1).real:
                                dve.wait_ge(turn_done, f.back(1).count(2, 2))
                            dve.nop(nofuse=True)
                            for b in range(2):
                                dve.bn_aggr(pre_mean_var[:, b], pre_stats[:, b]).then_inc(pre_done, 1)
                        if k == 2:
                            dve.wait_ge(pre_rstd_done, f.count(1, 1))
                            if f.back(1).real:
                                dve.wait_ge(front_ps, f.back(1).count(FU, FU))
                            for b in range(2):
                                dve.tensor_scalar(xn[:, b], xin[:, f.c % 4, b], pre_mean_var[:, b, 0:1], pre_rstd[:, b:b + 1],
                                                  ALU.subtract, ALU.mult).then_inc(turn_done, 1)
                    if f is not None and kind == "rotary":
                        four = qk[:].rearrange("p b t h d -> p (b t) h d")
                        if k == 2:
                            dve.wait_ge(front_done, f.count(FU, 2))
                            dve.tensor_reduce(qk_sum[:].rearrange("p (n h) -> p n h", n=4), qk_sq[:], AX.X, ALU.add).then_inc(square_done, 1)
                            inverse_root(f, 0)
                        if k == 3:
                            inverse_root(f, 1)
                            inverse_root(f, 2)
                        if k == 4:
                            inverse_root(f, 3)
                            dve.wait_ge(turn_done, f.count(TURNS, TURNS))
                            if f.back(1).real:
                                dve.wait_ge(front_ps, f.back(1).count(FU, 3))
                            dve.tensor_tensor(turned[:].rearrange("p n h d -> p (n h) d"), crossed[:].rearrange("p n h d -> p (n h) d"),
                                              qk_rstd[:].unsqueeze(2).to_broadcast([P, 4 * H, 8]), ALU.mult).then_inc(scaled_done, 1)
                    if u is not None and k == Z_AT:
                        s = u.c % 4
                        dve.wait_ge(y_ps, u.count(1, 1))
                        if kind == "rotary":
                            x_part = xin[:, s]
                        else:
                            dve.wait_ge(residual_done, u.count(1, 1))
                            x_part = residual[:, u.c % 2]
                        dve.tensor_tensor(z[:, s], y_bank[:, 0:2 * P].rearrange("p (b q) -> p b q", b=2), x_part, ALU.add).then_inc(z_done, 1)
                        dve.wait_ge(z_done, u.count(1, 1))
                        for b in range(2):
                            dve.bn_stats(stats[:, b], z[:, s, b]).then_inc(stats_done, 1)
                        dve.wait_ge(stats_done, u.count(2, 2))
                        dve.nop(nofuse=True)
                        for b in range(2):
                            dve.bn_aggr(mean_var[:, s, b], stats[:, b]).then_inc(mean_done, 1)

            run_steps(dve, step, n_pairs, 4, 4)


def mixture(chip, kind, n_seq, X, out_dram, w, consts):
    nc = chip.nc
    swiglu = kind == "swiglu"
    E = 8
    NE = E + 1 if swiglu else E
    C = 2 if swiglu else 4
    T = 4
    groups = n_seq // T
    HS = 4
    LAG = 2
    R = 19
    with ExitStack() as ctx:
        def sb(name, shape):
            return chip.sb(ctx, kind + "_" + name, shape)

        def sem(name):
            return chip.sem(ctx, kind + "_" + name)

        power, eps = sb("power", [P, T]), sb("eps", [P, T])
        xin = sb("xin", [P, 4, T, P])
        xT = sb("xT", [P, T * P])
        xT_masked = sb("xT_masked", [P, T * P])
        xT_high, xT_low = (chip.sb(ctx, f"{kind}_{n}", [P, 2, T * P], F32R) for n in ("xT_high", "xT_low"))
        hidden = sb("hidden", [P, HS, C, T * P])
        in_names = ("w1", "w3") if swiglu else ("w1",)
        w_high, w_low = ({n: chip.sb(ctx, f"{kind}_{n}_{part}", [P, NE * C * P], F32R) for n in in_names} for part in ("high", "low"))
        gate = sb("gate", [P, 2, T, NE])
        small = {n: sb(n, [P, T, E]) for n in ("logits", "expd", "choice", "equal", "ranked", "picked", "first")}
        tops = {n: sb(n, [P, T]) for n in ("top", "key_top", "rank_top", "total", "inv_total")}
        z = sb("z", [P, 4, T, P])
        stats = sb("stats", [P, T, 6])
        mean_var = sb("mean_var", [P, 4, T, 2])
        var_eps = sb("var_eps", [P, T])
        rstd = sb("rstd", [P, 2, T])
        if swiglu:
            silu = sb("silu", [P, 2, T * P])
        else:
            gateT = sb("gateT", [E, T * P])
        h_bank = [chip.banks[:, n] for n in range(4)]
        y_bank = [chip.banks[:, 4], chip.banks[:, 5]]
        x_bank, r_bank = chip.banks[:, 6], chip.banks[:, 7]

        x_loaded = [sem(f"x_loaded{n}") for n in range(4)]
        ready, xT_ps, xT_done, logits_ps, routed, exp_done, gateT_ps, gateT_done, base_ps, base_done = (
            sem(n) for n in ("ready", "xT_ps", "xT_done", "logits_ps", "routed", "exp_done", "gateT_ps", "gateT_done",
                             "base_ps", "base_done"))
        h_ps, silu_done, h_done, y_ps, summed = (sem(n) for n in ("h_ps", "silu_done", "h_done", "y_ps", "summed"))
        masked_done, w_split, xT_masked_done, xT_split = (sem(n) for n in ("masked_done", "w_split", "xT_masked_done", "xT_split"))
        stats_done, mean_done, var_done, rstd_done, x_written, stored = (
            sem(n) for n in ("stats_done", "mean_done", "var_done", "rstd_done", "x_written", "stored"))
        block = ctx.enter_context(nc.Block())
        ident = consts["ident"]

        def lagged(c, u, e):
            if e >= LAG:
                return (c, e - LAG) if c is not None else None
            return (u, e - LAG + NE) if u is not None else None

        def before(g, e, n):
            if e >= n:
                return (g, e - n)
            return (g.back(1), e - n + NE) if g.back(1).real else None

        @block.sync
        def _(sp):
            def step(f, c, u, n):
                if f is not None:
                    s = f.c % 4
                    if f.back(4).real:
                        sp.wait_ge(mean_done, f.back(4).count(T, T))
                    sp.dma_start(xin[:, s], X[:, bass.ds(f.index(T), T), :]).then_inc(x_loaded[s], 16)
                if n is not None and out_dram is not None:
                    sp.wait_ge(x_written, n.count(T, T))
                    sp.dma_start(out_dram[bass.ds(n.index(T), T)].rearrange("b t d -> t b d"),
                                 X[:, bass.ds(n.index(T), T), :]).then_inc(stored, 16)

            run_steps(sp, step, groups, 4, 4)
            if out_dram is not None:
                sp.wait_ge(stored, 16 * groups)

        @block.gpsimd
        def _(pool):
            pool.memset(power[:], -0.5).then_inc(ready, 1)
            pool.memset(gate[:], 1.0).then_inc(ready, 1)
            pool.memset(eps[:], LN_EPS).then_inc(ready, 1)
            pool.wait_ge(ready, 3)

            def step(f, c, u):
                if f is not None:
                    pool.wait_ge(xT_masked_done, f.count(1, 1))
                    if f.back(2).real:
                        pool.wait_ge(h_ps, f.back(2).count(NE * C, NE * C))
                    pool.nop(nofuse=True)
                    pool.tensor_copy(xT_high[:, f.c % 2], xT_masked[:]).then_inc(xT_split, 1)
                    pool.tensor_tensor(xT_low[:, f.c % 2], xT[:], xT_masked[:], ALU.subtract).then_inc(xT_split, 1)
                if u is not None:
                    s = u.c % 4
                    pool.wait_ge(mean_done, u.count(T, T))
                    if u.back(1).real:
                        pool.wait_ge(rstd_done, u.back(1).count(1, 1))
                    pool.tensor_tensor(var_eps[:], mean_var[:, s, :, 1], eps[:], ALU.add).then_inc(var_done, 1)
                    pool.wait_ge(var_done, u.count(1, 1))
                    if u.back(2).real:
                        pool.wait_ge(x_written, u.back(2).count(T, T))
                    pool.tensor_tensor(rstd[:, u.c % 2], var_eps[:], power[:], ALU.pow).then_inc(rstd_done, 1)

            run_steps(pool, step, groups, 3, 4)

        @block.scalar
        def _(act):
            def step(f, c, u):
                for e in range(NE):
                    if c is not None:
                        par = (c.c * NE + e) % HS
                        if before(c, e, HS) is not None:
                            g, be = before(c, e, HS)
                            act.wait_ge(y_ps, g.count(NE, be + 1))
                        for m in range(C):
                            act.wait_ge(h_ps, c.count(NE * C, e * C + m + 1))
                            if swiglu:
                                if e >= 1 or c.back(1).real:
                                    act.wait_ge(h_done, c.count(NE * C, (e - 1) * C + m + 1))
                                act.activation(silu[:, m], h_bank[2 * m], ACT.Silu).then_inc(silu_done, 1)
                            else:
                                act.activation(hidden[:, par, m], h_bank[m], ACT.Gelu, bias=w["b1"][:, e, m:m + 1]).then_inc(h_done, 1)
                    if f is not None:
                        if e == 1:
                            act.wait_ge(xT_ps, f.count(1, 1))
                            if f.back(1).real:
                                act.wait_ge(xT_split, f.back(1).count(2, 2))
                                act.wait_ge(logits_ps, f.back(1).count(1, 1))
                            act.activation(xT[:], x_bank, ACT.Copy).then_inc(xT_done, 1)
                        if e == 3:
                            act.wait_ge(routed, f.count(R, 2))
                            act.activation(small["expd"][:], small["logits"][:], ACT.Exp).then_inc(exp_done, 1)
                        if e == 6 and not swiglu:
                            act.wait_ge(gateT_ps, f.count(1, 1))
                            act.activation(gateT[:], r_bank[0:E], ACT.Copy).then_inc(gateT_done, 1)

            run_steps(act, step, groups, 3, 4)

        @block.vector
        def _(dve):
            dve.wait_ge(ready, 3)
            for n, t in enumerate(in_names):
                masked = hidden[:].rearrange("p s c t -> p (s c t)")[:, 0:NE * C * P]
                if n >= 1:
                    dve.wait_ge(w_split, 2 * n)
                dve.tensor_scalar(masked.bitcast(I32), w[t].bitcast(I32), HIGH, None, ALU.bitwise_and).then_inc(masked_done, 1)
                dve.wait_ge(masked_done, n + 1)
                dve.tensor_copy(w_high[t][:], masked).then_inc(w_split, 1)
                dve.tensor_tensor(w_low[t][:], w[t], masked, ALU.subtract).then_inc(w_split, 1)

            def route(f, part):
                n = [0 if part == 0 else 2]

                def link(ins):
                    n[0] += 1
                    ins.then_inc(routed, 1)
                    dve.wait_ge(routed, f.count(R, n[0]))

                def over(t):
                    return t[:].unsqueeze(2).to_broadcast([P, T, E])

                def row(t):
                    return t.unsqueeze(1).to_broadcast([P, T, E])

                logits, expd, choice, equal, ranked, picked, first = (
                    small[n][:] for n in ("logits", "expd", "choice", "equal", "ranked", "picked", "first"))
                top, key_top, rank_top, total, inv_total = (tops[n] for n in ("top", "key_top", "rank_top", "total", "inv_total"))
                if part == 0:
                    dve.wait_ge(logits_ps, f.count(1, 1))
                    ps = r_bank[:, 0:T * E].rearrange("p (t e) -> p t e", t=T)
                    link(dve.tensor_reduce(top[:], ps, AX.X, ALU.max))
                    link(dve.tensor_tensor(logits, ps, over(top), ALU.subtract))
                    return
                dve.wait_ge(exp_done, f.count(1, 1))
                if swiglu:
                    link(dve.tensor_reduce(total[:], expd, AX.X, ALU.add))
                    link(dve.reciprocal(inv_total[:], total[:]))
                    link(dve.tensor_tensor(expd, expd, over(inv_total), ALU.mult))
                    link(dve.tensor_tensor(choice, expd, row(w["gate_bias"]), ALU.add))
                else:
                    link(dve.tensor_copy(choice, expd))
                for turn in range(2):
                    link(dve.tensor_reduce(key_top[:], choice, AX.X, ALU.max))
                    link(dve.tensor_tensor(equal, choice, over(key_top), ALU.is_equal))
                    link(dve.tensor_tensor(ranked, equal, row(consts["rank8"]), ALU.mult))
                    link(dve.tensor_reduce(rank_top[:], ranked, AX.X, ALU.max))
                    link(dve.tensor_tensor(first if turn == 0 else picked, ranked, over(rank_top), ALU.is_equal))
                    if turn == 0:
                        link(dve.scalar_tensor_tensor(out=choice.rearrange("p t e -> p (t e)"), in0=first.rearrange("p t e -> p (t e)"),
                                                      scalar=-1e30, in1=choice.rearrange("p t e -> p (t e)"), op0=ALU.mult, op1=ALU.add))
                if swiglu:
                    link(dve.tensor_tensor(picked, picked, first, ALU.add))
                else:
                    link(dve.tensor_tensor(picked, picked, first, ALU.add))
                    dve_gate(f, picked, expd, link, over, total, inv_total)
                    assert n[0] == R, n
                    return
                out = gate[:, f.c % 2, :, 0:E]
                if f.back(2).real:
                    dve.wait_ge(summed, f.back(2).count(NE * T, NE * T))
                link(dve.tensor_tensor(out, picked, expd, ALU.mult))
                assert n[0] == R, n

            def dve_gate(f, picked, expd, link, over, total, inv_total):
                link(dve.tensor_tensor(picked, picked, expd, ALU.mult))
                link(dve.tensor_reduce(total[:], picked, AX.X, ALU.add))
                link(dve.reciprocal(inv_total[:], total[:]))
                link(dve.tensor_tensor(gate[:, f.c % 2, :, 0:E], picked, over(inv_total), ALU.mult))

            def step(f, c, u, n):
                for e in range(NE):
                    if c is not None and swiglu:
                        par = (c.c * NE + e) % HS
                        for m in range(C):
                            dve.wait_ge(silu_done, c.count(NE * C, e * C + m + 1))
                            dve.tensor_tensor(hidden[:, par, m], silu[:, m], h_bank[2 * m + 1], ALU.mult).then_inc(h_done, 1)
                    if f is not None and e == 2:
                        dve.wait_ge(xT_done, f.count(1, 1))
                        if f.back(1).real:
                            dve.wait_ge(xT_split, f.back(1).count(2, 2))
                        dve.tensor_scalar(xT_masked[:].bitcast(I32), xT[:].bitcast(I32), HIGH, None,
                                          ALU.bitwise_and).then_inc(xT_masked_done, 1)
                    at = lagged(c, u, e)
                    if at is not None:
                        g, n_exp = at
                        dve.wait_ge(y_ps, g.count(NE, n_exp + 1))
                        if n_exp >= 1:
                            dve.wait_ge(summed, g.count(NE * T, n_exp * T))
                        elif not swiglu:
                            dve.wait_ge(base_done, g.count(1, 1))
                        for t in range(T):
                            rest = z[:, g.c % 4, t] if n_exp >= 1 or not swiglu else xin[:, g.c % 4, t]
                            dve.scalar_tensor_tensor(out=z[:, g.c % 4, t], in0=y_bank[(g.c * NE + n_exp) % 2][:, t * P:(t + 1) * P],
                                                     scalar=gate[:, g.c % 2, t, n_exp:n_exp + 1], in1=rest,
                                                     op0=ALU.mult, op1=ALU.add).then_inc(summed, 1)
                    if u is not None and e == LAG - 1:
                        s = u.c % 4
                        dve.wait_ge(summed, u.count(NE * T, NE * T))
                        for t in range(T):
                            dve.bn_stats(stats[:, t], z[:, s, t]).then_inc(stats_done, 1)
                        dve.wait_ge(stats_done, u.count(T, T))
                        dve.nop(nofuse=True)
                        for t in range(T):
                            dve.bn_aggr(mean_var[:, s, t], stats[:, t]).then_inc(mean_done, 1)
                    if n is not None and e == 1:
                        s = n.c % 4
                        dve.wait_ge(rstd_done, n.count(1, 1))
                        for t in range(T):
                            dve.tensor_scalar(X[:, n.index(T, t), :], z[:, s, t], mean_var[:, s, t, 0:1],
                                              rstd[:, n.c % 2, t:t + 1], ALU.subtract, ALU.mult).then_inc(x_written, 1)
                    if f is not None and e in (2, 4):
                        route(f, 0 if e == 2 else 1)
                    if f is not None and e == 7 and not swiglu:
                        dve.wait_ge(base_ps, f.count(1, 1))
                        dve.tensor_tensor(z[:, f.c % 4], r_bank.rearrange("p (t d) -> p t d", t=T), xin[:, f.c % 4], ALU.add).then_inc(base_done, 1)

            run_steps(dve, step, groups, 4, 4)

        @block.tensor
        def _(pe):
            def product(out, a_high, a_low, b_high, b_low):
                pe.matmul(out, a_high, b_high, start=True, stop=False)
                pe.matmul(out, a_high, b_low, start=False, stop=False)
                return pe.matmul(out, a_low, b_high, start=False, stop=True)

            pe.wait_ge(w_split, 2 * len(in_names))

            def step(f, c, u):
                for e in range(NE):
                    if c is not None:
                        if e == 0:
                            pe.wait_ge(xT_split, c.count(2, 2))
                        for m in range(C):
                            if e >= 1 or c.back(1).real:
                                pe.wait_ge(h_done, c.count(NE * C, (e - 1) * C + m + 1))
                            cols = slice(e * C * P + m * P, e * C * P + (m + 1) * P)
                            for n, name in enumerate(in_names):
                                last = product(h_bank[len(in_names) * m + n], w_high[name][:, cols], w_low[name][:, cols],
                                               xT_high[:, c.c % 2], xT_low[:, c.c % 2])
                            last.then_inc(h_ps, 1)
                    at = lagged(c, u, e)
                    if at is not None:
                        g, n_exp = at
                        par = (g.c * NE + n_exp) % 2
                        slot = (g.c * NE + n_exp) % HS
                        if before(g, n_exp, 2) is not None:
                            bg, be = before(g, n_exp, 2)
                            pe.wait_ge(summed, bg.count(NE * T, (be + 1) * T))
                        for t in range(T):
                            for m in range(C):
                                if t == 0:
                                    pe.wait_ge(h_done, g.count(NE * C, n_exp * C + m + 1))
                                tokens = slice(t * P, (t + 1) * P)
                                last = pe.matmul(y_bank[par][:, tokens], hidden[:, slot, m, tokens], w["w2"][:, n_exp, m],
                                                 start=m == 0, stop=m == C - 1)
                        last.then_inc(y_ps, 1)
                    if f is not None and e == 0:
                        pe.wait_ge(x_loaded[f.c % 4], f.load(4))
                        if f.back(1).real:
                            pe.wait_ge(xT_done, f.back(1).count(1, 1))
                        for t in range(T):
                            last = pe.transpose(x_bank[:, t * P:(t + 1) * P], xin[:, f.c % 4, t], ident)
                        last.then_inc(xT_ps, 1)
                    if f is not None and e == 2:
                        pe.wait_ge(xT_done, f.count(1, 1))
                        if f.back(1).real:
                            if swiglu:
                                pe.wait_ge(routed, f.back(1).count(R, 2))
                            else:
                                pe.wait_ge(base_done, f.back(1).count(1, 1))
                        for t in range(T):
                            last = pe.matmul(r_bank[:, t * E:(t + 1) * E], xT[:, t * P:(t + 1) * P], w["router"],
                                             start=True, stop=True)
                        last.then_inc(logits_ps, 1)
                    if f is not None and not swiglu:
                        if e == 6:
                            pe.wait_ge(routed, f.count(R, R))
                            for t in range(T):
                                last = pe.transpose(r_bank[0:E, t * P:(t + 1) * P], gate[:, f.c % 2, t, 0:E], ident)
                            last.then_inc(gateT_ps, 1)
                        if e == 7:
                            pe.wait_ge(gateT_done, f.count(1, 1))
                            for t in range(T):
                                last = pe.matmul(r_bank[:, t * P:(t + 1) * P], gateT[:, t * P:(t + 1) * P], w["b2"],
                                                 start=True, stop=True)
                            last.then_inc(base_ps, 1)

            run_steps(pe, step, groups, 3, 4)


SMALL = {
    "ident": [P, P], "heads8": [P, 8], "heads16": [P, 16], "rank8": [P, 8], "rope": [P, 2, 2, 8],
    "ta_gamma": [P, 1], "ta_wq": [P, P], "ta_wk": [P, P], "ta_wv": [P, P], "ta_wo": [P, P],
    "cx_gamma": [P, 1], "cx_beta": [P, 1], "cx_gate": [P, 1], "cx_bo": [P, P],
    "g_router": [P, 8], "g_b1": [P, 8, 4], "g_b2": [8, P],
    "sa_wq": [P, P], "sa_wk": [P, P], "sa_wv": [P, P], "sa_wo": [P, 4, P], "sa_bq": [P, 1], "sa_bk": [P, 1], "sa_bv": [P, 4], "sa_bo": [P, P],
    "ra_wq": [P, P], "ra_wk": [P, P], "ra_wv": [P, P], "ra_wo": [P, 4, P], "ra_qn": [P, 8], "ra_kn": [P, 8],
    "s_router": [P, 8], "s_bias": [P, 8],
}
LARGE = {
    "cx_wqT": [64, 16, P], "cx_wkT": [64, 16, P], "cx_wv": [P, 1024], "cx_wo": [P, 8, P],
    "g_w1": [P, 8 * 512], "g_w2": [P, 8, 4, P],
    "alibi": [P, 16 * P],
    "s_w1": [P, 9 * 256], "s_w3": [P, 9 * 256], "s_w2": [P, 9, 2, P],
}


def build(nc, n_seq, x_dram, ctxT_dram, weights_dram, out_dram, blocks=(1, 2, 3, 4, 5, 6), x_state=None):
    with ExitStack() as ctx:
        chip = Chip(nc, ctx)
        X = chip.sb(ctx, "X", [P, n_seq, P])
        small = {n: chip.sb(ctx, n, s) for n, s in SMALL.items()}
        tanh_gate = chip.sb(ctx, "tanh_gate", [P, 1])
        region_a = chip.sb(ctx, "region_a", [P, 8 * 512 * 2])
        region_b = chip.sb(ctx, "region_b", [P, 2048 * 2 + 1024 * 3])
        sems = {n: ctx.enter_context(nc.semaphore("loaded_" + n)) for n in ("first", "small", "cx", "gelu", "alibi", "swiglu")}

        def cut(region, at, shape):
            n = 1
            for k in shape[1:]:
                n *= k
            v = region[0:shape[0], at:at + n]
            if len(shape) == 3:
                v = v.rearrange("p (a b) -> p a b", a=shape[1])
            if len(shape) == 4:
                v = v.rearrange("p (a b c) -> p a b c", a=shape[1], b=shape[2])
            return v

        large, at = {}, {"a": 0, "b": 0}
        for names, region, key in ((("cx_wqT", "cx_wkT", "cx_wv", "cx_wo"), region_b, "b"), (("g_w1", "g_w2"), region_a, "a")):
            for n in names:
                large[n] = cut(region, at[key], LARGE[n])
                at[key] += _free(LARGE[n])
        wo_scaled = cut(region_b, at["b"], [P, 8, P])
        large["alibi"] = cut(region_b, 0, LARGE["alibi"])
        a = 0
        for n in ("s_w1", "s_w3", "s_w2"):
            large[n] = cut(region_a, a, LARGE[n])
            a += _free(LARGE[n])

        first = ["ident", "heads8", "ta_gamma", "ta_wq", "ta_wk", "ta_wv", "ta_wo"]
        rest = [n for n in SMALL if n not in first]

        def load_block(queue, names, sem, wait=True):
            with nc.Block() as block:
                @block.scalar
                def _(act):
                    for names_, sem_ in queue:
                        for n in names_:
                            dst = small[n] if n in small else None
                            act.dma_start(dst[:] if dst is not None else large[n], weights_dram[n]).then_inc(sem_, 16)
                    if wait:
                        act.wait_ge(sem, 16 * len(names))

        load_block([(first, sems["first"]), (rest, sems["small"]),
                    (["cx_wqT", "cx_wkT", "cx_wv", "cx_wo"], sems["cx"]), (["g_w1", "g_w2"], sems["gelu"])], first, sems["first"])
        if x_state is not None:
            with nc.semaphore("x_state_loaded") as loaded, nc.Block() as block:
                @block.sync
                def _(sp):
                    sp.dma_start(X[:], x_state.rearrange("b t d -> t b d")).then_inc(loaded, 16)
                    sp.wait_ge(loaded, 16)
        consts = {n: small[n][:] for n in ("ident", "heads8", "heads16", "rank8", "rope")}
        consts["alibi"] = large["alibi"]
        if 1 in blocks:
            taylor_attention(chip, n_seq, x_dram, X, {"gamma": small["ta_gamma"][:], "wq": small["ta_wq"][:], "wk": small["ta_wk"][:],
                                                      "wv": small["ta_wv"][:], "wo": small["ta_wo"][:]}, consts)
            chip.clear_semaphores()
        with nc.Block() as block:
            @block.scalar
            def _(act):
                act.wait_ge(sems["small"], 16 * len(rest))
                act.wait_ge(sems["cx"], 16 * 4)
                act.activation(tanh_gate[:], small["cx_gate"][:], ACT.Tanh)
        if 2 in blocks:
            softmax_attention(chip, "wide", n_seq, X, ctxT_dram, {
                "wqT": large["cx_wqT"], "wkT": large["cx_wkT"], "wv": large["cx_wv"], "wo": large["cx_wo"], "wo_scaled": wo_scaled,
                "gamma": small["cx_gamma"][:], "beta": small["cx_beta"][:], "tanh_gate": tanh_gate[:], "bo": small["cx_bo"][:]}, consts)
            chip.clear_semaphores()
        load_block([(["alibi"], sems["alibi"])], ["g_w1", "g_w2"], sems["gelu"])
        if 3 in blocks:
            mixture(chip, "gelu", n_seq, X, out_dram if blocks[-1] == 3 else None, {
                "w1": large["g_w1"], "w2": large["g_w2"], "b1": small["g_b1"][:], "b2": small["g_b2"][:], "router": small["g_router"][:]}, consts)
            chip.clear_semaphores()
        load_block([(["s_w1", "s_w3", "s_w2"], sems["swiglu"])], ["alibi"], sems["alibi"])
        if 4 in blocks:
            softmax_attention(chip, "causal", n_seq, X, None, {
                "wq": small["sa_wq"][:], "wk": small["sa_wk"][:], "wv": small["sa_wv"][:], "wo": small["sa_wo"][:],
                "bq": small["sa_bq"][:], "bk": small["sa_bk"][:], "bv": small["sa_bv"][:], "bo": small["sa_bo"][:]}, consts)
            chip.clear_semaphores()
        if 5 in blocks:
            softmax_attention(chip, "rotary", n_seq, X, ctxT_dram, {
                "wq": small["ra_wq"][:], "wk": small["ra_wk"][:], "wv": small["ra_wv"][:], "wo": small["ra_wo"][:],
                "q_norm": small["ra_qn"][:], "k_norm": small["ra_kn"][:]}, consts)
            chip.clear_semaphores()
        with nc.Block() as block:
            @block.scalar
            def _(act):
                act.wait_ge(sems["swiglu"], 16 * 3)
        if 6 in blocks:
            mixture(chip, "swiglu", n_seq, X, out_dram, {
                "w1": large["s_w1"], "w3": large["s_w3"], "w2": large["s_w2"], "router": small["s_router"][:],
                "gate_bias": small["s_bias"][:]}, consts)
        if blocks[-1] not in (3, 6):
            with nc.semaphore("x_stored") as stored, nc.Block() as block:
                @block.sync
                def _(sp):
                    sp.dma_start(out_dram.rearrange("b t d -> t b d"), X[:]).then_inc(stored, 16)
                    sp.wait_ge(stored, 16)


def _free(shape):
    n = 1
    for k in shape[1:]:
        n *= k
    return n


def layouts(inputs, np):
    g = {k: np.asarray(v) for k, v in inputs.items()}

    def down(v):
        return v.reshape(-1, 1)

    def rows(v):
        return np.broadcast_to(v.reshape(1, -1), (P, v.size))

    def hidden_major(w1):
        return w1.transpose(2, 0, 1).reshape(P, -1)

    def chunks(w2):
        e, d, h = w2.shape
        return w2.transpose(0, 2, 1).reshape(e, h // P, P, d).transpose(2, 0, 1, 3)

    def strips(w):
        v = np.zeros((4, 32, 4, w.shape[-1]), w.dtype)
        v[:, :8] = w.reshape(4, 4, 8, -1).transpose(1, 2, 0, 3)
        return v.reshape(P, 4, -1)

    q = np.arange(P)
    slopes = np.power(np.float32(2.0), np.float32(-8.0) * np.arange(1, 17, dtype=np.float32) / np.float32(16))
    rel = np.abs(q[:, None] - q[None, :]).astype(np.float32)
    alibi = np.where((q[:, None] >= q[None, :])[:, None, :], -slopes[None, :, None] * rel[:, None, :], np.float32(-1e30))
    rope = np.zeros((P, 2, 2, 8), np.float32)
    for t, theta in enumerate((32.0, 1000.0)):
        freqs = np.power(np.float32(theta), -np.arange(0, 8, 2, dtype=np.float32) / np.float32(8))
        angle = np.arange(P, dtype=np.float32)[:, None] * freqs[None, :]
        rope[:, 0, t] = np.concatenate([np.cos(angle), np.cos(angle)], -1)
        rope[:, 1, t] = np.concatenate([-np.sin(angle), np.sin(angle)], -1)
    w_kv, x_kv = g["L0_attn_w_kv"], g["L0_xattn_w_kv"]
    return {
        "ident": np.eye(P, dtype=np.float32),
        "heads8": (q[:, None] // 16 == np.arange(8)[None, :]).astype(np.float32),
        "heads16": (q[:, None] // 8 == np.arange(16)[None, :]).astype(np.float32),
        "rank8": np.broadcast_to(np.arange(8, 0, -1).astype(np.float32)[None, :], (P, 8)),
        "rope": rope,
        "alibi": alibi.reshape(P, -1).astype(np.float32),
        "ta_gamma": down(g["L0_attn_gamma"]), "ta_wq": g["L0_attn_w_q"], "ta_wk": w_kv[:, :P], "ta_wv": w_kv[:, P:],
        "ta_wo": g["L0_attn_w_out"],
        "cx_gamma": down(g["L0_xattn_ln_gamma"]), "cx_beta": down(g["L0_xattn_ln_beta"]),
        "cx_gate": rows(g["L0_xattn_gate"]), "cx_bo": rows(g["L0_xattn_b_out"]),
        "cx_wqT": g["L0_xattn_w_q"].T.reshape(16, 64, P).transpose(1, 0, 2),
        "cx_wkT": x_kv[:, :1024].T.reshape(16, 64, P).transpose(1, 0, 2),
        "cx_wv": x_kv[:, 1024:], "cx_wo": g["L0_xattn_w_out"].reshape(8, P, P).transpose(1, 0, 2),
        "g_router": g["L0_ffn_Wr"].T, "g_w1": hidden_major(g["L0_ffn_W1"]), "g_w2": chunks(g["L0_ffn_W2"]),
        "g_b1": g["L0_ffn_b1"].reshape(8, 4, P).transpose(2, 0, 1), "g_b2": g["L0_ffn_b2"],
        "sa_wq": g["L1_attn_Wq"].T, "sa_wk": g["L1_attn_Wk"].T, "sa_wv": g["L1_attn_Wv"].T, "sa_wo": strips(g["L1_attn_Wo"].T),
        "sa_bq": down(g["L1_attn_bq"]), "sa_bk": down(g["L1_attn_bk"]), "sa_bv": strips(g["L1_attn_bv"].reshape(P, 1)).reshape(P, 4), "sa_bo": rows(g["L1_attn_bo"]),
        "ra_wq": g["L1_xattn_Wq"].T, "ra_wk": g["L1_xattn_Wk"].T, "ra_wv": g["L1_xattn_Wv"].T, "ra_wo": strips(g["L1_xattn_Wo"].T),
        "ra_qn": rows(g["L1_xattn_q_norm_w"]), "ra_kn": rows(g["L1_xattn_k_norm_w"]),
        "s_router": g["L1_ffn_gate_w"].T, "s_bias": rows(g["L1_ffn_gate_bias"]),
        "s_w1": hidden_major(np.concatenate([g["L1_ffn_w1"], g["L1_ffn_sw1"][None]])),
        "s_w3": hidden_major(np.concatenate([g["L1_ffn_w3"], g["L1_ffn_sw3"][None]])),
        "s_w2": chunks(np.concatenate([g["L1_ffn_w2"], g["L1_ffn_sw2"][None]])),
    }


def kernel(**inputs):
    import numpy as np
    import concourse.bacc as bacc
    from concourse.bass_utils import run_bass_kernel_spmd

    nc = bacc.Bacc("TRN2", target_bir_lowering=False, num_devices=1)
    arrays = {n: np.ascontiguousarray(a) for n, a in layouts(inputs, np).items()}
    arrays["x"] = np.ascontiguousarray(inputs["x"])
    arrays["ctxT"] = np.ascontiguousarray(np.asarray(inputs["ctx_1024"]).transpose(2, 0, 1))
    arrays = {"in_" + n: a for n, a in arrays.items()}
    dram = {n: nc.dram_tensor(n, list(a.shape), F32, kind="ExternalInput").ap() for n, a in arrays.items()}
    n_seq = arrays["in_x"].shape[0]
    out = nc.dram_tensor("out", [n_seq, P, P], F32, kind="ExternalOutput").ap()
    build(nc, n_seq, dram["in_x"], dram["in_ctxT"], {n[3:]: a for n, a in dram.items()}, out)
    result = run_bass_kernel_spmd(nc, [arrays], core_ids=[0])
    return result.results[0]["out"]
```

```python
from contextlib import ExitStack

import concourse.bass as bass
from concourse import mybir

P = 128
F32 = mybir.dt.float32
ALU = mybir.AluOpType
ACT = mybir.ActivationFunctionType
AX = mybir.AxisListType
CONTEXT = 77
PEEL = 4
LN_EPS = 1e-5
F32R = mybir.dt.float32r
I32 = mybir.dt.int32
HIGH = -4096
NEWTON = 3
SEED_SCALE = 1.8352578e-20


class At:

    def __init__(self, c, i=None, unroll=4, peel=PEEL):
        self.c, self.i, self.unroll, self.peel = c, i, unroll, peel

    def back(self, n):
        return At(self.c - n, self.i, self.unroll, self.peel)

    @property
    def real(self):
        return self.c >= 0 if self.i is None else self.c + self.peel >= 0

    def count(self, per, k):
        assert self.real
        v = self.c * per + k
        return v if self.i is None else self.i * (self.unroll * per) + v

    def load(self, slots):
        v = 16 * (self.c // slots + 1)
        return v if self.i is None else self.i * (16 * self.unroll // slots) + v

    def index(self, scale=1, plus=0):
        v = self.c * scale + plus
        return v if self.i is None else self.i * (self.unroll * scale) + v


def run_steps(engine, step, units, stages, unroll, peel=PEEL):
    for t in range(peel):
        step(*[At(t - s, None, unroll) if 0 <= t - s < units else None for s in range(stages)])
    with engine.Fori(peel // unroll, units // unroll) as i:
        for t in range(unroll):
            step(*[At(t - s, i, unroll, peel) for s in range(stages)])
    for t in range(units, units + stages - 1):
        step(*[At(t - s, None, unroll) if 0 <= t - s < units else None for s in range(stages)])


class Chip:

    def __init__(self, nc, ctx):
        self.nc, self.used = nc, []
        self.banks = ctx.enter_context(nc.psum_tensor("banks", [P, 8, 512], F32))

    def sb(self, ctx, name, shape, dt=F32):
        return ctx.enter_context(self.nc.sbuf_tensor(name, shape, dt))

    def sem(self, ctx, name):
        self.used.append(ctx.enter_context(self.nc.semaphore(name)))
        return self.used[-1]

    def clear_semaphores(self):
        used, self.used = self.used, []
        with self.nc.Block() as block:
            @block.gpsimd
            def _(pool):
                for s in used:
                    pool.sem_clear(s)


def taylor_attention(chip, n_seq, X, w, consts):
    nc = chip.nc
    H, D = 8, 16
    with ExitStack() as ctx:
        def sb(name, shape):
            return chip.sb(ctx, "taylor_" + name, shape)

        def sem(name):
            return chip.sem(ctx, "taylor_" + name)

        wq, wk, wv = (sb(n, [P, P]) for n in ("wq", "wk", "wv"))
        ones = sb("ones", [P, P])
        power, eps = sb("power", [P, 1]), sb("eps", [P, 1])
        squares = sb("squares", [P, P])
        sumsq = sb("sumsq", [P, 4])
        guarded = sb("guarded", [P, 4])
        inv_norm = sb("inv_norm", [P, 4])
        xs = sb("xs", [P, 2, P])
        xsT = sb("xsT", [P, 2, P])
        q_masked = sb("q_masked", [P, 2, H, P])
        kT = sb("kT", [P, 2, P])
        v_one = sb("v_one", [P, 4, H, D + 1])
        weights = sb("weights", [P, 2, 2, 4, P])
        den = sb("den", [P, 2, H])
        inv_den = sb("inv_den", [P, 2, H])
        o = sb("o", [P, 2, P])
        oT = sb("oT", [P, 2, P])
        z = sb("z", [P, 4, P])
        stats = sb("stats", [P, 6])
        mean_var = sb("mean_var", [P, 4, 2])
        var_eps = sb("var_eps", [P, 4])
        rstd = sb("rstd", [P, 4])
        xsT_bank, q_bank, kv_bank, o_bank, oT_bank, y_bank = (chip.banks[:, n] for n in (0, 1, 2, 5, 6, 7))
        s_bank = [chip.banks[:, 3], chip.banks[:, 4]]

        power_ready, ready = sem("power_ready"), sem("ready")
        sumsq_done, guarded_done, inv_norm_done, xs_done, xsT_ps, xsT_done = (
            sem(n) for n in ("sumsq_done", "guarded_done", "inv_norm_done", "xs_done", "xsT_ps", "xsT_done"))
        q_ps, kv_ps, q_done, k_done, v_done, s_ps, weights_done = (
            sem(n) for n in ("q_ps", "kv_ps", "q_done", "k_done", "v_done", "s_ps", "weights_done"))
        o_ps, den_done, inv_den_done, o_done, oT_ps, oT_done, y_ps = (
            sem(n) for n in ("o_ps", "den_done", "inv_den_done", "o_done", "oT_ps", "oT_done", "y_ps"))
        z_done, stats_done, mean_done, var_done, rstd_done, x_written = (
            sem(n) for n in ("z_done", "stats_done", "mean_done", "var_done", "rstd_done", "x_written"))
        block = ctx.enter_context(nc.Block())

        @block.gpsimd
        def _(pool):
            pool.memset(power[:], -0.5).then_inc(power_ready, 1)
            pool.memset(eps[:], LN_EPS).then_inc(power_ready, 1)
            pool.wait_ge(power_ready, 2)

            def step(a, f, c, p, u, n):
                if a is not None:
                    s = a.c % 4
                    pool.wait_ge(sumsq_done, a.count(1, 1))
                    pool.nop(nofuse=True)
                    pool.tensor_scalar(guarded[:, s:s + 1], sumsq[:, s:s + 1], 1e-24, None, ALU.max).then_inc(guarded_done, 1)
                    pool.wait_ge(guarded_done, a.count(1, 1))
                    pool.tensor_tensor(inv_norm[:, s:s + 1], guarded[:, s:s + 1], power[:], ALU.pow).then_inc(inv_norm_done, 1)
                if u is not None:
                    s = u.c % 4
                    pool.wait_ge(mean_done, u.count(1, 1))
                    pool.tensor_tensor(var_eps[:, s:s + 1], mean_var[:, s, 1:2], eps[:], ALU.add).then_inc(var_done, 1)
                    pool.wait_ge(var_done, u.count(1, 1))
                    pool.tensor_tensor(rstd[:, s:s + 1], var_eps[:, s:s + 1], power[:], ALU.pow).then_inc(rstd_done, 1)

            run_steps(pool, step, n_seq, 6, 4, 2 * PEEL)

        @block.scalar
        def _(act):
            def step(a, f, c, p, u):
                if c is not None:
                    if c.back(2).real:
                        act.wait_ge(o_ps, c.back(2).count(1, 1))
                    for j in range(2):
                        act.wait_ge(s_ps, c.count(2, j + 1))
                        act.activation(weights[:, c.c % 2, j], s_bank[j].rearrange("p (h q) -> p h q", h=4), ACT.Square,
                                       bias=1.0, scale=0.25).then_inc(weights_done, 1)
                if f is not None:
                    act.wait_ge(xsT_ps, f.count(1, 1))
                    act.activation(xsT[:, f.c % 2], xsT_bank[:, 0:P], ACT.Copy).then_inc(xsT_done, 1)
                if u is not None:
                    act.wait_ge(oT_ps, u.count(1, 1))
                    act.activation(oT[:, u.c % 2], oT_bank[:, 0:P], ACT.Copy).then_inc(oT_done, 1)
                if f is not None:
                    s = f.c % 2
                    act.wait_ge(kv_ps, f.count(1, 1))
                    act.activation(kT[:, s], kv_bank[:, 0:P], ACT.Copy).then_inc(k_done, 1)
                    act.activation(v_one[:, f.c % 4, :, 0:D], kv_bank[:, P:2 * P].rearrange("p (h d) -> p h d", h=H),
                                   ACT.Copy).then_inc(v_done, 1)
                if a is not None:
                    s = a.c % 4
                    if a.back(4).real:
                        act.wait_ge(inv_norm_done, a.back(4).count(1, 1))
                    act.activation(squares[:], X[:, a.index(), :], ACT.Square, accum_out=sumsq[:, s:s + 1]).then_inc(sumsq_done, 1)

            run_steps(act, step, n_seq, 5, 4, 2 * PEEL)

        @block.vector
        def _(dve):
            for t, name in ((wq, "wq"), (wk, "wk"), (wv, "wv")):
                dve.tensor_scalar(t[:], w[name], w["gamma"], float(P) ** 0.5, ALU.mult, ALU.mult).then_inc(ready, 1)
            dve.memset(ones[:], 1.0).then_inc(ready, 1)
            dve.memset(v_one[:], 1.0).then_inc(ready, 1)

            def step(a, f, c, p, u, n):
                if f is not None:
                    dve.wait_ge(inv_norm_done, f.count(1, 1))
                    dve.tensor_scalar(xs[:, f.c % 2], X[:, f.index(), :], inv_norm[:, f.c % 4:f.c % 4 + 1], None,
                                      ALU.mult).then_inc(xs_done, 1)
                if n is not None:
                    s = n.c % 4
                    dve.wait_ge(rstd_done, n.count(1, 1))
                    dve.tensor_scalar(X[:, n.index(), :], z[:, s], mean_var[:, s, 0:1], rstd[:, s:s + 1],
                                      ALU.subtract, ALU.mult).then_inc(x_written, 1)
                if f is not None:
                    s = f.c % 2
                    dve.wait_ge(q_ps, f.count(1, 1))
                    if f.back(2).real:
                        dve.wait_ge(s_ps, f.back(2).count(2, 2))
                    dve.tensor_tensor(q_masked[:, s], q_bank[:, 0:P].unsqueeze(1).to_broadcast([P, H, P]),
                                      consts["heads8"].unsqueeze(2).to_broadcast([P, H, P]), ALU.mult).then_inc(q_done, 1)
                if p is not None:
                    s = p.c % 2
                    sums = o_bank[:, 0:H * (D + 1)].rearrange("p (h d) -> p h d", h=H)
                    dve.wait_ge(o_ps, p.count(1, 1))
                    dve.tensor_scalar(den[:, s], sums[:, :, D], 2e-5, None, ALU.max).then_inc(den_done, 1)
                    dve.wait_ge(den_done, p.count(1, 1))
                    dve.reciprocal(inv_den[:, s], den[:, s]).then_inc(inv_den_done, 1)
                    dve.wait_ge(inv_den_done, p.count(1, 1))
                    dve.tensor_tensor(o[:, s].rearrange("p (h d) -> p h d", h=H), sums[:, :, 0:D],
                                      inv_den[:, s].unsqueeze(2).to_broadcast([P, H, D]), ALU.mult).then_inc(o_done, 1)
                if u is not None:
                    s = u.c % 4
                    dve.wait_ge(y_ps, u.count(1, 1))
                    dve.tensor_tensor(z[:, s], y_bank[:, 0:P], X[:, u.index(), :], ALU.add).then_inc(z_done, 1)
                    dve.wait_ge(z_done, u.count(1, 1))
                    dve.bn_stats(stats[:], z[:, s]).then_inc(stats_done, 1)
                    dve.wait_ge(stats_done, u.count(1, 1))
                    dve.nop(nofuse=True)
                    dve.bn_aggr(mean_var[:, s], stats[:]).then_inc(mean_done, 1)

            run_steps(dve, step, n_seq, 6, 4, 2 * PEEL)

        @block.tensor
        def _(pe):
            pe.wait_ge(ready, 5)
            ident = consts["ident"]

            def sum_heads(p, heads):
                for h in heads:
                    last = pe.matmul(o_bank[:, h * (D + 1):(h + 1) * (D + 1)], weights[:, p.c % 2, h // 4, h % 4], v_one[:, p.c % 4, h],
                                     start=False, stop=h == H - 1, skip_group_check=True)
                return last

            def step(a, f, c, p, u):
                if c is not None:
                    s = c.c % 2
                    pe.wait_ge(q_done, c.count(1, 1))
                    pe.wait_ge(k_done, c.count(1, 1))
                    for j in range(2):
                        if c.back(1).real:
                            pe.wait_ge(weights_done, c.back(1).count(2, j + 1))
                        pe.matmul(s_bank[j], kT[:, s], q_masked[:, s, 4 * j:4 * j + 4], start=True, stop=True).then_inc(s_ps, 1)
                if f is not None:
                    pe.wait_ge(xs_done, f.count(1, 1))
                    if f.back(1).real:
                        pe.wait_ge(xsT_done, f.back(1).count(1, 1))
                    pe.transpose(xsT_bank[:, 0:P], xs[:, f.c % 2], ident).then_inc(xsT_ps, 1)
                if u is not None:
                    pe.wait_ge(o_done, u.count(1, 1))
                    if u.back(1).real:
                        pe.wait_ge(oT_done, u.back(1).count(1, 1))
                    pe.transpose(oT_bank[:, 0:P], o[:, u.c % 2], ident).then_inc(oT_ps, 1)
                if p is not None:
                    pe.wait_ge(v_done, p.count(1, 1))
                    if p.back(1).real:
                        pe.wait_ge(o_done, p.back(1).count(1, 1))
                    pe.matmul(o_bank[:, 0:H * (D + 1)], ones[:], v_one[:, p.c % 4].rearrange("p h d -> p (h d)"),
                              start=True, stop=False, skip_group_check=True)
                    pe.wait_ge(weights_done, p.count(2, 2))
                    sum_heads(p, range(4))
                if f is not None:
                    s = f.c % 2
                    pe.wait_ge(xsT_done, f.count(1, 1))
                    if f.back(1).real:
                        pe.wait_ge(q_done, f.back(1).count(1, 1))
                        pe.wait_ge(v_done, f.back(1).count(1, 1))
                    pe.matmul(q_bank[:, 0:P], wq[:], xsT[:, s], start=True, stop=True).then_inc(q_ps, 1)
                    pe.matmul(kv_bank[:, 0:P], wk[:], xsT[:, s], start=True, stop=True)
                    pe.matmul(kv_bank[:, P:2 * P], xsT[:, s], wv[:], start=True, stop=True).then_inc(kv_ps, 1)
                if p is not None:
                    sum_heads(p, range(4, H)).then_inc(o_ps, 1)
                if u is not None:
                    pe.wait_ge(oT_done, u.count(1, 1))
                    if u.back(1).real:
                        pe.wait_ge(z_done, u.back(1).count(1, 1))
                    pe.matmul(y_bank[:, 0:P], oT[:, u.c % 2], w["wo"], start=True, stop=True).then_inc(y_ps, 1)

            run_steps(pe, step, n_seq, 5, 4, 2 * PEEL)


def softmax_attention(chip, kind, n_seq, X, ctxT_dram, w, consts):
    nc = chip.nc
    H = 16
    D = 64 if kind == "wide" else 8
    NK = P if kind == "causal" else CONTEXT
    HU = 4
    UB = H // HU
    NU = 2 * UB
    OG = NU // 2
    n_pairs = n_seq // 2
    FU = {"wide": 11, "causal": 4, "rotary": 4}[kind]
    STRIP = 64 if kind == "wide" else 32
    CU = HU * STRIP // P
    NC = UB * CU
    SLOTS = 2
    with ExitStack() as ctx:
        def sb(name, shape):
            return chip.sb(ctx, kind + "_" + name, shape)

        def sem(name):
            return chip.sem(ctx, kind + "_" + name)

        power = sb("power", [P, 64])
        eps = sb("eps", [P, 2])
        xin = sb("xin", [P, 4, 2, P])
        xT = sb("xT", [P, 2, 2, P])
        values = sb("values", [P, 2, 2, H, STRIP])
        keys = sb("keys", [P, 2, H, 2, NK] if kind == "wide" else [P, 2, H, NK])
        exps = sb("exps", [P, SLOTS, HU, NK])
        exp_sum = sb("exp_sum", [P, SLOTS, HU])
        inv_sum = sb("inv_sum", [P, SLOTS, HU])
        probs = sb("probs", [P, SLOTS, HU, NK])
        probsT = sb("probsT", [P, 2, HU * P])
        neg_max = sb("neg_max", [P, SLOTS, HU])
        oT = sb("oT", [P, 2, 2, NC, P])
        residual = sb("residual", [P, 2, 2, P])
        z = sb("z", [P, 4, 2, P])
        stats = sb("stats", [P, 2, 6])
        mean_var = sb("mean_var", [P, 4, 2, 2])
        var_eps = sb("var_eps", [P, 4, 2])
        rstd = sb("rstd", [P, 4, 2])
        if kind != "causal":
            ctxT = sb("ctxT", [P, 4, 2, P])
        if kind == "wide":
            xn = sb("xn", [P, 2, P])
            pre_stats = sb("pre_stats", [P, 2, 6])
            pre_mean_var = sb("pre_mean_var", [P, 2, 2])
            pre_var_eps = sb("pre_var_eps", [P, 2])
            pre_rstd = sb("pre_rstd", [P, 2])
            product = sb("product", [P, H, P])
        else:
            qT = sb("qT", [P, 2, 2, P])
            kT = sb("kT", [P, 2, 2, P])
        if kind == "rotary":
            qk = sb("qk", [P, 2, 2, H, 8])
            qk_sq = sb("qk_sq", [P, 4, H, 8])
            qk_sum = sb("qk_sum", [P, 4 * H])
            root_part = sb("root_part", [P, 4 * H])
            qk_rstd = sb("qk_rstd", [P, 4 * H])
            turned = sb("turned", [P, 4, H, 8])
            crossed = sb("crossed", [P, 4, H, 8])
            table = sb("table", [P, 2, 2, 8])
        if kind == "causal":
            biased = sb("biased", [P, SLOTS, HU * NK])
            value_row = sb("value_row", [P, NC, P])
            q_bias = sb("q_bias", [P, 1])
        extra = sb("extra", [P, P])

        s_bank = [chip.banks[:, 0], chip.banks[:, 1]]
        p_bank = [chip.banks[:, 2], chip.banks[:, 3]]
        o_bank = [chip.banks[:, 4], chip.banks[:, 5]]
        f_bank, y_bank = chip.banks[:, 6], chip.banks[:, 7]

        x_loaded = [sem(f"x_loaded{n}") for n in range(4)]
        ready, prepared, prepared_ps, product_done = (sem(n) for n in ("ready", "prepared", "prepared_ps", "product_done"))
        READY = 4
        ROOT = 3 + 3 * NEWTON
        PREPARED = {"wide": 2, "causal": 3, "rotary": 6}[kind]
        front_ps, front_done = sem("front_ps"), sem("front_done")
        keys_done = [sem("keys_done_even"), sem("keys_done_odd")]
        s_ps, max_done, exps_done, inv_done, probs_done = (
            sem(n) for n in ("s_ps", "max_done", "exps_done", "inv_done", "probs_done"))
        biased_done = sem("biased_done")
        probsT_ps, probsT_done, pv_done = (sem(n) for n in ("probsT_ps", "probsT_done", "pv_done"))
        o_done, y_ps, residual_done = (sem(n) for n in ("o_done", "y_ps", "residual_done"))
        z_done, stats_done, mean_done, var_done, rstd_done, x_written = (
            sem(n) for n in ("z_done", "stats_done", "mean_done", "var_done", "rstd_done", "x_written"))
        pre_done, pre_var_done, pre_rstd_done, turn_done = (
            sem(n) for n in ("pre_done", "pre_var_done", "pre_rstd_done", "turn_done"))
        square_done, qk_rstd_done, scaled_done = (sem(n) for n in ("square_done", "qk_rstd_done", "scaled_done"))
        block = ctx.enter_context(nc.Block())
        TURNS = 3
        POOL_KEYS, DVE_KEYS = ((0,), (1,)) if kind == "causal" else ((0, 1), ())
        MLAG = 1
        KEYS_LEAD = 3 if kind == "causal" else 2

        def lagged(c, u, k, lag):
            if k - lag >= 0:
                return (c, k - lag) if c is not None else None
            return (u, k - lag + NU) if u is not None else None

        def before(pair, k, n):
            pair = pair.back((n - k + NU - 1) // NU) if n > k else pair
            return (pair, (k - n) % NU) if pair.real else None

        @block.sync
        def _(sp):
            def step(f):
                if f is None:
                    return
                s = f.c % 4
                if f.back(4).real:
                    sp.wait_ge(z_done, f.back(4).count(1, 1))
                sp.dma_start(xin[:, s], X[:, bass.ds(f.index(2), 2), :]).then_inc(x_loaded[s], 16)
                if kind != "causal":
                    sp.dma_start(ctxT[:, s, :, 0:NK], ctxT_dram[:, bass.ds(f.index(2), 2), :]).then_inc(x_loaded[s], 16)

            if kind != "causal":
                sp.wait_ge(ready, READY)
            run_steps(sp, step, n_pairs, 1, 4)

        def wait_loaded(engine, f):
            m = 2 if kind != "causal" else 1
            v = 16 * m * (f.c // 4 + 1)
            engine.wait_ge(x_loaded[f.c % 4], v if f.i is None else f.i * (16 * m) + v)

        def make_keys(engine, pair, piece):
            engine.wait_ge(front_done, pair.count(FU, 3 if kind == "rotary" else 2))
            if pair.back(1).real:
                engine.wait_ge(s_ps, pair.back(1).count(NU, piece + 1))
            b, j = divmod(piece, UB)
            heads = slice(HU * j, HU * (j + 1))
            engine.tensor_tensor(keys[:, b, heads], kT[:, pair.c % 2, b, 0:NK].unsqueeze(1).to_broadcast([P, HU, NK]),
                                 consts["heads16"][:, heads].unsqueeze(2).to_broadcast([P, HU, NK]),
                                 ALU.mult).then_inc(keys_done[piece % 2], 1)

        def keys_ahead(engine, f, c, k, pieces):
            pair, piece = (f, k - NU + KEYS_LEAD) if k >= NU - KEYS_LEAD else (c, k + KEYS_LEAD)
            if pair is not None and piece % 2 in pieces:
                make_keys(engine, pair, piece)

        @block.gpsimd
        def _(pool):
            pool.memset(power[:], -0.5).then_inc(ready, 1)
            pool.memset(values[:], 0.0).then_inc(ready, 1)
            pool.memset(eps[:, 0:2], LN_EPS).then_inc(ready, 1)
            pool.memset(value_row[:] if kind == "causal" else ctxT[:], 1.0 if kind == "causal" else 0.0).then_inc(ready, 1)
            pool.wait_ge(ready, READY)
            pool.wait_ge(prepared, PREPARED)

            def rotate(f, seq):
                for which, out, a, b, src in ((0, turned, 0, 8, 0), (1, crossed, 0, 4, 4), (1, crossed, 4, 8, 0)):
                    last = pool.tensor_tensor(out[:, 2 * seq:2 * seq + 2, :, a:b], qk[:, seq, :, :, src:src + b - a],
                                              table[:, which, :, a:b].unsqueeze(2).to_broadcast([P, 2, H, b - a]), ALU.mult)
                last.then_inc(turn_done, 1)

            def add_halves(f):
                pool.wait_ge(turn_done, f.count(TURNS, 2))
                pool.tensor_tensor(crossed[:], turned[:], crossed[:], ALU.add).then_inc(turn_done, 1)

            def step(f, c, u, n):
                for k in range(NU):
                    if kind != "wide":
                        keys_ahead(pool, f, c, k, POOL_KEYS)
                    at = lagged(c, u, k, MLAG)
                    if at is not None:
                        pair, m = at
                        pool.wait_ge(inv_done, pair.count(NU, m + 1))
                        if before(pair, m, SLOTS) is not None:
                            bc, bk = before(pair, m, SLOTS)
                            pool.wait_ge(probsT_ps, bc.count(NU, bk + 1))
                        pool.tensor_tensor(probs[:, m % SLOTS], exps[:, m % SLOTS],
                                           inv_sum[:, m % SLOTS].unsqueeze(2).to_broadcast([P, HU, NK]), ALU.mult).then_inc(probs_done, 1)
                    if f is not None and kind == "wide" and k == 1:
                        pool.wait_ge(pre_done, f.count(4, 4))
                        pool.tensor_tensor(pre_var_eps[:], pre_mean_var[:, :, 1], eps[:], ALU.add).then_inc(pre_var_done, 1)
                        pool.wait_ge(pre_var_done, f.count(1, 1))
                        pool.tensor_tensor(pre_rstd[:], pre_var_eps[:], power[:, 0:2], ALU.pow).then_inc(pre_rstd_done, 1)
                    if f is not None and kind == "rotary" and k in (1, 2):
                        pool.wait_ge(front_done, f.count(FU, 2))
                        if f.back(1).real:
                            pool.wait_ge(scaled_done, f.back(1).count(1, 1))
                        rotate(f, k - 1)
                    if f is not None and kind == "rotary" and k == 3:
                        add_halves(f)
                    if c is not None and kind != "rotary" and k == 3:
                        wait_loaded(pool, c)
                        if c.back(2).real:
                            pool.wait_ge(z_done, c.back(2).count(1, 1))
                        pool.tensor_tensor(residual[:, c.c % 2], xin[:, c.c % 4], extra[:].unsqueeze(1).to_broadcast([P, 2, P]),
                                           ALU.add).then_inc(residual_done, 1)
                    if n is not None and k == 0:
                        s = n.c % 4
                        pool.wait_ge(mean_done, n.count(2, 2))
                        pool.tensor_tensor(var_eps[:, s], mean_var[:, s, :, 1], eps[:], ALU.add).then_inc(var_done, 1)
                        pool.wait_ge(var_done, n.count(1, 1))
                        pool.tensor_tensor(rstd[:, s], var_eps[:, s], power[:, 0:2], ALU.pow).then_inc(rstd_done, 1)

            run_steps(pool, step, n_pairs, 4, 4)

        ident = consts["ident"]

        def front_pe(pe, f, m):
            s2, s4 = f.c % 2, f.c % 4
            if m == (10 if kind == "wide" else 0):
                if kind == "wide":
                    pe.wait_ge(turn_done, f.count(2, 2))
                else:
                    wait_loaded(pe, f)
                for b in range(2):
                    last = pe.transpose(f_bank[:, b * P:(b + 1) * P], xn[:, b] if kind == "wide" else xin[:, s4, b], ident)
                return last
            if kind == "wide":
                if m <= 5:
                    first = 3 * m
                    wait_loaded(pe, f)
                    for n in range(min(3, H - first)):
                        last = pe.matmul(f_bank[:, n * 2 * NK:(n + 1) * 2 * NK], product[:, first + n], ctxT[:, s4, :, 0:NK],
                                         start=True, stop=True)
                else:
                    b, half = divmod(m - 6, 2)
                    last = pe.matmul(f_bank[0:NK, :], ctxT[:, s4, b, 0:NK], w["wv"][:, half * 512:(half + 1) * 512],
                                     start=True, stop=True)
                return last
            pe.wait_ge(front_done, f.count(FU, 1))
            if kind == "causal":
                if m == 3:
                    for b in range(2):
                        last = pe.matmul(f_bank[:, b * P:(b + 1) * P], xT[:, s2, b], w["wv"], start=True, stop=True)
                    return last
                return pe.matmul(f_bank[:, 0:2 * P], w["wk"] if m == 1 else w["wq"], xT[:, s2], start=True, stop=True)
            if m == 1:
                for b in range(2):
                    pe.matmul(f_bank[:, 2 * b * P:(2 * b + 1) * P], xT[:, s2, b], w["wq"], start=True, stop=True)
                    last = pe.matmul(f_bank[:, (2 * b + 1) * P:(2 * b + 2) * P], ctxT[:, s4, b], w["wk"], start=True, stop=True)
            elif m == 3:
                for b in range(2):
                    last = pe.matmul(f_bank[0:NK, b * P:(b + 1) * P], ctxT[:, s4, b, 0:NK], w["wv"], start=True, stop=True)
            else:
                pe.wait_ge(scaled_done, f.count(1, 1))
                for n in range(4):
                    last = pe.transpose(f_bank[:, n * P:(n + 1) * P], turned[:, n].rearrange("p h d -> p (h d)"), ident)
            return last

        def front_act(act, f, m):
            s2 = f.c % 2
            copy = ACT.Copy
            if kind == "wide":
                if m == 10:
                    return act.activation(xT[:, s2], f_bank[:, 0:2 * P].rearrange("p (b q) -> p b q", b=2), ACT.Identity,
                                          scale=w["gamma"], bias=w["beta"])
                if m <= 5:
                    first = 3 * m
                    n = min(3, H - first)
                    return act.activation(keys[:, s2, first:first + n],
                                          f_bank[:, 0:n * 2 * NK].rearrange("p (h b k) -> p h b k", h=n, b=2), copy)
                b, half = divmod(m - 6, 2)
                return act.activation(values[0:NK, s2, b, 8 * half:8 * half + 8, 0:D],
                                      f_bank[0:NK, :].rearrange("p (h d) -> p h d", h=8), copy)
            if m == 0:
                return act.activation(xT[:, s2], f_bank[:, 0:2 * P].rearrange("p (b q) -> p b q", b=2), copy)
            if kind == "causal":
                two = f_bank[:, 0:2 * P].rearrange("p (b q) -> p b q", b=2)
                if m == 1:
                    if f.back(2).real:
                        for done in keys_done:
                            act.wait_ge(done, f.back(2).count(NU // 2, NU // 2))
                    return act.activation(kT[:, s2], two, ACT.Identity, bias=w["bk"])
                if m == 2:
                    return act.activation(qT[:, s2], two, ACT.Identity, bias=q_bias[:], scale=8.0 ** -0.5)
                return act.activation(values[:, s2, :, :, 0:D], f_bank[:, 0:2 * P].rearrange("p (b h d) -> p b h d", b=2, h=H), copy)
            if m == 1:
                if f.back(1).real:
                    act.wait_ge(turn_done, f.back(1).count(TURNS, 1))
                    act.wait_ge(square_done, f.back(1).count(1, 1))
                act.activation(qk_sq[:].rearrange("p n h d -> p (n h d)"), f_bank, ACT.Square)
                return act.activation(qk[:].rearrange("p b t h d -> p (b t h d)"), f_bank, copy)
            if m == 3:
                return act.activation(values[0:NK, s2, :, :, 0:D],
                                      f_bank[0:NK, 0:2 * P].rearrange("p (b h d) -> p b h d", b=2, h=H), copy)
            if f.back(2).real:
                for done in keys_done:
                    act.wait_ge(done, f.back(2).count(NU // 2, NU // 2))
            four = f_bank.rearrange("p (b t q) -> p b t q", b=2, t=2)
            act.activation(qT[:, s2], four[:, :, 0], copy)
            return act.activation(kT[:, s2], four[:, :, 1], copy)

        FRONT_AT = {"wide": [(0, 0), (0, 1), (1, 0), (2, 0), (3, 0), (4, 0), (5, 0), (5, 1), (6, 0), (6, 1), (7, 0)],
                    "causal": [(0, 0), (1, 0), (3, 0), (5, 0)], "rotary": [(0, 0), (1, 0), (6, 0), (7, 0)]}[kind]
        TLAG, PLAG, OLAG = 3, 4, 5
        Y_AT, Z_AT = 6, 7

        @block.tensor
        def _(pe):
            pe.wait_ge(ready, READY)
            if kind == "wide":
                for n in range(UB):
                    if n >= 2:
                        pe.wait_ge(product_done, n - 1)
                    for h in range(HU):
                        last = pe.matmul((f_bank, y_bank)[n % 2][:, h * P:(h + 1) * P], w["wkT"][:, HU * n + h], w["wqT"][:, HU * n + h],
                                         start=True, stop=True)
                    last.then_inc(prepared_ps, 1)
                pe.wait_ge(product_done, UB)
                pe.wait_ge(prepared, PREPARED)
            elif kind == "causal":
                pe.wait_ge(prepared, 1)
                for n in range(NC):
                    last = pe.matmul(f_bank[:, 0:P], value_row[:, n], w["wo"][:, n], start=n == 0, stop=n == NC - 1)
                last.then_inc(prepared_ps, 1)
                pe.wait_ge(prepared, PREPARED)
            else:
                pe.wait_ge(prepared, PREPARED)

            def front(f, k, place):
                for m in range(FU):
                    if FRONT_AT[m] == (k, place):
                        if m >= 1:
                            pe.wait_ge(front_done, f.count(FU, m))
                        elif f.back(1).real:
                            pe.wait_ge(front_done, f.back(1).count(FU, FU))
                        front_pe(pe, f, m).then_inc(front_ps, 1)

            def project(u):
                pe.wait_ge(o_done, u.count(OG, OG))
                if u.back(1).real:
                    pe.wait_ge(z_done, u.back(1).count(1, 1))
                for b in range(2):
                    for n in range(NC):
                        last = pe.matmul(y_bank[:, b * P:(b + 1) * P], oT[:, u.c % 2, b, n],
                                         w["wo_scaled" if kind == "wide" else "wo"][:, n], start=n == 0, stop=n == NC - 1)
                last.then_inc(y_ps, 1)

            def step(f, c, u):
                for k in range(NU):
                    if c is not None:
                        b, j = divmod(k, UB)
                        if k == 0:
                            pe.wait_ge(front_done, c.count(FU, FU))
                        if kind != "wide":
                            pe.wait_ge(keys_done[k % 2], c.count(NU // 2, k // 2 + 1))
                        if before(c, k, 2) is not None:
                            bc, bk = before(c, k, 2)
                            pe.wait_ge(biased_done if kind == "causal" else exps_done, bc.count(NU, bk + 1))
                        if kind == "wide":
                            q = xT[:, c.c % 2, b]
                            moving = keys[:, c.c % 2, HU * j:HU * j + HU, b]
                        else:
                            q = qT[:, c.c % 2, b]
                            moving = keys[:, b, HU * j:HU * j + HU]
                        pe.matmul(s_bank[k % 2][:, 0:HU * NK], q, moving, start=True, stop=True).then_inc(s_ps, 1)
                    at = lagged(c, u, k, TLAG)
                    if at is not None:
                        pair, n = at
                        pe.wait_ge(probs_done, pair.count(NU, n + 1))
                        if before(pair, n, 2) is not None:
                            bc, bk = before(pair, n, 2)
                            pe.wait_ge(probsT_done, bc.count(NU, bk + 1))
                        for h in range(HU):
                            last = pe.transpose(p_bank[n % 2][0:NK, h * P:(h + 1) * P], probs[:, n % SLOTS, h], ident)
                        last.then_inc(probsT_ps, 1)
                    if f is not None:
                        front(f, k, 0)
                    at = lagged(c, u, k, PLAG)
                    if at is not None:
                        pair, n = at
                        b, j = divmod(n, UB)
                        g = n // 2
                        pe.wait_ge(probsT_done, pair.count(NU, n + 1))
                        if n % 2 == 0 and before(pair, n, 4) is not None:
                            bc, bk = before(pair, n, 4)
                            pe.wait_ge(o_done, bc.count(OG, bk // 2 + 1))
                        for h in range(HU):
                            chunk, row = divmod(STRIP * h, P)
                            col = ((n % 2) * CU + chunk) * P
                            last = pe.matmul(o_bank[g % 2][row:row + STRIP, col:col + P], values[0:NK, pair.c % 2, b, HU * j + h],
                                             probsT[0:NK, n % 2, h * P:(h + 1) * P], start=True, stop=True)
                        last.then_inc(pv_done, 1)
                    if f is not None:
                        front(f, k, 1)
                    if u is not None and k == Y_AT:
                        project(u)

            run_steps(pe, step, n_pairs, 3, 4)

        @block.scalar
        def _(act):
            if kind == "wide":
                for n in range(UB):
                    act.wait_ge(prepared_ps, n + 1)
                    act.activation(product[:, HU * n:HU * (n + 1)].rearrange("p h d -> p (h d)"), (f_bank, y_bank)[n % 2], ACT.Copy,
                                   scale=64.0 ** -0.5).then_inc(product_done, 1)

            def front(f, k, place):
                for m in range(FU):
                    if FRONT_AT[m] == (k, place):
                        act.wait_ge(front_ps, f.count(FU, m + 1))
                        if f.back(2).real:
                            if m == (0 if kind == "wide" else 2):
                                act.wait_ge(s_ps, f.back(2).count(NU, NU))
                            if m == (6 if kind == "wide" else 3):
                                act.wait_ge(pv_done, f.back(2).count(NU, NU))
                        front_act(act, f, m).then_inc(front_done, 1)

            def step(f, c, u):
                for k in range(NU):
                    at = lagged(c, u, k, TLAG)
                    if at is not None:
                        pair, n = at
                        act.wait_ge(probsT_ps, pair.count(NU, n + 1))
                        if before(pair, n, 2) is not None:
                            bc, bk = before(pair, n, 2)
                            act.wait_ge(pv_done, bc.count(NU, bk + 1))
                        act.activation(probsT[0:NK, n % 2], p_bank[n % 2][0:NK], ACT.Copy).then_inc(probsT_done, 1)
                    if f is not None:
                        front(f, k, 0)
                    if c is not None:
                        act.wait_ge(max_done, c.count(NU, k + 1))
                        scores = biased[:, k % SLOTS] if kind == "causal" else s_bank[k % 2]
                        if before(c, k, SLOTS) is not None:
                            bc, bk = before(c, k, SLOTS)
                            act.wait_ge(probs_done, bc.count(NU, bk + 1))
                        for h in range(HU):
                            last = act.activation(exps[:, k % SLOTS, h], scores[:, h * NK:(h + 1) * NK], ACT.Exp,
                                                  bias=neg_max[:, k % SLOTS, h:h + 1],
                                                  accum_out=exp_sum[:, k % SLOTS, h:h + 1])
                        last.then_inc(exps_done, 1)
                    if f is not None:
                        front(f, k, 1)

            run_steps(act, step, n_pairs, 3, 4)

        @block.vector
        def _(dve):
            if kind == "wide":
                dve.tensor_scalar(w["wo_scaled"], w["wo"], w["tanh_gate"], None, ALU.mult).then_inc(prepared, 1)
                dve.tensor_scalar(extra[:], w["bo"], w["tanh_gate"], None, ALU.mult).then_inc(prepared, 1)
            elif kind == "causal":
                dve.wait_ge(ready, READY)
                dve.tensor_tensor(value_row[:], value_row[:], w["bv"].unsqueeze(2).to_broadcast([P, NC, P]), ALU.mult).then_inc(prepared, 1)
                dve.tensor_scalar(q_bias[:], w["bq"], 8.0 ** -0.5, None, ALU.mult).then_inc(prepared, 1)
                dve.wait_ge(prepared_ps, 1)
                dve.tensor_tensor(extra[:], f_bank[:, 0:P], w["bo"], ALU.add).then_inc(prepared, 1)
            else:
                for t, name in enumerate(("q_norm", "k_norm")):
                    wn = w[name]
                    scale = 1.0 if t == 0 else 8.0 ** 0.5
                    dve.scalar_tensor_tensor(out=table[:, 0, t], in0=consts["rope"][:, 0, t], scalar=scale, in1=wn,
                                             op0=ALU.mult, op1=ALU.mult).then_inc(prepared, 1)
                    for half in range(2):
                        a, b = 4 * half, 4 * (1 - half)
                        dve.scalar_tensor_tensor(out=table[:, 1, t, a:a + 4], in0=consts["rope"][:, 1, t, a:a + 4], scalar=scale,
                                                 in1=wn[:, b:b + 4], op0=ALU.mult, op1=ALU.mult).then_inc(prepared, 1)
                dve.wait_ge(prepared, 6)

            def inverse_root(f, part):
                n = [3 * part]

                def link(ins):
                    n[0] += 1
                    ins.then_inc(qk_rstd_done, 1)
                    dve.wait_ge(qk_rstd_done, f.count(ROOT, n[0]))

                y, bits = qk_rstd[:], qk_rstd[:].bitcast(I32)
                if part == 0:
                    dve.wait_ge(square_done, f.count(1, 1))
                    link(dve.tensor_scalar(qk_sum[:], qk_sum[:], 8e-6, None, ALU.add))
                    link(dve.tensor_scalar(bits, qk_sum[:].bitcast(I32), 1, 0x7fffffff,
                                           ALU.logical_shift_right, ALU.bitwise_xor))
                    link(dve.tensor_scalar(y, y, SEED_SCALE, None, ALU.mult))
                else:
                    link(dve.tensor_tensor(root_part[:], y, y, ALU.mult))
                    link(dve.scalar_tensor_tensor(out=root_part[:], in0=root_part[:], scalar=-0.5, in1=qk_sum[:], op0=ALU.mult, op1=ALU.mult))
                    link(dve.scalar_tensor_tensor(out=y, in0=root_part[:], scalar=1.5, in1=y, op0=ALU.add, op1=ALU.mult))
                assert n[0] == 3 * part + 3, n

            def step(f, c, u, n):
                for k in range(NU):
                    if n is not None and k in (3, 4):
                        s, b = n.c % 4, k - 3
                        dve.wait_ge(rstd_done, n.count(1, 1))
                        dve.tensor_scalar(X[:, n.index(2, b), :], z[:, s, b], mean_var[:, s, b, 0:1], rstd[:, s, b:b + 1],
                                          ALU.subtract, ALU.mult).then_inc(x_written, 1)
                    if c is not None:
                        dve.wait_ge(s_ps, c.count(NU, k + 1))
                        scores = s_bank[k % 2][:, 0:HU * NK]
                        if before(c, k, SLOTS) is not None:
                            bc, bk = before(c, k, SLOTS)
                            dve.wait_ge(exps_done, bc.count(NU, bk + 1))
                        if kind == "causal":
                            j = k % UB
                            dve.tensor_tensor(biased[:, k % SLOTS], scores, consts["alibi"][:, HU * NK * j:HU * NK * (j + 1)],
                                              ALU.add).then_inc(biased_done, 1)
                            dve.wait_ge(biased_done, c.count(NU, k + 1))
                            scores = biased[:, k % SLOTS]
                        dve.tensor_reduce(neg_max[:, k % SLOTS], scores.rearrange("p (h n) -> p h n", h=HU), AX.X, ALU.max,
                                          negate=True).then_inc(max_done, 1)
                    at = lagged(c, u, k, MLAG)
                    if at is not None:
                        pair, m = at
                        dve.wait_ge(exps_done, pair.count(NU, m + 1))
                        if before(pair, m, SLOTS) is not None:
                            bc, bk = before(pair, m, SLOTS)
                            dve.wait_ge(probs_done, bc.count(NU, bk + 1))
                        dve.reciprocal(inv_sum[:, m % SLOTS], exp_sum[:, m % SLOTS]).then_inc(inv_done, 1)
                    if kind != "wide":
                        keys_ahead(dve, f, c, k, DVE_KEYS)
                    at = lagged(c, u, k, OLAG)
                    if at is not None and at[1] % 2 == 1:
                        pair, m = at
                        b, j = divmod(m - 1, UB)
                        dve.wait_ge(pv_done, pair.count(NU, m + 1))
                        if pair.back(2).real:
                            dve.wait_ge(y_ps, pair.back(2).count(1, 1))
                        dve.tensor_copy(oT[:, pair.c % 2, b, CU * j:CU * (j + 2)].rearrange("p n q -> p (n q)"),
                                        o_bank[(m // 2) % 2][:, 0:2 * CU * P]).then_inc(o_done, 1)
                    if f is not None and kind == "wide":
                        if k == 0:
                            wait_loaded(dve, f)
                            for b in range(2):
                                dve.bn_stats(pre_stats[:, b], xin[:, f.c % 4, b]).then_inc(pre_done, 1)
                            dve.wait_ge(pre_done, f.count(4, 2))
                            if f.back(1).real:
                                dve.wait_ge(turn_done, f.back(1).count(2, 2))
                            dve.nop(nofuse=True)
                            for b in range(2):
                                dve.bn_aggr(pre_mean_var[:, b], pre_stats[:, b]).then_inc(pre_done, 1)
                        if k == 2:
                            dve.wait_ge(pre_rstd_done, f.count(1, 1))
                            if f.back(1).real:
                                dve.wait_ge(front_ps, f.back(1).count(FU, FU))
                            for b in range(2):
                                dve.tensor_scalar(xn[:, b], xin[:, f.c % 4, b], pre_mean_var[:, b, 0:1], pre_rstd[:, b:b + 1],
                                                  ALU.subtract, ALU.mult).then_inc(turn_done, 1)
                    if f is not None and kind == "rotary":
                        four = qk[:].rearrange("p b t h d -> p (b t) h d")
                        if k == 2:
                            dve.wait_ge(front_done, f.count(FU, 2))
                            dve.tensor_reduce(qk_sum[:].rearrange("p (n h) -> p n h", n=4), qk_sq[:], AX.X, ALU.add).then_inc(square_done, 1)
                            inverse_root(f, 0)
                        if k == 3:
                            inverse_root(f, 1)
                            inverse_root(f, 2)
                        if k == 4:
                            inverse_root(f, 3)
                            dve.wait_ge(turn_done, f.count(TURNS, TURNS))
                            if f.back(1).real:
                                dve.wait_ge(front_ps, f.back(1).count(FU, 3))
                            dve.tensor_tensor(turned[:].rearrange("p n h d -> p (n h) d"), crossed[:].rearrange("p n h d -> p (n h) d"),
                                              qk_rstd[:].unsqueeze(2).to_broadcast([P, 4 * H, 8]), ALU.mult).then_inc(scaled_done, 1)
                    if u is not None and k == Z_AT:
                        s = u.c % 4
                        dve.wait_ge(y_ps, u.count(1, 1))
                        if kind == "rotary":
                            x_part = xin[:, s]
                        else:
                            dve.wait_ge(residual_done, u.count(1, 1))
                            x_part = residual[:, u.c % 2]
                        dve.tensor_tensor(z[:, s], y_bank[:, 0:2 * P].rearrange("p (b q) -> p b q", b=2), x_part, ALU.add).then_inc(z_done, 1)
                        dve.wait_ge(z_done, u.count(1, 1))
                        for b in range(2):
                            dve.bn_stats(stats[:, b], z[:, s, b]).then_inc(stats_done, 1)
                        dve.wait_ge(stats_done, u.count(2, 2))
                        dve.nop(nofuse=True)
                        for b in range(2):
                            dve.bn_aggr(mean_var[:, s, b], stats[:, b]).then_inc(mean_done, 1)

            run_steps(dve, step, n_pairs, 4, 4)


def mixture(chip, kind, n_seq, X, out_dram, w, consts):
    nc = chip.nc
    swiglu = kind == "swiglu"
    E = 8
    NE = E + 1 if swiglu else E
    C = 2 if swiglu else 4
    T = 4
    groups = n_seq // T
    HS = 4
    LAG = 2
    R = 19 if swiglu else 18
    with ExitStack() as ctx:
        def sb(name, shape):
            return chip.sb(ctx, kind + "_" + name, shape)

        def sem(name):
            return chip.sem(ctx, kind + "_" + name)

        power, eps = sb("power", [P, T]), sb("eps", [P, T])
        xin = sb("xin", [P, 4, T, P])
        xT = sb("xT", [P, T * P])
        xT_masked = sb("xT_masked", [P, T * P])
        xT_high, xT_low = (chip.sb(ctx, f"{kind}_{n}", [P, 2, T * P], F32R) for n in ("xT_high", "xT_low"))
        hidden = sb("hidden", [P, HS, C, T * P])
        in_names = ("w1", "w3") if swiglu else ("w1",)
        w_high, w_low = ({n: chip.sb(ctx, f"{kind}_{n}_{part}", [P, NE * C * P], F32R) for n in in_names} for part in ("high", "low"))
        gate = sb("gate", [P, 2, T, NE])
        small = {n: sb(n, [P, T, E]) for n in ("logits", "expd", "choice", "equal", "ranked", "picked", "first")}
        tops = {n: sb(n, [P, T]) for n in ("top", "key_top", "rank_top", "total", "inv_total")}
        z = sb("z", [P, 4, T, P])
        stats = sb("stats", [P, T, 6])
        mean_var = sb("mean_var", [P, 4, T, 2])
        var_eps = sb("var_eps", [P, T])
        rstd = sb("rstd", [P, 2, T])
        if swiglu:
            silu = sb("silu", [P, 2, T * P])
        else:
            gateT = sb("gateT", [E, T * P])
        h_bank = [chip.banks[:, n] for n in range(4)]
        y_bank = [chip.banks[:, 4], chip.banks[:, 5]]
        x_bank, r_bank = chip.banks[:, 6], chip.banks[:, 7]

        x_loaded = [sem(f"x_loaded{n}") for n in range(4)]
        ready, xT_ps, xT_done, logits_ps, routed, exp_done, gateT_ps, gateT_done, base_ps, base_done = (
            sem(n) for n in ("ready", "xT_ps", "xT_done", "logits_ps", "routed", "exp_done", "gateT_ps", "gateT_done",
                             "base_ps", "base_done"))
        h_ps, silu_done, h_done, y_ps, summed = (sem(n) for n in ("h_ps", "silu_done", "h_done", "y_ps", "summed"))
        masked_done, w_split, xT_masked_done, xT_split = (sem(n) for n in ("masked_done", "w_split", "xT_masked_done", "xT_split"))
        stats_done, mean_done, var_done, rstd_done, x_written, stored = (
            sem(n) for n in ("stats_done", "mean_done", "var_done", "rstd_done", "x_written", "stored"))
        block = ctx.enter_context(nc.Block())
        ident = consts["ident"]

        def lagged(c, u, e):
            if e >= LAG:
                return (c, e - LAG) if c is not None else None
            return (u, e - LAG + NE) if u is not None else None

        def before(g, e, n):
            if e >= n:
                return (g, e - n)
            return (g.back(1), e - n + NE) if g.back(1).real else None

        @block.sync
        def _(sp):
            def step(f, c, u, n):
                if f is not None:
                    s = f.c % 4
                    if f.back(4).real:
                        sp.wait_ge(mean_done, f.back(4).count(T, T))
                    sp.dma_start(xin[:, s], X[:, bass.ds(f.index(T), T), :]).then_inc(x_loaded[s], 16)
                if n is not None and out_dram is not None:
                    sp.wait_ge(x_written, n.count(T, T))
                    sp.dma_start(out_dram[bass.ds(n.index(T), T)].rearrange("b t d -> t b d"),
                                 X[:, bass.ds(n.index(T), T), :]).then_inc(stored, 16)

            run_steps(sp, step, groups, 4, 4)
            if out_dram is not None:
                sp.wait_ge(stored, 16 * groups)

        @block.gpsimd
        def _(pool):
            pool.memset(power[:], -0.5).then_inc(ready, 1)
            pool.memset(gate[:], 1.0).then_inc(ready, 1)
            pool.memset(eps[:], LN_EPS).then_inc(ready, 1)
            pool.wait_ge(ready, 3)

            def step(f, c, u):
                if f is not None:
                    pool.wait_ge(xT_masked_done, f.count(1, 1))
                    if f.back(2).real:
                        pool.wait_ge(h_ps, f.back(2).count(NE * C, NE * C))
                    pool.nop(nofuse=True)
                    pool.tensor_copy(xT_high[:, f.c % 2], xT_masked[:]).then_inc(xT_split, 1)
                    pool.tensor_tensor(xT_low[:, f.c % 2], xT[:], xT_masked[:], ALU.subtract).then_inc(xT_split, 1)
                if u is not None:
                    s = u.c % 4
                    pool.wait_ge(mean_done, u.count(T, T))
                    if u.back(1).real:
                        pool.wait_ge(rstd_done, u.back(1).count(1, 1))
                    pool.tensor_tensor(var_eps[:], mean_var[:, s, :, 1], eps[:], ALU.add).then_inc(var_done, 1)
                    pool.wait_ge(var_done, u.count(1, 1))
                    if u.back(2).real:
                        pool.wait_ge(x_written, u.back(2).count(T, T))
                    pool.tensor_tensor(rstd[:, u.c % 2], var_eps[:], power[:], ALU.pow).then_inc(rstd_done, 1)

            run_steps(pool, step, groups, 3, 4)

        @block.scalar
        def _(act):
            def step(f, c, u):
                for e in range(NE):
                    if c is not None:
                        par = (c.c * NE + e) % HS
                        if before(c, e, HS) is not None:
                            g, be = before(c, e, HS)
                            act.wait_ge(y_ps, g.count(NE, be + 1))
                        for m in range(C):
                            act.wait_ge(h_ps, c.count(NE * C, e * C + m + 1))
                            if swiglu:
                                if e >= 1 or c.back(1).real:
                                    act.wait_ge(h_done, c.count(NE * C, (e - 1) * C + m + 1))
                                act.activation(silu[:, m], h_bank[2 * m], ACT.Silu).then_inc(silu_done, 1)
                            else:
                                act.activation(hidden[:, par, m], h_bank[m], ACT.Gelu, bias=w["b1"][:, e, m:m + 1]).then_inc(h_done, 1)
                    if f is not None:
                        if e == 1:
                            act.wait_ge(xT_ps, f.count(1, 1))
                            if f.back(1).real:
                                act.wait_ge(xT_split, f.back(1).count(2, 2))
                                act.wait_ge(logits_ps, f.back(1).count(1, 1))
                            act.activation(xT[:], x_bank, ACT.Copy).then_inc(xT_done, 1)
                        if e == 3:
                            act.wait_ge(routed, f.count(R, 2))
                            act.activation(small["expd"][:], small["logits"][:], ACT.Exp).then_inc(exp_done, 1)
                        if e == 6 and not swiglu:
                            act.wait_ge(gateT_ps, f.count(1, 1))
                            act.activation(gateT[:], r_bank[0:E], ACT.Copy).then_inc(gateT_done, 1)

            run_steps(act, step, groups, 3, 4)

        @block.vector
        def _(dve):
            dve.wait_ge(ready, 3)
            for n, t in enumerate(in_names):
                masked = hidden[:].rearrange("p s c t -> p (s c t)")[:, 0:NE * C * P]
                if n >= 1:
                    dve.wait_ge(w_split, 2 * n)
                dve.tensor_scalar(masked.bitcast(I32), w[t].bitcast(I32), HIGH, None, ALU.bitwise_and).then_inc(masked_done, 1)
                dve.wait_ge(masked_done, n + 1)
                dve.tensor_copy(w_high[t][:], masked).then_inc(w_split, 1)
                dve.tensor_tensor(w_low[t][:], w[t], masked, ALU.subtract).then_inc(w_split, 1)

            def route(f, part):
                n = [0 if part == 0 else 2]

                def link(ins):
                    n[0] += 1
                    ins.then_inc(routed, 1)
                    dve.wait_ge(routed, f.count(R, n[0]))

                def over(t):
                    return t[:].unsqueeze(2).to_broadcast([P, T, E])

                def row(t):
                    return t.unsqueeze(1).to_broadcast([P, T, E])

                logits, expd, choice, equal, ranked, picked, first = (
                    small[n][:] for n in ("logits", "expd", "choice", "equal", "ranked", "picked", "first"))
                top, key_top, rank_top, total, inv_total = (tops[n] for n in ("top", "key_top", "rank_top", "total", "inv_total"))
                if part == 0:
                    dve.wait_ge(logits_ps, f.count(1, 1))
                    ps = r_bank[:, 0:T * E].rearrange("p (t e) -> p t e", t=T)
                    link(dve.tensor_reduce(top[:], ps, AX.X, ALU.max))
                    link(dve.tensor_tensor(logits, ps, over(top), ALU.subtract))
                    return
                dve.wait_ge(exp_done, f.count(1, 1))
                if swiglu:
                    link(dve.tensor_reduce(total[:], expd, AX.X, ALU.add))
                    link(dve.reciprocal(inv_total[:], total[:]))
                    link(dve.tensor_tensor(expd, expd, over(inv_total), ALU.mult))
                    link(dve.tensor_tensor(choice, expd, row(w["gate_bias"]), ALU.add))
                keys = choice if swiglu else expd
                for turn in range(2):
                    link(dve.tensor_reduce(key_top[:], keys, AX.X, ALU.max))
                    link(dve.tensor_tensor(equal, keys, over(key_top), ALU.is_equal))
                    link(dve.tensor_tensor(ranked, equal, row(consts["rank8"]), ALU.mult))
                    link(dve.tensor_reduce(rank_top[:], ranked, AX.X, ALU.max))
                    link(dve.tensor_tensor(first if turn == 0 else picked, ranked, over(rank_top), ALU.is_equal))
                    if turn == 0:
                        link(dve.scalar_tensor_tensor(out=choice.rearrange("p t e -> p (t e)"), in0=first.rearrange("p t e -> p (t e)"),
                                                      scalar=-1e30, in1=keys.rearrange("p t e -> p (t e)"), op0=ALU.mult, op1=ALU.add))
                        keys = choice
                link(dve.tensor_tensor(picked, picked, first, ALU.add))
                out = gate[:, f.c % 2, :, 0:E]
                if f.back(2).real:
                    dve.wait_ge(summed, f.back(2).count(NE * T, NE * T))
                if swiglu:
                    link(dve.tensor_tensor(out, picked, expd, ALU.mult))
                else:
                    link(dve.tensor_tensor(picked, picked, expd, ALU.mult))
                    link(dve.tensor_reduce(total[:], picked, AX.X, ALU.add))
                    link(dve.reciprocal(inv_total[:], total[:]))
                    link(dve.tensor_tensor(out, picked, over(inv_total), ALU.mult))
                assert n[0] == R, n

            def step(f, c, u, n):
                for e in range(NE):
                    if c is not None and swiglu:
                        par = (c.c * NE + e) % HS
                        for m in range(C):
                            dve.wait_ge(silu_done, c.count(NE * C, e * C + m + 1))
                            dve.tensor_tensor(hidden[:, par, m], silu[:, m], h_bank[2 * m + 1], ALU.mult).then_inc(h_done, 1)
                    if f is not None and e == 2:
                        dve.wait_ge(xT_done, f.count(1, 1))
                        if f.back(1).real:
                            dve.wait_ge(xT_split, f.back(1).count(2, 2))
                        dve.tensor_scalar(xT_masked[:].bitcast(I32), xT[:].bitcast(I32), HIGH, None,
                                          ALU.bitwise_and).then_inc(xT_masked_done, 1)
                    at = lagged(c, u, e)
                    if at is not None:
                        g, n_exp = at
                        dve.wait_ge(y_ps, g.count(NE, n_exp + 1))
                        if n_exp >= 1:
                            dve.wait_ge(summed, g.count(NE * T, n_exp * T))
                        elif not swiglu:
                            dve.wait_ge(base_done, g.count(1, 1))
                        for t in range(T):
                            rest = z[:, g.c % 4, t] if n_exp >= 1 or not swiglu else xin[:, g.c % 4, t]
                            dve.scalar_tensor_tensor(out=z[:, g.c % 4, t], in0=y_bank[(g.c * NE + n_exp) % 2][:, t * P:(t + 1) * P],
                                                     scalar=gate[:, g.c % 2, t, n_exp:n_exp + 1], in1=rest,
                                                     op0=ALU.mult, op1=ALU.add).then_inc(summed, 1)
                    if u is not None and e == LAG - 1:
                        s = u.c % 4
                        dve.wait_ge(summed, u.count(NE * T, NE * T))
                        for t in range(T):
                            dve.bn_stats(stats[:, t], z[:, s, t]).then_inc(stats_done, 1)
                        dve.wait_ge(stats_done, u.count(T, T))
                        dve.nop(nofuse=True)
                        for t in range(T):
                            dve.bn_aggr(mean_var[:, s, t], stats[:, t]).then_inc(mean_done, 1)
                    if n is not None and e == 1:
                        s = n.c % 4
                        dve.wait_ge(rstd_done, n.count(1, 1))
                        for t in range(T):
                            dve.tensor_scalar(X[:, n.index(T, t), :], z[:, s, t], mean_var[:, s, t, 0:1],
                                              rstd[:, n.c % 2, t:t + 1], ALU.subtract, ALU.mult).then_inc(x_written, 1)
                    if f is not None and e in (2, 5):
                        route(f, 0 if e == 2 else 1)
                    if f is not None and e == 7 and not swiglu:
                        dve.wait_ge(base_ps, f.count(1, 1))
                        dve.tensor_tensor(z[:, f.c % 4], r_bank.rearrange("p (t d) -> p t d", t=T), xin[:, f.c % 4], ALU.add).then_inc(base_done, 1)

            run_steps(dve, step, groups, 4, 4)

        @block.tensor
        def _(pe):
            def product(out, a_high, a_low, b_high, b_low):
                pe.matmul(out, a_high, b_high, start=True, stop=False)
                pe.matmul(out, a_high, b_low, start=False, stop=False)
                return pe.matmul(out, a_low, b_high, start=False, stop=True)

            pe.wait_ge(w_split, 2 * len(in_names))

            def step(f, c, u):
                for e in range(NE):
                    if c is not None:
                        if e == 0:
                            pe.wait_ge(xT_split, c.count(2, 2))
                        for m in range(C):
                            if e >= 1 or c.back(1).real:
                                pe.wait_ge(h_done, c.count(NE * C, (e - 1) * C + m + 1))
                            cols = slice(e * C * P + m * P, e * C * P + (m + 1) * P)
                            for n, name in enumerate(in_names):
                                last = product(h_bank[len(in_names) * m + n], w_high[name][:, cols], w_low[name][:, cols],
                                               xT_high[:, c.c % 2], xT_low[:, c.c % 2])
                            last.then_inc(h_ps, 1)
                    at = lagged(c, u, e)
                    if at is not None:
                        g, n_exp = at
                        par = (g.c * NE + n_exp) % 2
                        slot = (g.c * NE + n_exp) % HS
                        if before(g, n_exp, 2) is not None:
                            bg, be = before(g, n_exp, 2)
                            pe.wait_ge(summed, bg.count(NE * T, (be + 1) * T))
                        for t in range(T):
                            for m in range(C):
                                if t == 0:
                                    pe.wait_ge(h_done, g.count(NE * C, n_exp * C + m + 1))
                                tokens = slice(t * P, (t + 1) * P)
                                last = pe.matmul(y_bank[par][:, tokens], hidden[:, slot, m, tokens], w["w2"][:, n_exp, m],
                                                 start=m == 0, stop=m == C - 1)
                        last.then_inc(y_ps, 1)
                    if f is not None and e == 0:
                        pe.wait_ge(x_loaded[f.c % 4], f.load(4))
                        if f.back(1).real:
                            pe.wait_ge(xT_done, f.back(1).count(1, 1))
                        for t in range(T):
                            last = pe.transpose(x_bank[:, t * P:(t + 1) * P], xin[:, f.c % 4, t], ident)
                        last.then_inc(xT_ps, 1)
                    if f is not None and e == 2:
                        pe.wait_ge(xT_done, f.count(1, 1))
                        if f.back(1).real:
                            if swiglu:
                                pe.wait_ge(routed, f.back(1).count(R, 2))
                            else:
                                pe.wait_ge(base_done, f.back(1).count(1, 1))
                        for t in range(T):
                            last = pe.matmul(r_bank[:, t * E:(t + 1) * E], xT[:, t * P:(t + 1) * P], w["router"],
                                             start=True, stop=True)
                        last.then_inc(logits_ps, 1)
                    if f is not None and not swiglu:
                        if e == 6:
                            pe.wait_ge(routed, f.count(R, R))
                            for t in range(T):
                                last = pe.transpose(r_bank[0:E, t * P:(t + 1) * P], gate[:, f.c % 2, t, 0:E], ident)
                            last.then_inc(gateT_ps, 1)
                        if e == 7:
                            pe.wait_ge(gateT_done, f.count(1, 1))
                            for t in range(T):
                                last = pe.matmul(r_bank[:, t * P:(t + 1) * P], gateT[:, t * P:(t + 1) * P], w["b2"],
                                                 start=True, stop=True)
                            last.then_inc(base_ps, 1)

            run_steps(pe, step, groups, 3, 4)


FIRST = {
    "ident": [P, P], "heads8": [P, 8],
    "ta_gamma": [P, 1], "ta_wq": [P, P], "ta_wk": [P, P], "ta_wv": [P, P], "ta_wo": [P, P],
}
REST = {
    "heads16": [P, 16], "rank8": [P, 8], "rope": [P, 2, 2, 8],
    "cx_gamma": [P, 1], "cx_beta": [P, 1], "cx_gate": [P, 1], "cx_bo": [P, P],
    "g_router": [P, 8], "g_b1": [P, 8, 4], "g_b2": [8, P],
    "sa_wq": [P, P], "sa_wk": [P, P], "sa_wv": [P, P], "sa_wo": [P, 4, P], "sa_bq": [P, 1], "sa_bk": [P, 1], "sa_bv": [P, 4], "sa_bo": [P, P],
    "ra_wq": [P, P], "ra_wk": [P, P], "ra_wv": [P, P], "ra_wo": [P, 4, P], "ra_qn": [P, 8], "ra_kn": [P, 8],
    "s_router": [P, 8], "s_bias": [P, 8],
}
LARGE = {
    "cx_wqT": [64, 16, P], "cx_wkT": [64, 16, P], "cx_wv": [P, 1024], "cx_wo": [P, 8, P],
    "g_w1": [P, 8 * 512], "g_w2": [P, 8, 4, P],
    "alibi": [P, 16 * P],
    "s_w1": [P, 9 * 256], "s_w3": [P, 9 * 256], "s_w2": [P, 9, 2, P],
}


def build(nc, n_seq, x_dram, ctxT_dram, weights_dram, out_dram):
    with ExitStack() as ctx:
        chip = Chip(nc, ctx)
        X = chip.sb(ctx, "X", [P, n_seq, P])
        tanh_gate = chip.sb(ctx, "tanh_gate", [P, 1])
        def columns(*names):
            return sum(_free(LARGE[n]) for n in names)

        region_a = chip.sb(ctx, "region_a", [P, max(columns("g_w1", "g_w2"), columns("s_w1", "s_w3", "s_w2"))])
        region_b = chip.sb(ctx, "region_b", [P, columns("cx_wqT", "cx_wkT", "cx_wv", "cx_wo", "cx_wo")])
        sems = {n: ctx.enter_context(nc.semaphore("loaded_" + n)) for n in ("first", "small", "cx", "gelu", "alibi", "swiglu")}

        def cut(region, at, shape):
            n = 1
            for k in shape[1:]:
                n *= k
            v = region[0:shape[0], at:at + n]
            if len(shape) == 3:
                v = v.rearrange("p (a b) -> p a b", a=shape[1])
            if len(shape) == 4:
                v = v.rearrange("p (a b c) -> p a b c", a=shape[1], b=shape[2])
            return v

        small, packed = {}, {}
        for name, shapes in (("first", FIRST), ("rest", REST)):
            packed[name] = chip.sb(ctx, name, [P, sum(_free(shape) for shape in shapes.values())])
            column = 0
            for n, shape in shapes.items():
                small[n] = cut(packed[name], column, shape)
                column += _free(shape)

        large, at = {}, {"a": 0, "b": 0}
        for names, region, key in ((("cx_wqT", "cx_wkT", "cx_wv", "cx_wo"), region_b, "b"), (("g_w1", "g_w2"), region_a, "a")):
            for n in names:
                large[n] = cut(region, at[key], LARGE[n])
                at[key] += _free(LARGE[n])
        wo_scaled = cut(region_b, at["b"], [P, 8, P])
        large["alibi"] = cut(region_b, 0, LARGE["alibi"])
        a = 0
        for n in ("s_w1", "s_w3", "s_w2"):
            large[n] = cut(region_a, a, LARGE[n])
            a += _free(LARGE[n])

        x_loaded = [ctx.enter_context(nc.semaphore(f"x_loaded{n}")) for n in range(4)]

        def load_block(queue, names, sem, x_too=False):
            with nc.Block() as block:
                if x_too:
                    @block.sync
                    def _(sp):
                        for n, loaded in enumerate(x_loaded):
                            part = slice(n * n_seq // len(x_loaded), (n + 1) * n_seq // len(x_loaded))
                            sp.dma_start(X[:, part, :], x_dram[part].rearrange("b t d -> t b d")).then_inc(loaded, 16)
                        for loaded in x_loaded:
                            sp.wait_ge(loaded, 16)

                @block.scalar
                def _(act):
                    for names_, sem_ in queue:
                        for n in names_:
                            act.dma_start(packed[n][:] if n in packed else large[n], weights_dram[n]).then_inc(sem_, 16)
                    act.wait_ge(sem, 16 * len(names))

        load_block([(["first"], sems["first"]), (["rest"], sems["small"]),
                    (["cx_wqT", "cx_wkT", "cx_wv", "cx_wo"], sems["cx"]), (["g_w1", "g_w2"], sems["gelu"])], ["first"], sems["first"], x_too=True)
        consts = {n: small[n] for n in ("ident", "heads8", "heads16", "rank8", "rope")}
        consts["alibi"] = large["alibi"]
        taylor_attention(chip, n_seq, X, {"gamma": small["ta_gamma"], "wq": small["ta_wq"], "wk": small["ta_wk"],
                                                  "wv": small["ta_wv"], "wo": small["ta_wo"]}, consts)
        chip.clear_semaphores()
        with nc.Block() as block:
            @block.scalar
            def _(act):
                act.wait_ge(sems["small"], 16)
                act.wait_ge(sems["cx"], 16 * 4)
                act.activation(tanh_gate[:], small["cx_gate"], ACT.Tanh)
        softmax_attention(chip, "wide", n_seq, X, ctxT_dram, {
            "wqT": large["cx_wqT"], "wkT": large["cx_wkT"], "wv": large["cx_wv"], "wo": large["cx_wo"], "wo_scaled": wo_scaled,
            "gamma": small["cx_gamma"], "beta": small["cx_beta"], "tanh_gate": tanh_gate[:], "bo": small["cx_bo"]}, consts)
        chip.clear_semaphores()
        load_block([(["alibi"], sems["alibi"])], ["g_w1", "g_w2"], sems["gelu"])
        mixture(chip, "gelu", n_seq, X, None, {
            "w1": large["g_w1"], "w2": large["g_w2"], "b1": small["g_b1"], "b2": small["g_b2"], "router": small["g_router"]}, consts)
        chip.clear_semaphores()
        load_block([(["s_w1", "s_w3", "s_w2"], sems["swiglu"])], ["alibi"], sems["alibi"])
        softmax_attention(chip, "causal", n_seq, X, None, {
            "wq": small["sa_wq"], "wk": small["sa_wk"], "wv": small["sa_wv"], "wo": small["sa_wo"],
            "bq": small["sa_bq"], "bk": small["sa_bk"], "bv": small["sa_bv"], "bo": small["sa_bo"]}, consts)
        chip.clear_semaphores()
        softmax_attention(chip, "rotary", n_seq, X, ctxT_dram, {
            "wq": small["ra_wq"], "wk": small["ra_wk"], "wv": small["ra_wv"], "wo": small["ra_wo"],
            "q_norm": small["ra_qn"], "k_norm": small["ra_kn"]}, consts)
        chip.clear_semaphores()
        with nc.Block() as block:
            @block.scalar
            def _(act):
                act.wait_ge(sems["swiglu"], 16 * 3)
        mixture(chip, "swiglu", n_seq, X, out_dram, {
            "w1": large["s_w1"], "w3": large["s_w3"], "w2": large["s_w2"], "router": small["s_router"],
            "gate_bias": small["s_bias"]}, consts)


def _free(shape):
    n = 1
    for k in shape[1:]:
        n *= k
    return n


def layouts(inputs, np):
    g = {k: np.asarray(v) for k, v in inputs.items()}

    def down(v):
        return v.reshape(-1, 1)

    def rows(v):
        return np.broadcast_to(v.reshape(1, -1), (P, v.size))

    def hidden_major(w1):
        return w1.transpose(2, 0, 1).reshape(P, -1)

    def chunks(w2):
        e, d, h = w2.shape
        return w2.transpose(0, 2, 1).reshape(e, h // P, P, d).transpose(2, 0, 1, 3)

    def strips(w):
        v = np.zeros((4, 32, 4, w.shape[-1]), w.dtype)
        v[:, :8] = w.reshape(4, 4, 8, -1).transpose(1, 2, 0, 3)
        return v.reshape(P, 4, -1)

    q = np.arange(P)
    slopes = np.power(np.float32(2.0), np.float32(-8.0) * np.arange(1, 17, dtype=np.float32) / np.float32(16))
    rel = np.abs(q[:, None] - q[None, :]).astype(np.float32)
    alibi = np.where((q[:, None] >= q[None, :])[:, None, :], -slopes[None, :, None] * rel[:, None, :], np.float32(-1e30))
    rope = np.zeros((P, 2, 2, 8), np.float32)
    for t, theta in enumerate((32.0, 1000.0)):
        freqs = np.power(np.float32(theta), -np.arange(0, 8, 2, dtype=np.float32) / np.float32(8))
        angle = np.arange(P, dtype=np.float32)[:, None] * freqs[None, :]
        rope[:, 0, t] = np.concatenate([np.cos(angle), np.cos(angle)], -1)
        rope[:, 1, t] = np.concatenate([-np.sin(angle), np.sin(angle)], -1)
    w_kv, x_kv = g["L0_attn_w_kv"], g["L0_xattn_w_kv"]
    arrays = {
        "ident": np.eye(P, dtype=np.float32),
        "heads8": (q[:, None] // 16 == np.arange(8)[None, :]).astype(np.float32),
        "heads16": (q[:, None] // 8 == np.arange(16)[None, :]).astype(np.float32),
        "rank8": np.broadcast_to(np.arange(8, 0, -1).astype(np.float32)[None, :], (P, 8)),
        "rope": rope,
        "alibi": alibi.reshape(P, -1).astype(np.float32),
        "ta_gamma": down(g["L0_attn_gamma"]), "ta_wq": g["L0_attn_w_q"], "ta_wk": w_kv[:, :P], "ta_wv": w_kv[:, P:],
        "ta_wo": g["L0_attn_w_out"],
        "cx_gamma": down(g["L0_xattn_ln_gamma"]), "cx_beta": down(g["L0_xattn_ln_beta"]),
        "cx_gate": rows(g["L0_xattn_gate"]), "cx_bo": rows(g["L0_xattn_b_out"]),
        "cx_wqT": g["L0_xattn_w_q"].T.reshape(16, 64, P).transpose(1, 0, 2),
        "cx_wkT": x_kv[:, :1024].T.reshape(16, 64, P).transpose(1, 0, 2),
        "cx_wv": x_kv[:, 1024:], "cx_wo": g["L0_xattn_w_out"].reshape(8, P, P).transpose(1, 0, 2),
        "g_router": g["L0_ffn_Wr"].T, "g_w1": hidden_major(g["L0_ffn_W1"]), "g_w2": chunks(g["L0_ffn_W2"]),
        "g_b1": g["L0_ffn_b1"].reshape(8, 4, P).transpose(2, 0, 1), "g_b2": g["L0_ffn_b2"],
        "sa_wq": g["L1_attn_Wq"].T, "sa_wk": g["L1_attn_Wk"].T, "sa_wv": g["L1_attn_Wv"].T, "sa_wo": strips(g["L1_attn_Wo"].T),
        "sa_bq": down(g["L1_attn_bq"]), "sa_bk": down(g["L1_attn_bk"]), "sa_bv": strips(g["L1_attn_bv"].reshape(P, 1)).reshape(P, 4), "sa_bo": rows(g["L1_attn_bo"]),
        "ra_wq": g["L1_xattn_Wq"].T, "ra_wk": g["L1_xattn_Wk"].T, "ra_wv": g["L1_xattn_Wv"].T, "ra_wo": strips(g["L1_xattn_Wo"].T),
        "ra_qn": rows(g["L1_xattn_q_norm_w"]), "ra_kn": rows(g["L1_xattn_k_norm_w"]),
        "s_router": g["L1_ffn_gate_w"].T, "s_bias": rows(g["L1_ffn_gate_bias"]),
        "s_w1": hidden_major(np.concatenate([g["L1_ffn_w1"], g["L1_ffn_sw1"][None]])),
        "s_w3": hidden_major(np.concatenate([g["L1_ffn_w3"], g["L1_ffn_sw3"][None]])),
        "s_w2": chunks(np.concatenate([g["L1_ffn_w2"], g["L1_ffn_sw2"][None]])),
    }
    for name, shapes in (("first", FIRST), ("rest", REST)):
        columns = []
        for n in shapes:
            part = arrays.pop(n)
            whole = np.zeros((P, _free(shapes[n])), np.float32)
            whole[:part.shape[0]] = part.reshape(part.shape[0], -1)
            columns.append(whole)
        arrays[name] = np.concatenate(columns, axis=1)
    return arrays


def kernel(**inputs):
    import numpy as np
    import concourse.bacc as bacc
    from concourse.bass_utils import run_bass_kernel_spmd

    nc = bacc.Bacc("TRN2", target_bir_lowering=False, num_devices=1)
    arrays = {n: np.ascontiguousarray(a) for n, a in layouts(inputs, np).items()}
    arrays["x"] = np.ascontiguousarray(inputs["x"])
    arrays["ctxT"] = np.ascontiguousarray(np.asarray(inputs["ctx_1024"]).transpose(2, 0, 1))
    arrays = {"in_" + n: a for n, a in arrays.items()}
    dram = {n: nc.dram_tensor(n, list(a.shape), F32, kind="ExternalInput").ap() for n, a in arrays.items()}
    n_seq = arrays["in_x"].shape[0]
    out = nc.dram_tensor("out", [n_seq, P, P], F32, kind="ExternalOutput").ap()
    build(nc, n_seq, dram["in_x"], dram["in_ctxT"], {n[3:]: a for n, a in dram.items()}, out)
    result = run_bass_kernel_spmd(nc, [arrays], core_ids=[0])
    return result.results[0]["out"]
```
